# Optimizing a Trainium2 kernel written in Bass

```python
import numpy as np
import jax
import jax.numpy as jnp

def _softmax(x, axis=-1):
    return jax.nn.softmax(x, axis=axis)

def _gelu(x):
    return jax.nn.gelu(x, approximate=True)

def _silu(x):
    return jax.nn.silu(x)

def _sigmoid(x):
    return jax.nn.sigmoid(x)

def _layernorm(x, axis=-1, eps=1e-05):
    m = jnp.mean(x, axis=axis, keepdims=True)
    v = jnp.var(x, axis=axis, keepdims=True)
    return (x - m) / jnp.sqrt(v + eps)

def _scatter_add(tgt, idx, src, axis=0):
    return tgt.at[idx].add(src)

def _segment_sum(src, seg, n):
    return jax.ops.segment_sum(src, seg, n)
kernel_name = 'mk_decoder_postln_d1_seqx_r8_51a411'

def setup_inputs(seed: int=0):
    np.random.seed(seed)
    _w = jnp.asarray

    def _rec_inputs():
        import jax
        import jax.numpy as jnp
        _rk = jax.random.key(seed)
        x = 0.01048 + 0.1018 * jax.random.normal(jax.random.fold_in(_rk, 1), (4, 256, 256), jnp.float32)
        _lenS = 256 - jax.random.randint(jax.random.fold_in(_rk, 7), (4,), 0, max(1, 256 // 4) + 1, jnp.int32)
        _lenS2 = 256 - jax.random.randint(jax.random.fold_in(_rk, 8), (4,), 0, max(1, 256 // 4) + 1, jnp.int32)
        _ctx_512P = jax.random.normal(jax.random.fold_in(_rk, 11), (4, 16, 64), jnp.float32)
        _ctx_512c = jax.random.dirichlet(jax.random.fold_in(_rk, 511), 0.3 * jnp.ones((16,), jnp.float32), (4, 256))
        _ctx_512t = jnp.einsum('bsk,bkd->bsd', _ctx_512c, _ctx_512P)
        _ctx_512t = _ctx_512t * jax.lax.rsqrt(jnp.mean(jnp.square(_ctx_512t)) + 1e-12) * 0.953939
        ctx_512 = -0.000292821 + 1.00034 * (_ctx_512t + 0.3 * jax.random.normal(jax.random.fold_in(_rk, 611), (4, 256, 64), jnp.float32))
        return (x, ctx_512)
    x, ctx_512 = _rec_inputs()

    def _L0_attn_setup():
        import jax, jax.numpy as jnp
        import numpy as np
        H = 32
        HKV = 8

        def _rope(t):
            B, h, S, dk = t.shape
            P = dk // 2
            theta = 1.0 / 10000.0 ** (2.0 * jnp.arange(P, dtype=jnp.float32) / dk)
            m_theta = jnp.arange(S, dtype=jnp.float32)[:, None] * theta[None, :]
            cos, sin = (jnp.cos(m_theta), jnp.sin(m_theta))
            tp = t.reshape(B, h, S, P, 2)
            t0, t1 = (tp[..., 0], tp[..., 1])
            rot = jnp.stack([t0 * cos - t1 * sin, t0 * sin + t1 * cos], axis=-1)
            return rot.reshape(B, h, S, dk)
        key = jax.random.key(seed)
        ks = jax.random.split(key, 5)
        B, S, D = (2, 128, 256)
        dk = D // H
        scale = 0.02
        x = jax.random.normal(ks[0], (B, S, D), dtype=jnp.float32)
        Wq = jax.random.normal(ks[1], (D, D), dtype=jnp.float32) * scale
        Wk = jax.random.normal(ks[2], (D, HKV * dk), dtype=jnp.float32) * scale
        Wv = jax.random.normal(ks[3], (D, HKV * dk), dtype=jnp.float32) * scale
        Wo = jax.random.normal(ks[4], (D, D), dtype=jnp.float32) * scale
        return {'x': x, 'Wq': Wq, 'Wk': Wk, 'Wv': Wv, 'Wo': Wo}
    _L0_attn_all = _L0_attn_setup()
    _L0_attn_in = {k: v for k, v in _L0_attn_all.items() if k in ('Wq', 'Wk', 'Wv', 'Wo')}
    del _L0_attn_all

    def _L0_xattn_setup():
        import jax, jax.numpy as jnp
        import numpy as np
        LRELU_ALPHA = 0.2
        MASK_VAL = -10000000000.0
        B, N, F_IN = (4, 256, 64)
        H, F_OUT = (8, 32)
        F_HID = H * F_OUT

        def gat_layer(x, adj, W, a_self, a_neigh, b):
            feat = jnp.einsum('nf,hfo->hno', x, W)
            attn_self = jnp.einsum('hno,ho->hn', feat, a_self)
            attn_neigh = jnp.einsum('hno,ho->hn', feat, a_neigh)
            e = attn_self[:, :, None] + attn_neigh[:, None, :]
            e = jax.nn.leaky_relu(e, LRELU_ALPHA)
            e = e + MASK_VAL * (1.0 - adj)[None, :, :]
            alpha = jax.nn.softmax(e, axis=-1)
            out = jnp.einsum('hnm,hmo->hno', alpha, feat) + b[:, None, :]
            out = jnp.transpose(out, (1, 0, 2)).reshape(out.shape[1], -1)
            return jax.nn.elu(out)
        key = jax.random.key(seed)
        ks = jax.random.split(key, 10)
        feats = jax.random.normal(ks[0], (B, N, F_IN), dtype=jnp.float32)
        a = (jax.random.uniform(ks[1], (B, N, N)) < 0.01).astype(jnp.float32)
        adj = jnp.maximum(a, jnp.eye(N, dtype=jnp.float32)[None])
        s0 = 1.0 / np.sqrt(F_IN)
        s1 = 1.0 / np.sqrt(F_HID)
        return {'feats': feats, 'adj': adj, 'W0': jax.random.normal(ks[2], (H, F_IN, F_OUT), dtype=jnp.float32) * s0, 'a_self0': jax.random.normal(ks[3], (H, F_OUT), dtype=jnp.float32) * 0.1, 'a_neigh0': jax.random.normal(ks[4], (H, F_OUT), dtype=jnp.float32) * 0.1, 'b0': jnp.zeros((H, F_OUT), dtype=jnp.float32), 'W1': jax.random.normal(ks[5], (H, F_HID, F_OUT), dtype=jnp.float32) * s1, 'a_self1': jax.random.normal(ks[6], (H, F_OUT), dtype=jnp.float32) * 0.1, 'a_neigh1': jax.random.normal(ks[7], (H, F_OUT), dtype=jnp.float32) * 0.1, 'b1': jnp.zeros((H, F_OUT), dtype=jnp.float32)}
    _L0_xattn_all = _L0_xattn_setup()
    _L0_xattn_in = {k: v for k, v in _L0_xattn_all.items() if k in ('W0', 'a_self0', 'a_neigh0', 'b0', 'W1', 'a_self1', 'a_neigh1', 'b1')}
    del _L0_xattn_all

    def _L0_ffn_setup():
        import jax, jax.numpy as jnp
        import numpy as np
        B, S, D, F, E, K = (2, 256, 256, 1024, 8, 2)
        key = jax.random.key(seed)
        k0, k1, k2, k3 = jax.random.split(key, 4)
        scale = lambda k, shape, fan_in: jax.random.normal(k, shape, jnp.float32) * fan_in ** (-0.5)
        return {'inputs': jax.random.normal(k0, (B, S, D), jnp.float32), 'gate_w': scale(k1, (D, E), D), 'gate_b': jnp.zeros((E,), jnp.float32), 'w1': scale(k2, (E, D, F), D), 'b1': jnp.zeros((E, F), jnp.float32), 'w2': scale(k3, (E, F, D), F), 'b2': jnp.zeros((E, D), jnp.float32)}
    _L0_ffn_all = _L0_ffn_setup()
    _L0_ffn_in = {k: v for k, v in _L0_ffn_all.items() if k in ('gate_w', 'gate_b', 'w1', 'b1', 'w2', 'b2')}
    del _L0_ffn_all
    return {'x': x, 'ctx_512': ctx_512, 'L0_attn_Wq': _L0_attn_in['Wq'], 'L0_attn_Wk': _L0_attn_in['Wk'], 'L0_attn_Wv': _L0_attn_in['Wv'], 'L0_attn_Wo': _L0_attn_in['Wo'], 'L0_xattn_W0': _L0_xattn_in['W0'], 'L0_xattn_a_self0': _L0_xattn_in['a_self0'], 'L0_xattn_a_neigh0': _L0_xattn_in['a_neigh0'], 'L0_xattn_b0': _L0_xattn_in['b0'], 'L0_xattn_W1': _L0_xattn_in['W1'], 'L0_xattn_a_self1': _L0_xattn_in['a_self1'], 'L0_xattn_a_neigh1': _L0_xattn_in['a_neigh1'], 'L0_xattn_b1': _L0_xattn_in['b1'], 'L0_ffn_gate_w': _L0_ffn_in['gate_w'], 'L0_ffn_gate_b': _L0_ffn_in['gate_b'], 'L0_ffn_w1': _L0_ffn_in['w1'], 'L0_ffn_b1': _L0_ffn_in['b1'], 'L0_ffn_w2': _L0_ffn_in['w2'], 'L0_ffn_b2': _L0_ffn_in['b2']}

def reference(x, ctx_512, L0_attn_Wq, L0_attn_Wk, L0_attn_Wv, L0_attn_Wo, L0_xattn_W0, L0_xattn_a_self0, L0_xattn_a_neigh0, L0_xattn_b0, L0_xattn_W1, L0_xattn_a_self1, L0_xattn_a_neigh1, L0_xattn_b1, L0_ffn_gate_w, L0_ffn_gate_b, L0_ffn_w1, L0_ffn_b1, L0_ffn_w2, L0_ffn_b2):
    import jax
    import jax.numpy as jnp

    def _L0_attn_ref(x, Wq, Wk, Wv, Wo):
        import jax, jax.numpy as jnp
        import numpy as np
        H = 32
        HKV = 8

        def _rope(t):
            B, h, S, dk = t.shape
            P = dk // 2
            theta = 1.0 / 10000.0 ** (2.0 * jnp.arange(P, dtype=jnp.float32) / dk)
            m_theta = jnp.arange(S, dtype=jnp.float32)[:, None] * theta[None, :]
            cos, sin = (jnp.cos(m_theta), jnp.sin(m_theta))
            tp = t.reshape(B, h, S, P, 2)
            t0, t1 = (tp[..., 0], tp[..., 1])
            rot = jnp.stack([t0 * cos - t1 * sin, t0 * sin + t1 * cos], axis=-1)
            return rot.reshape(B, h, S, dk)
        B, S, D = x.shape
        dk = D // H
        G = H // HKV
        q = (x @ Wq).reshape(B, S, H, dk).transpose(0, 2, 1, 3)
        k = (x @ Wk).reshape(B, S, HKV, dk).transpose(0, 2, 1, 3)
        v = (x @ Wv).reshape(B, S, HKV, dk).transpose(0, 2, 1, 3)
        q = _rope(q)
        k = _rope(k)
        qg = q.reshape(B, HKV, G, S, dk)
        scores = jnp.einsum('bhgqd,bhkd->bhgqk', qg, k) / jnp.sqrt(jnp.float32(dk))
        mask = jnp.triu(jnp.full((S, S), jnp.finfo(jnp.float32).min, dtype=jnp.float32), 1)
        attn = jax.nn.softmax(scores + mask, axis=-1)
        out = jnp.einsum('bhgqk,bhkd->bhgqd', attn, v)
        out = out.reshape(B, H, S, dk).transpose(0, 2, 1, 3).reshape(B, S, D)
        return out @ Wo

    def _L0_xattn_ref(feats, adj, W0, a_self0, a_neigh0, b0, W1, a_self1, a_neigh1, b1):
        import jax, jax.numpy as jnp
        import numpy as np
        LRELU_ALPHA = 0.2
        MASK_VAL = -10000000000.0
        B, N, F_IN = (4, 256, 64)
        H, F_OUT = (8, 32)
        F_HID = H * F_OUT

        def gat_layer(x, adj, W, a_self, a_neigh, b):
            feat = jnp.einsum('nf,hfo->hno', x, W)
            attn_self = jnp.einsum('hno,ho->hn', feat, a_self)
            attn_neigh = jnp.einsum('hno,ho->hn', feat, a_neigh)
            e = attn_self[:, :, None] + attn_neigh[:, None, :]
            e = jax.nn.leaky_relu(e, LRELU_ALPHA)
            e = e + MASK_VAL * (1.0 - adj)[None, :, :]
            alpha = jax.nn.softmax(e, axis=-1)
            out = jnp.einsum('hnm,hmo->hno', alpha, feat) + b[:, None, :]
            out = jnp.transpose(out, (1, 0, 2)).reshape(out.shape[1], -1)
            return jax.nn.elu(out)

        def per_graph(x, a):
            h = gat_layer(x, a, W0, a_self0, a_neigh0, b0)
            return gat_layer(h, a, W1, a_self1, a_neigh1, b1)
        return jax.vmap(per_graph)(feats, adj)

    def _L0_ffn_ref(inputs, gate_w, gate_b, w1, b1, w2, b2):
        import jax, jax.numpy as jnp
        import numpy as np
        B, S, D, F, E, K = (2, 256, 256, 1024, 8, 2)
        x = inputs.reshape(-1, inputs.shape[-1])
        n = x.shape[0]
        gate_probs = jax.nn.softmax(x @ gate_w + gate_b, axis=-1)
        weights, selected = jax.lax.top_k(gate_probs, K)
        weights = weights / jnp.sum(weights, axis=-1, keepdims=True)
        comb = jnp.zeros((n, E), x.dtype).at[jnp.arange(n)[:, None], selected].set(weights)
        h = jax.nn.gelu(jnp.einsum('nd,edf->enf', x, w1) + b1[:, None, :])
        expert_out = jnp.einsum('enf,efd->end', h, w2) + b2[:, None, :]
        out = jnp.einsum('ne,end->nd', comb, expert_out)
        return out.reshape(inputs.shape[:-1] + (out.shape[-1],))
    x = _layernorm(x + _L0_attn_ref(x, L0_attn_Wq, L0_attn_Wk, L0_attn_Wv, L0_attn_Wo), axis=-1)
    x = _layernorm(x + _L0_xattn_ref(ctx_512, x, L0_xattn_W0, L0_xattn_a_self0, L0_xattn_a_neigh0, L0_xattn_b0, L0_xattn_W1, L0_xattn_a_self1, L0_xattn_a_neigh1, L0_xattn_b1), axis=-1)
    x = _layernorm(x + _L0_ffn_ref(x, L0_ffn_gate_w, L0_ffn_gate_b, L0_ffn_w1, L0_ffn_b1, L0_ffn_w2, L0_ffn_b2), axis=-1)
    return x

_drawn_inputs = setup_inputs


def setup_inputs(seed=0):
    import zlib

    import numpy as np

    out = dict(_drawn_inputs(seed))
    spreads = {'L0_xattn_b0': (0.0, 0.1),
     'L0_xattn_b1': (0.0, 0.1),
     'L0_ffn_gate_b': (0.0, 0.1),
     'L0_ffn_b1': (0.0, 0.1),
     'L0_ffn_b2': (0.0, 0.1)}
    factors = {'L0_attn_Wq': 8.0, 'L0_attn_Wk': 22.153}
    for name, (base, spread) in spreads.items():
        noise = np.random.default_rng([zlib.crc32(name.encode()), seed]).standard_normal(out[name].shape)
        drawn = base * np.exp(spread * noise) if base else spread * noise
        out[name] = jnp.asarray(drawn.astype(out[name].dtype))
    for name, factor in factors.items():
        out[name] = (out[name] * factor).astype(out[name].dtype)
    return out
```

```python
from contextlib import ExitStack

import concourse.bass as bass
from concourse import mybir

F32 = mybir.dt.float32
BF16 = mybir.dt.bfloat16
F16 = mybir.dt.float16
U32 = mybir.dt.uint32
I32 = mybir.dt.int32
ALU = mybir.AluOpType
ACT = mybir.ActivationFunctionType
AX = mybir.AxisListType

P = 128
B, S, D = 4, 256, 256
N = B * S
T = N // P
H, HKV, DK = 32, 8, 8
G = H // HKV
GH, GO, FIN = 8, 32, 64
E, F = 8, 1024
SCALE = float(DK) ** -0.5
MASK_VAL = -10000000000.0
EPS = 1e-5
Q_PART = (0, 0, 1, 1, 0, 2)
K_PART = (0, 1, 0, 1, 2, 0)
DATA_ROWS = 8 * len(Q_PART)
MAX_ROWS = 2
SLOTS = 3
MISC = 12
TURNS = 6
SLOT_ROWS = N + P
TILES = 2 * N // P + E - 1
PTU = 10


def bc(ap, axis, n):
    a = ap.unsqueeze(axis)
    shape = list(a.shape)
    shape[axis] = n
    return a.to_broadcast(shape)


def decoder_layer(nc, t, out):
    with ExitStack() as ctx:
        def sb(name, shape, dt=F32):
            return ctx.enter_context(nc.sbuf_tensor(name, shape, dt))

        def sem(name):
            return ctx.enter_context(nc.semaphore(name))

        ps = ctx.enter_context(nc.psum_tensor("ps", [P, 8, 512], F32))
        SB, TB, OB, EB, PB, MB = (0, 1), (2, 3), 4, 5, 6, 7

        w1 = sb("w1", [P, E, 2, F])
        w2 = sb("w2", [P, E, 8, D])
        work = sb("work", [P, 8192])

        def carver(area):
            at = [0]

            def carve(shape, dt=F32):
                size = 1
                for n in shape[1:]:
                    size *= n
                words = size if dt in (F32, U32, I32) else size // 2
                ap = area[0:shape[0], at[0]:at[0] + words]
                at[0] += words
                assert at[0] <= area.shape[1], (at[0], shape)
                if dt is not F32:
                    ap = ap.bitcast(dt)
                names = "abcdef"[:len(shape) - 1]
                if len(shape) == 2:
                    return ap
                return ap.rearrange("p (" + " ".join(names) + ") -> p " + " ".join(names),
                                    **{n: v for n, v in zip(names[1:], shape[2:])})
            return carve

        carve = carver(w1[:, :, :, :].rearrange("p e k f -> p (e k f)"))
        cmask = carve([P, 2, P])
        umat = carve([P, P])
        ropeq = carve([P, 2, S])
        ropek = carve([32, 2, S])
        xT = carve([P, 2, N])
        wq = carve([P, 2, 256])
        wk = carve([P, 2, 64])
        wv = carve([P, 2, 64])
        avec = carve([P, 4, D])
        watmp = carve([P, D])
        rc = carve([P, 2, 512])
        rs = carve([P, 2, 512])
        rot = carve([P, 2, 512])
        qp = carve([P, 2, 3, 2, 512], BF16)
        kp = carve([32, 2, 3, 2, 512], BF16)
        carve = carver(w2[:, 2:E].rearrange("p e k f -> p (e k f)"))
        QS = carve([P, 2, 16, S], BF16)
        KS = carve([P, 2, 4, S], BF16)
        PT = carve([P, 2, SLOTS, 512])
        V = carve([P, T, HKV, 9])
        attn = carve([P, 2, D])
        attnT = carve([P, 2, S])
        mneg = carve([P, 2, 2, 16])
        mb = carve([P, 2, 2, MAX_ROWS, 16], BF16)
        mT = carve([64, 2, S], BF16)
        wo = carve([P, 2, D])
        carve = carver(work[:, :])
        es = carve([P, 2, 2, S])
        Pm = carve([P, 2, 2, S])
        PTg = carve([P, 2, 2, 2, P])
        Mt = carve([P, 2, S])
        feat = carve([P, 2, D])
        z = carve([P, 2, D])
        zm = carve([P, D])
        ze = carve([P, D])
        h1T = carve([P, 2, S])
        w1g = carve([P, 2, D])
        x2T = carve([P, 2, S])
        carve = carver(work[:, :])
        xg = carve([P, 2, D])
        xgT = carve([P, 2, 2, P])
        hs = carve([P, 2, F])
        gT = carve([P, 2, 8, P])
        ys = carve([P, 2, D])
        b2s = carve([P, E, D])
        carve = carver(w1[:, :, :, :].rearrange("p e k f -> p (e k f)"))
        yg = carve([P, T, 2, D])
        outs = carve([P, T, D])
        ident = sb("ident", [P, P])
        ident_b = sb("ident_b", [P, P], BF16)
        maskS = sb("maskS", [P, P], BF16)
        maskT = sb("maskT", [P, P], BF16)
        before = sb("before", [P, P], BF16)
        ones_b = sb("ones_b", [P, P], BF16)
        delta8 = sb("delta8", [24, GH])
        delta = sb("delta", [24, GH, S], BF16)
        x_sb = sb("x_sb", [P, 2, 2, D])
        ctxT = sb("ctxT", [FIN, N])
        w0 = sb("w0", [FIN, D])
        bvec = sb("bvec", [P, 2, D])
        wa0 = sb("wa0", [FIN, 16])
        wa1 = sb("wa1", [P, 2, 16])
        orv = sb("orv", [P, 32])
        res = sb("res", [P, 2, D])
        stats = sb("stats", [P, T, 6])
        mv = sb("mv", [P, T, 2])
        vare = sb("vare", [P, T])
        rstd = sb("rstd", [P, T])
        mhalf = sb("mhalf", [P, T])
        x1 = sb("x1", [P, 2, D])
        x2 = sb("x2", [P, T, D])
        snp = sb("snp", [P, 2, 2, 3, GH], BF16)
        snr = sb("snr", [P, 2, 2, GH])
        snT = sb("snT", [24, 2, S], BF16)
        mx = sb("mx", [P, 2, 2])
        nmx = sb("nmx", [P, 2, 2])
        psums = sb("psums", [P, 2, GH])
        grv = sb("grv", [P, GH])
        gw = sb("gw", [P, 2, E])
        gb = sb("gb", [P, E])
        rowc = sb("rowc", [P, 3 * E + E * E + 24])
        iota_e, stride_e, tile_j = (rowc[:, E * i:E * i + E] for i in range(3))
        lower = rowc[:, 3 * E:3 * E + E * E].rearrange("p (a b) -> p a b", a=E)
        tau = rowc[:, 3 * E + E * E:3 * E + E * E + TILES]
        lg = sb("lg", [P, 2, E])
        lmax = sb("lmax", [P, 2])
        lsum = sb("lsum", [P, 2])
        prob = sb("prob", [P, 2, E])
        top = sb("top", [P, 2, 8])
        topi = sb("topi", [P, 2, 8], U32)
        topf = sb("topf", [P, 2, 2])
        wsum = sb("wsum", [P, 2])
        wk2 = sb("wk2", [P, T, 2])
        oh = sb("oh", [P, T, 2, E])
        chosen = sb("chosen", [P, 2, E], BF16)
        run = sb("run", [P, E])
        pos = sb("pos", [P, 2, E])
        ohp = sb("ohp", [P, 2, 2, E])
        slotf = sb("slotf", [P, T, 2])
        shift = sb("shift", [P, E])
        tsh = sb("tsh", [P, 2 * T])
        oht = sb("oht", [P, T * 2, E])
        yslot = sb("yslot", [P, T, 2], I32)
        slot = sb("slot", [P, T, 2], I32)
        big = sb("big", [P, TILES, E])
        big2 = sb("big2", [P, TILES, E])
        tiles_e = sb("tiles_e", [P, E])
        base_e = sb("base_e", [P, E])
        end_e = sb("end_e", [P, E])
        tcl = sb("tcl", [P, TILES])
        te = sb("te", [P, TILES])
        tb = sb("tb", [P, TILES])
        trow = sb("trow", [P, TILES])
        last = sb("last", [P, 1])
        tab = sb("tab", [P, 2 * TILES + E], I32)
        padf = sb("padf", [P, E])
        zero = sb("zero", [P, D])
        b1s = sb("b1s", [P, E, 8])
        b1t = sb("b1t", [P, 2, 8])

        qd = nc.dram_tensor("q_parts", (2, 2, 3, 8, 16, 512), BF16, kind="Internal").ap()
        kd = nc.dram_tensor("k_parts", (2, 2, 3, 8, 4, 512), BF16, kind="Internal").ap()
        xd = nc.dram_tensor("x_rows", (E * SLOT_ROWS, D), F32, kind="Internal").ap()
        yd = nc.dram_tensor("y_rows", (TILES * P, D), F32, kind="Internal").ap()

        ld_const, ld_x, ld_w, ld_gat = (sem(n) for n in ("ld_const", "ld_x", "ld_w", "ld_gat"))
        consts_ready = sem("consts_ready")
        ones_ready = sem("ones_ready")
        proj_ready = sem("proj_ready")
        v_ready = sem("v_ready")
        v_done = sem("v_done")
        rot_done = sem("rot_done")
        part_a = sem("part_a")
        rem_a = sem("rem_a")
        parts_out = [sem(f"parts_out{c}") for c in range(2)]
        stacks_in = [sem(f"stacks_in{b}") for b in range(B)]
        maxrows_in = [sem(f"maxrows_in{b}") for b in range(B)]
        s_full, s_free = sem("s_full"), sem("s_free")
        mparts = sem("mparts")
        misc_full, misc_free = sem("misc_full"), sem("misc_free")
        t_full, t_free = sem("t_full"), sem("t_free")
        pv_done = sem("pv_done")
        o_full, o_free = sem("o_full"), sem("o_free")
        wo_ready, x1_ready = sem("wo_ready"), sem("x1_ready")
        var_ready, rstd_ready = sem("var_ready"), sem("rstd_ready")
        wa_ready = sem("wa_ready")
        pt_full, pt_free = sem("pt_full"), sem("pt_free")
        snp_ready = sem("snp_ready")
        e_full, e_free, e_fifth = sem("e_full"), sem("e_free"), sem("e_fifth")
        masked = sem("masked")
        p_ready = sem("p_ready")
        agg_done = sem("agg_done")
        zneg, zexp = sem("zneg"), sem("zexp")
        h_ready = sem("h_ready")
        x2_ready = sem("x2_ready")
        dve_step, act_step, pool_step = sem("dve_step"), sem("act_step"), sem("pool_step")
        stored = sem("stored")
        w1_in, w2a_in, w2b_in, rt_in = sem("w1_in"), sem("w2a_in"), sem("w2b_in"), sem("rt_in")
        x_in1 = [sem(f"x_in1_{i}") for i in range(2)]
        logit_ready, lexp_in, lexp = sem("logit_ready"), sem("lexp_in"), sem("lexp")
        chosen_ready, rank_ready = sem("chosen_ready"), sem("rank_ready")
        slots_ready, scattered = sem("slots_ready"), sem("scattered")
        yslots_ready = sem("yslots_ready")
        tab_ready, padded = sem("tab_ready"), sem("padded")
        xg_in, x_turned, xgT_ready = [sem(f"xg_in{i}") for i in range(2)], sem("x_turned"), sem("xgT_ready")
        h_full, hs_a, hs_d, ht_full = sem("h_full"), sem("hs_a"), sem("hs_d"), sem("ht_full")
        b1_ready, g_ready, y_full, y_out = (sem(n) for n in ("b1_ready", "g_ready", "y_full", "y_out"))
        y_stored = [sem(f"y_stored{i}") for i in range(2)]
        b2_in = sem("b2_in")
        gathered = [sem(f"gathered{i}") for i in range(2)]
        zero_ready = sem("zero_ready")
        out_ready = sem("out_ready")

        def wait(eng, sm, value):
            if not isinstance(value, int) or value > 0:
                eng.wait_ge(sm, value)

        def tiles_of(eng, step):
            with eng.Fori(1, 10) as i:
                step(2 * i + 1, 1)
                step(2 * i + 2, 0)

        block = ctx.enter_context(nc.Block())
        LN_OPS = 2

        @block.sync
        def _(sp):
            sp.dma_start(xT[:, :, :], t["xT"].rearrange("(k p) n -> p k n", p=P)).then_inc(ld_x, 16)
            sp.dma_start(wq[:, :, :], t["wq"].rearrange("(k p) n -> p k n", p=P)).then_inc(ld_x, 16)
            sp.dma_start(wk[:, :, :], t["wk"].rearrange("(k p) n -> p k n", p=P)).then_inc(ld_x, 16)
            sp.dma_start(wv[:, :, :], t["wv"].rearrange("(k p) n -> p k n", p=P)).then_inc(ld_x, 16)
            x_tok = t["x"].rearrange("(b t p) d -> b p t d", b=B, p=P)
            for b in range(2):
                sp.dma_start(x_sb[:, b], x_tok[b]).then_inc(x_in1[b], 16)
            sp.dma_start(wo[:, :, :], t["wo"].rearrange("(k p) n -> p k n", p=P)).then_inc(ld_w, 16)
            sp.dma_start(ctxT[:, :], t["ctxT"]).then_inc(ld_gat, 16)
            sp.dma_start(w0[:, :], t["w0"]).then_inc(ld_gat, 16)
            sp.dma_start(w1g[:, :, :], t["w1g"].rearrange("(k p) n -> p k n", p=P)).then_inc(ld_gat, 16)
            sp.dma_start(bvec[:, 0, :], t["avec"][4, :].partition_broadcast(P)).then_inc(ld_gat, 16)
            sp.dma_start(bvec[:, 1, :], t["avec"][5, :].partition_broadcast(P)).then_inc(ld_gat, 16)
            sp.dma_start(gw[:, :, :], t["gw"].rearrange("(k p) n -> p k n", p=P)).then_inc(rt_in, 16)
            sp.dma_start(gb[:, :], t["gb"].partition_broadcast(P)).then_inc(rt_in, 16)
            sp.dma_start(rowc[:, :], t["rowc"].partition_broadcast(P)).then_inc(rt_in, 16)
            sp.dma_start(b1s[:, :, :], t["b1"]).then_inc(rt_in, 16)
            for i in range(4):
                sp.dma_start(avec[:, i, :], t["avec"][i, :].partition_broadcast(P)).then_inc(ld_gat, 16)

            def parts(c):
                sp.wait_ge(rem_a, 4 * (c + 1))
                sp.wait_ge(part_a, 4 * (c + 1))
                for par in range(2):
                    sp.dma_start(qd[c, par].rearrange("a (e p) h n -> (p h) (a e) n", e=2),
                                 qp[64 * par:64 * par + 64, c].rearrange("p a e n -> p (a e) n")
                                 ).then_inc(parts_out[c], 16)
                    sp.dma_start(kd[c, par].rearrange("a (e p) h n -> (p h) (a e) n", e=2),
                                 kp[16 * par:16 * par + 16, c].rearrange("p a e n -> p (a e) n")
                                 ).then_inc(parts_out[c], 16)

            def stacks(b):
                c, half = b // 2, b % 2
                sp.wait_ge(parts_out[c], 4 * 16)
                if b >= 2:
                    sp.wait_ge(t_full, HKV * SLOTS * (b - 1))
                tok = slice(S * half, S * half + S)
                for j in range(len(Q_PART)):
                    for par in range(2):
                        rows = slice(64 * par + 8 * j, 64 * par + 8 * j + 8)
                        sp.dma_start(QS[rows, b % 2, :, :], qd[c, par, Q_PART[j], :, :, tok]
                                     ).then_inc(stacks_in[b], 16)
                        sp.dma_start(KS[rows, b % 2, :, :], kd[c, par, K_PART[j], :, :, tok]
                                     ).then_inc(stacks_in[b], 16)

            def max_rows(b):
                sp.wait_ge(misc_free, MISC * b + 1)
                for par in range(2):
                    for part in range(MAX_ROWS):
                        r = 64 * par + DATA_ROWS + part
                        q0 = 32 * par + 16 * part
                        sp.dma_start(QS[r:r + 1, b % 2, :, :], mT[q0:q0 + 16, b % 2, :]).then_inc(maxrows_in[b], 16)

            w1_rows = t["w1"].rearrange("e (k p) f -> e p k f", p=P)
            w2_rows = t["w2"].rearrange("e (k p) d -> e p k d", p=P)
            sp.wait_ge(ones_ready, 1)
            parts(0)
            stacks(0)
            stacks(1)
            parts(1)
            sp.wait_ge(parts_out[1], 4 * 16)
            for e in range(2):
                sp.dma_start(w2[:, e], w2_rows[e]).then_inc(w2a_in, 16)
            max_rows(0)
            sp.wait_ge(v_ready, 1)
            sp.wait_ge(wa_ready, 6)
            sp.wait_ge(consts_ready, 5)
            for e in range(E):
                sp.dma_start(w1[:, e], w1_rows[e]).then_inc(w1_in, 16)
            stacks(2)
            max_rows(1)
            stacks(3)
            max_rows(2)
            for b in range(2, B):
                sp.wait_ge(x1_ready, b - 1)
                sp.dma_start(x_sb[:, b % 2], x_tok[b]).then_inc(x_in1[b % 2], 16)
            max_rows(3)
            sp.wait_ge(x1_ready, B)
            for e in range(2, E):
                sp.dma_start(w2[:, e], w2_rows[e]).then_inc(w2b_in, 16)
            sp.wait_ge(tab_ready, 3)
            sp.wait_ge(zero_ready, 1)
            for e in range(E):
                row = sp.value_load(tab[0:1, 2 * TILES + e:2 * TILES + e + 1], min_val=0, max_val=E * SLOT_ROWS - P)
                sp.dma_start(xd[bass.ds(row, P), :], zero[:, :]).then_inc(padded, 16)
            sp.wait_ge(x2_ready, B)
            for e in range(E):
                sp.dma_start(b2s[:, e, :], t["b2"][e, :].partition_broadcast(P)).then_inc(b2_in, 16)
            sp.wait_ge(scattered, 16 * 4 * B)
            sp.wait_ge(padded, 16 * E)

            def tile_row(n):
                return sp.value_load(tab[0:1, bass.ds(n + TILES, 1)], min_val=0, max_val=E * SLOT_ROWS - P)

            def load_tile(n, par):
                wait(sp, x_turned, n - 1)
                sp.dma_start(xg[:, par, :], xd[bass.ds(tile_row(n), P), :]).then_inc(xg_in[par], 16)

            def store_tile(n, par):
                sp.wait_ge(y_out, n + 1)
                sp.dma_start(yd[bass.ds(n * P, P), :], ys[:, par, :]).then_inc(y_stored[par], 16)

            def step(n, par):
                load_tile(n + 2, par)
                store_tile(n - 1, 1 - par)

            load_tile(0, 0)
            load_tile(1, 1)
            load_tile(2, 0)
            step(1, 1)
            step(2, 0)
            with sp.Fori(1, 9) as i:
                step(2 * i + 1, 1)
                step(2 * i + 2, 0)
            step(19, 1)
            step(20, 0)
            store_tile(20, 0)
            store_tile(21, 1)
            store_tile(22, 0)
            out_rows = out.rearrange("(t p) d -> p t d", p=P)
            for half in range(2):
                sp.wait_ge(out_ready, half + 1)
                sp.dma_start(out_rows[:, 4 * half:4 * half + 4, :], outs[:, 4 * half:4 * half + 4, :]).then_inc(stored, 16)
            sp.wait_ge(stored, 32)

        @block.gpsimd
        def _(pool):
            nc.gpsimd.memset(KS[:, :, :, :], 1.0).then_inc(ones_ready, 1)
            nc.gpsimd.memset(V[:, :, :, :], 1.0).then_inc(ones_ready, 1)
            nc.gpsimd.memset(mhalf[:, :], -0.5).then_inc(pool_step, 1)
            pool.wait_ge(ld_const, 16 * 6)
            nc.gpsimd.tensor_copy(ident_b[:, :], ident[:, :]).then_inc(consts_ready, 1)
            nc.gpsimd.tensor_copy(maskS[:, :], cmask[:, 0, :]).then_inc(consts_ready, 1)
            nc.gpsimd.tensor_copy(maskT[:, :], cmask[:, 1, :]).then_inc(consts_ready, 1)
            nc.gpsimd.tensor_copy(before[:, :], umat[:, :]).then_inc(consts_ready, 1)
            nc.gpsimd.tensor_copy(delta[:, :, :], bc(delta8[:, :], 2, S)).then_inc(consts_ready, 1)
            nc.gpsimd.memset(ones_b[:, :], 1.0).then_inc(consts_ready, 1)
            nc.gpsimd.memset(run[:, :], 0.0).then_inc(consts_ready, 1)
            nc.gpsimd.memset(zero[:, :], 0.0).then_inc(zero_ready, 1)
            steps = [1]

            def inverse_root(k, n):
                pool.wait_ge(var_ready, k + 1)
                nc.gpsimd.tensor_scalar(vare[:, 0:n], mv[:, 0:n, 1], EPS, None, ALU.add).then_inc(pool_step, 1)
                steps[0] += 1
                pool.wait_ge(pool_step, steps[0])
                nc.gpsimd.tensor_tensor(rstd[:, 0:n], vare[:, 0:n], mhalf[:, 0:n], ALU.pow).then_inc(rstd_ready, 1)

            for b in range(B):
                inverse_root(2 * b, 2)
                inverse_root(2 * b + 1, 2)
                pool.wait_ge(slots_ready, b + 1)
                for i in range(2):
                    for k in range(2):
                        nc.gpsimd.indirect_dma_start(
                            out=xd, out_offset=bass.IndirectOffsetOnAxis(ap=slot[:, 2 * b + i, k:k + 1], axis=0),
                            in_=x2[:, 2 * b + i, :], in_offset=None).then_inc(scattered, 16)

            def bias_tile(n, par):
                wait(pool, g_ready, n - 1)
                e = pool.value_load(tab[0:1, bass.ds(n, 1)], min_val=0, max_val=E - 1)
                nc.gpsimd.tensor_copy(b1t[:, par, :], b1s[:, bass.ds(e, 1), :].rearrange("p o k -> p (o k)")
                                      ).then_inc(b1_ready, 1)

            pool.wait_ge(tab_ready, 3)
            pool.wait_ge(rt_in, 64)
            for n in range(3):
                bias_tile(n, n % 2)
            tiles_of(pool, bias_tile)
            bias_tile(21, 1)
            bias_tile(22, 0)
            pool.wait_ge(y_stored[0], 8 * (TILES + 1))
            pool.wait_ge(y_stored[1], 8 * (TILES - 1))
            pool.wait_ge(y_full, TILES)
            pool.wait_ge(yslots_ready, 1)
            for i in range(T):
                for k in range(2):
                    nc.gpsimd.indirect_dma_start(
                        out=yg[:, i, k, :], out_offset=None, in_=yd,
                        in_offset=bass.IndirectOffsetOnAxis(ap=yslot[:, i, k:k + 1], axis=0)).then_inc(gathered[i // 4], 16)
            inverse_root(2 * B, 4)
            inverse_root(2 * B + 1, 4)

        @block.scalar
        def _(act):
            act.dma_start(ident[:, :], t["ident"]).then_inc(ld_const, 16)
            act.dma_start(cmask[:, :, :], t["cmask"]).then_inc(ld_const, 16)
            act.dma_start(ropeq[:, :, :], t["ropeq"]).then_inc(ld_const, 16)
            act.dma_start(ropek[:, :, :], t["ropek"]).then_inc(ld_const, 16)
            act.dma_start(delta8[:, :], t["delta"]).then_inc(ld_const, 16)
            act.dma_start(umat[:, :], t["umat"]).then_inc(ld_const, 16)

            for c in range(2):
                for u, dst in ((2 * c, qp[:, c]), (2 * c + 1, kp[:, c])):
                    rows = P if u % 2 == 0 else 32
                    src = rot[0:rows]
                    act.wait_ge(rot_done, u + 1)
                    nc.scalar.activation(dst[:, 0], src, ACT.Copy).then_inc(part_a, 1)
                    act.wait_ge(rem_a, 2 * u + 1)
                    nc.scalar.activation(dst[:, 1], src, ACT.Copy).then_inc(part_a, 1)
            act.wait_ge(ones_ready, 2)
            act.wait_ge(v_ready, 1)
            nc.scalar.activation(V[:, :, :, 0:DK],
                                 ps[:, SB[0], :].rearrange("p (t g d) -> p t g d", t=T, g=HKV),
                                 ACT.Copy).then_inc(v_done, 1)

            def exps(b):
                for n in range(HKV * SLOTS):
                    g, u = n // SLOTS, n % SLOTS
                    k = b * HKV * SLOTS + n
                    act.wait_ge(t_full, k + 1)
                    if b * HKV + g >= 2:
                        act.wait_ge(pv_done, b * HKV + g - 1)
                    nc.scalar.activation(PT[:, g % 2, u, :], ps[:, TB[k % 2], :], ACT.Exp,
                                         scale=SCALE).then_inc(t_free, 1)

            def misc_copy(dst, src, k):
                act.wait_ge(misc_full, k + 1)
                nc.scalar.activation(dst, src, ACT.Copy).then_inc(misc_free, 1)

            def slope(gl, q):
                n = gl * 8 + q
                act.wait_ge(e_full, n + 1)
                if n >= 2:
                    act.wait_ge(p_ready, n - 1)
                nc.scalar.activation(es[:, q % 2].rearrange("p a j -> p (a j)"), ps[:, EB, :], ACT.Copy,
                                     scale=0.2).then_inc(e_fifth, 1)

            def gexp(gl, q):
                n = gl * 8 + q
                it, hp = q // 4, q % 4
                act.wait_ge(masked, n + 1)
                if n >= 2:
                    m = n - 2
                    act.wait_ge(pt_full, (m // 8) * PTU + 2 + m % 8 + 1)
                for i in range(2):
                    ins = nc.scalar.activation(Pm[:, q % 2, i, :], es[:, q % 2, i, :], ACT.Exp,
                                               bias=nmx[:, q % 2, i:i + 1],
                                               accum_out=psums[:, it, 2 * hp + i:2 * hp + i + 1])
                ins.then_inc(p_ready, 1)

            def gat(b, L):
                gl = 2 * b + L
                base = MISC * b
                misc_copy(feat[:, :, :], ps[:, MB, :].rearrange("p (a d) -> p a d", a=2), TURNS * b + (2 if L == 0 else 4))
                for q in range(9):
                    if q < 8:
                        slope(gl, q)
                    if q >= 1:
                        gexp(gl, q - 1)
                    if q == 6:
                        elu_exp(gl, 0)
                elu_exp(gl, 1)
                if L == 0:
                    misc_copy(h1T[:, :, :], ps[:, MB, :].rearrange("p (a d) -> p a d", a=2), TURNS * b + 3)

            def elu_exp(gl, it):
                act.wait_ge(zneg, 2 * gl + it + 1)
                nc.scalar.activation(ze[:, :], zm[:, :], ACT.Exp).then_inc(zexp, 1)

            for b in range(B):
                misc_copy(mT[:, b % 2, :], ps[0:64, MB, 0:S // 2].bitcast(BF16), TURNS * b)
                exps(b)
                misc_copy(attnT[:, :, :], ps[:, MB, :].rearrange("p (a d) -> p a d", a=2), TURNS * b + 1)
                gat(b, 0)
                gat(b, 1)
                misc_copy(x2T[:, :, :], ps[:, MB, :].rearrange("p (a d) -> p a d", a=2), TURNS * b + 5)
                act.wait_ge(lexp_in, b + 1)
                nc.scalar.activation(prob[:, :, :], lg[:, :, :], ACT.Exp).then_inc(lexp, 1)

            def gelu_tile(n, par):
                wait(act, ht_full, 2 * n - 2)
                act.wait_ge(h_full, 2 * n + 1)
                nc.scalar.activation(hs[:, par, 0:512], ps[:, 2, :], ACT.Copy).then_inc(hs_a, 1)
                wait(act, y_full, n - 1)
                act.wait_ge(b1_ready, n + 1)
                for k in range(8):
                    if k % 4 == 0:
                        act.wait_ge(ht_full, 2 * n + 1 + k // 4)
                    ins = nc.scalar.activation(gT[:, par, k, :], ps[:, 4 + k // 4, 128 * (k % 4):128 * (k % 4) + 128],
                                               ACT.Gelu_apprx_tanh, bias=b1t[:, par, k:k + 1])
                ins.then_inc(g_ready, 1)

            for n in range(3):
                gelu_tile(n, n % 2)
            tiles_of(act, gelu_tile)
            gelu_tile(21, 1)
            gelu_tile(22, 0)

        @block.vector
        def _(dve):
            chain = [0]

            def link(ins):
                chain[0] += 1
                ins.then_inc(dve_step, 1)
                dve.wait_ge(dve_step, chain[0])

            dve.wait_ge(ld_const, 16 * 6)
            for c in range(2):
                dve.wait_ge(proj_ready, c + 1)
                for kind in range(2):
                    u = 2 * c + kind
                    rows = P if kind == 0 else 32
                    bank = 4 * c + 2 * kind
                    table = ropeq if kind == 0 else ropek
                    dst = qp[:, c] if kind == 0 else kp[:, c]
                    src = ps[0:rows, bank:bank + 2, :].rearrange("p e (b n) -> p (e b) n", b=2)
                    cos, sin = (bc(table[0:rows, i, :], 1, 4) for i in range(2))
                    link(nc.vector.tensor_tensor(rc[0:rows].rearrange("p e (b n) -> p (e b) n", b=2), src, cos, ALU.mult))
                    link(nc.vector.tensor_tensor(rs[0:rows].rearrange("p e (b n) -> p (e b) n", b=2), src, sin, ALU.mult))
                    if u >= 1:
                        dve.wait_ge(part_a, 2 * u)
                    nc.vector.tensor_tensor(rot[0:rows, 0, :], rc[0:rows, 0, :], rs[0:rows, 1, :], ALU.subtract)
                    nc.vector.tensor_tensor(rot[0:rows, 1, :], rs[0:rows, 0, :], rc[0:rows, 1, :], ALU.add
                                            ).then_inc(rot_done, 1)
                    dve.wait_ge(part_a, 2 * u + 1)
                    nc.vector.tensor_tensor(rot[0:rows], rot[0:rows], dst[:, 0], ALU.subtract).then_inc(rem_a, 1)
                    dve.wait_ge(part_a, 2 * u + 2)
                    nc.vector.tensor_tensor(dst[:, 2], rot[0:rows], dst[:, 1], ALU.subtract).then_inc(rem_a, 1)

            dve.wait_ge(ld_gat, 16 * 9)
            for L in range(2):
                for k in range(1 if L == 0 else 2):
                    rows = FIN if L == 0 else P
                    w = w0[:, :] if L == 0 else w1g[:, k, :]
                    for i in range(2):
                        o = wa0[:, 8 * i:8 * i + 8] if L == 0 else wa1[:, k, 8 * i:8 * i + 8]
                        nth = 2 * (L + k) + i
                        if nth:
                            dve.wait_ge(wa_ready, nth)
                        link(nc.vector.tensor_tensor(watmp[0:rows, :], w, avec[0:rows, 2 * L + i, :], ALU.mult))
                        nc.vector.tensor_reduce(o, watmp[0:rows, :].rearrange("p (h o) -> p h o", h=GH), AX.X, ALU.add
                                                ).then_inc(wa_ready, 1)

            def maxima(b):
                for n in range(HKV * SLOTS):
                    g, u = n // SLOTS, n % SLOTS
                    par, gg = g % 2, g // 2
                    k = b * HKV * SLOTS + n
                    dve.wait_ge(s_full, k + 1)
                    if u == 0:
                        o, w = mneg[:, 0, par, 4 * gg:4 * gg + 4], 4
                    else:
                        o, w = mneg[:, 1, par, 4 * gg + 2 * u - 2:4 * gg + 2 * u], 2
                    ins = nc.vector.tensor_reduce(o, ps[:, SB[k % 2], :].rearrange("p (h j) -> p h j", h=w), AX.X,
                                                  ALU.max, negate=True)
                    ins.then_inc(s_free, 1)
                dve.wait_ge(s_free, (b + 1) * HKV * SLOTS)
                if b >= 1:
                    dve.wait_ge(misc_full, TURNS * (b - 1) + 1)
                link(nc.vector.tensor_copy(mb[:, :, :, 0, :], mneg[:, :, :, :]))
                nc.vector.tensor_tensor(mb[:, :, :, 1, :], mneg[:, :, :, :], mb[:, :, :, 0, :], ALU.subtract
                                        ).then_inc(mparts, 1)

            def normalise(b, half):
                dve.wait_ge(pv_done, HKV * b + 4 * half + 4)
                o = ps[:, OB, 0:288].rearrange("p (g q i d) -> p g q i d", g=4, q=2, i=4)
                link(nc.vector.reciprocal(orv[:, :], ps[:, OB, 0:288].rearrange("p (k d) -> p k d", d=9)[:, :, 8]))
                rv = orv[:, :].rearrange("p (g q i) -> p g q i", g=4, q=2)
                for qt in range(2):
                    ins = nc.vector.tensor_tensor(
                        attn[:, qt, P * half:P * half + P].rearrange("p (g i d) -> p g i d", g=4, i=4),
                        o[:, :, qt, :, 0:DK], bc(rv[:, :, qt, :], 3, DK), ALU.mult)
                ins.then_inc(o_free, 1)

            def layer_norm(k, dst, src=None, n=2):
                src = res if src is None else src
                for i in range(n):
                    nc.vector.bn_stats(stats[:, i, :], src[:, i, :]).then_inc(dve_step, 1)
                    chain[0] += 1
                dve.wait_ge(dve_step, chain[0])
                if k >= 1:
                    dve.wait_ge(rstd_ready, k)
                for i in range(n):
                    ins = nc.vector.bn_aggr(mv[:, i, :], stats[:, i, :])
                ins.then_inc(var_ready, 1)
                dve.wait_ge(rstd_ready, k + 1)
                for i in range(n):
                    ins = nc.vector.tensor_scalar(dst[:, i, :], src[:, i, :], mv[:, i, 0:1], rstd[:, i:i + 1],
                                                  ALU.subtract, ALU.mult)
                return ins

            def attn_out(b):
                dve.wait_ge(wo_ready, b + 1)
                dve.wait_ge(x_in1[b % 2], 16 * (b // 2) + 16)
                link(nc.vector.tensor_tensor(res[:, :, :], ps[:, OB, :].rearrange("p (a d) -> p a d", a=2),
                                             x_sb[:, b % 2], ALU.add))
                layer_norm(2 * b, x1).then_inc(x1_ready, 1)
                dve.wait_ge(x1_ready, b + 1)
                link(nc.vector.tensor_scalar(Mt[:, :, :], x1[:, :, :], -1.0, 1.0, ALU.mult, ALU.add))
                link(nc.vector.tensor_scalar(Mt[:, :, :], Mt[:, :, :], MASK_VAL, None, ALU.mult))

            def gat(b, L):
                gl = 2 * b + L
                dve.wait_ge(pt_full, gl * PTU + 1)
                sn = ps[:, PB, 0:32].rearrange("p (t s h) -> p t s h", t=2, s=2)
                if gl >= 1:
                    dve.wait_ge(pt_full, (gl - 1) * PTU + 2)
                link(nc.vector.tensor_copy(snp[:, :, :, 0, :], sn))
                nc.vector.tensor_tensor(snr[:, :, :, :], sn, snp[:, :, :, 0, :], ALU.subtract).then_inc(pt_free, 1)
                dve.wait_ge(pt_free, gl * PTU + 1)
                link(nc.vector.tensor_copy(snp[:, :, :, 1, :], snr[:, :, :, :]))
                nc.vector.tensor_tensor(snp[:, :, :, 2, :], snr[:, :, :, :], snp[:, :, :, 1, :], ALU.subtract
                                        ).then_inc(snp_ready, 1)
                dve.wait_ge(pt_full, gl * PTU + 2)
                if gl >= 1:
                    dve.wait_ge(e_full, gl * 8)
                nc.vector.tensor_copy(snT[:, :, :], ps[0:24, PB, 0:S].bitcast(BF16).rearrange("p (s n) -> p s n", s=2)
                                      ).then_inc(pt_free, 1)

                def mask_max(q):
                    n = gl * 8 + q
                    it = q // 4
                    dve.wait_ge(e_fifth, n + 1)
                    ee = es[:, q % 2].rearrange("p a j -> p (a j)")
                    nc.vector.tensor_tensor(ee, ps[:, EB, :], ee, ALU.max).then_inc(e_free, 1)
                    dve.wait_ge(e_free, n + 1)
                    if n >= 2:
                        dve.wait_ge(p_ready, n - 1)
                    for i in range(2):
                        ins = nc.vector.tensor_tensor_reduce(
                            out=es[:, q % 2, i, :], in0=es[:, q % 2, i, :], in1=Mt[:, it, :], scale=1.0,
                            scalar=-3.0e38, op0=ALU.add, op1=ALU.max, accum_out=mx[:, q % 2, i:i + 1])
                    link(ins)
                    nc.vector.tensor_scalar(nmx[:, q % 2, :], mx[:, q % 2, :], -1.0, None, ALU.mult).then_inc(masked, 1)

                def pt_copy(q):
                    n = gl * 8 + q
                    dve.wait_ge(pt_full, gl * PTU + 2 + q + 1)
                    if n >= 2:
                        dve.wait_ge(agg_done, n - 1)
                    nc.vector.tensor_copy(PTg[:, q % 2].rearrange("p h j i -> p (h j i)"), ps[:, PB, :]).then_inc(pt_free, 1)

                def elu(it):
                    k = MISC * b + (3 if L == 0 else 7) + it
                    dve.wait_ge(agg_done, 8 * gl + 4 * it + 4)
                    link(nc.vector.reciprocal(grv[:, :], psums[:, it, :]))
                    nc.vector.tensor_tensor(z[:, it, :].rearrange("p (h o) -> p h o", h=GH),
                                            ps[:, MB, 0:D].rearrange("p (h o) -> p h o", h=GH),
                                            bc(grv[:, :], 2, GO), ALU.mult).then_inc(misc_free, 1)
                    dve.wait_ge(misc_free, k + 1)
                    link(nc.vector.tensor_tensor(z[:, it, :], z[:, it, :], bvec[:, L, :], ALU.add))
                    nc.vector.tensor_scalar(zm[:, :], z[:, it, :], 0.0, None, ALU.min).then_inc(zneg, 1)
                    dve.wait_ge(zexp, 2 * gl + it + 1)
                    nc.vector.scalar_tensor_tensor(out=z[:, it, :], in0=ze[:, :], scalar=-1.0, in1=z[:, it, :],
                                                   op0=ALU.add, op1=ALU.max).then_inc(h_ready, 1)

                for q in range(9):
                    if q < 8:
                        mask_max(q)
                    if q >= 1:
                        pt_copy(q - 1)
                    if q == 5:
                        elu(0)
                elu(1)
                if L == 1:
                    dve.wait_ge(h_ready, 4 * b + 4)
                    link(nc.vector.tensor_tensor(res[:, :, :], z[:, :, :], x1[:, :, :], ALU.add))
                    layer_norm(2 * b + 1, x2[:, 2 * b:2 * b + 2, :]).then_inc(x2_ready, 1)
                    dve.wait_ge(x2_ready, b + 1)

            def route(b):
                base = MISC * b
                dve.wait_ge(logit_ready, b + 1)
                nc.vector.tensor_tensor(lg[:, :, :], ps[:, MB, 0:2 * E].rearrange("p (t e) -> p t e", t=2),
                                        bc(gb[:, :], 1, 2), ALU.add).then_inc(misc_free, 1)
                dve.wait_ge(misc_free, base + 11)
                link(nc.vector.tensor_reduce(lmax[:, :], lg[:, :, :], AX.X, ALU.max))
                link(nc.vector.tensor_tensor(lg[:, :, :], lg[:, :, :], bc(lmax[:, :], 2, E), ALU.subtract))
                nc.vector.tensor_copy(lmax[:, :], lmax[:, :]).then_inc(lexp_in, 1)
                dve.wait_ge(lexp, b + 1)
                link(nc.vector.tensor_reduce(lsum[:, :], prob[:, :, :], AX.X, ALU.add))
                link(nc.vector.reciprocal(lsum[:, :], lsum[:, :]))
                link(nc.vector.tensor_tensor(prob[:, :, :], prob[:, :, :], bc(lsum[:, :], 2, E), ALU.mult))
                for i in range(2):
                    link(nc.vector.max(top[:, i, :], prob[:, i, :]))
                    link(nc.vector.max_index(topi[:, i, :], top[:, i, :], prob[:, i, :]))
                link(nc.vector.tensor_copy(topf[:, :, :], topi[:, :, 0:2]))
                link(nc.vector.tensor_tensor(wsum[:, :], top[:, :, 0], top[:, :, 1], ALU.add))
                link(nc.vector.reciprocal(wsum[:, :], wsum[:, :]))
                link(nc.vector.tensor_tensor(wk2[:, 2 * b:2 * b + 2, :], top[:, :, 0:2], bc(wsum[:, :], 2, 2), ALU.mult))
                for i in range(2):
                    link(nc.vector.tensor_tensor(oh[:, 2 * b + i], bc(iota_e, 1, 2), bc(topf[:, i, :], 2, E), ALU.is_equal))
                nc.vector.tensor_tensor(chosen[:, :, :], oh[:, 2 * b:2 * b + 2, 0, :], oh[:, 2 * b:2 * b + 2, 1, :], ALU.add).then_inc(chosen_ready, 1)
                dve.wait_ge(rank_ready, b + 1)
                link(nc.vector.tensor_tensor(pos[:, :, :], ps[:, MB, 0:2 * E].rearrange("p (t e) -> p t e", t=2),
                                             bc(run[:, :], 1, 2), ALU.add))
                nc.vector.tensor_tensor(run[:, :], run[:, :], ps[:, MB, 2 * E:3 * E], ALU.add).then_inc(misc_free, 1)
                link(nc.vector.tensor_tensor(pos[:, :, :], pos[:, :, :], bc(stride_e, 1, 2), ALU.add))
                for i in range(2):
                    link(nc.vector.tensor_tensor(ohp[:, i], oh[:, 2 * b + i], bc(pos[:, i, :], 1, 2), ALU.mult))
                link(nc.vector.tensor_reduce(slotf[:, 2 * b:2 * b + 2, :], ohp[:, :, :, :], AX.X, ALU.add))
                nc.vector.tensor_copy(slot[:, 2 * b:2 * b + 2, :], slotf[:, 2 * b:2 * b + 2, :]).then_inc(slots_ready, 1)
                dve.wait_ge(slots_ready, b + 1)
                dve.wait_ge(misc_free, base + 12)

            def tables():
                link(nc.vector.tensor_tensor(big[:, 0:E, :], bc(run[:, :], 2, E), bc(tile_j, 1, E), ALU.is_gt))
                link(nc.vector.tensor_reduce(tiles_e[:, :], big[:, 0:E, :], AX.X, ALU.add))
                link(nc.vector.tensor_tensor(big[:, 0:E, :], lower, bc(tiles_e[:, :], 1, E), ALU.mult))
                link(nc.vector.tensor_reduce(base_e[:, :], big[:, 0:E, :], AX.X, ALU.add))
                link(nc.vector.tensor_tensor(end_e[:, :], base_e[:, :], tiles_e[:, :], ALU.add))
                link(nc.vector.tensor_scalar(last[:, :], end_e[:, E - 1:E], -1.0, None, ALU.add))
                link(nc.vector.tensor_scalar(tcl[:, :], tau, last[:, 0:1], None, ALU.min))
                link(nc.vector.tensor_tensor(big[:, :, :], bc(tcl[:, :], 2, E), bc(end_e[:, :], 1, TILES), ALU.is_ge))
                link(nc.vector.tensor_reduce(te[:, :], big[:, :, :], AX.X, ALU.add))
                link(nc.vector.tensor_tensor(big2[:, :, :], big[:, :, :], bc(tiles_e[:, :], 1, TILES), ALU.mult))
                link(nc.vector.tensor_reduce(tb[:, :], big2[:, :, :], AX.X, ALU.add))
                link(nc.vector.tensor_tensor(trow[:, :], tcl[:, :], tb[:, :], ALU.subtract))
                link(nc.vector.tensor_scalar(trow[:, :], trow[:, :], float(P), None, ALU.mult))
                link(nc.vector.tensor_scalar(tcl[:, :], te[:, :], float(SLOT_ROWS), None, ALU.mult))
                link(nc.vector.tensor_tensor(trow[:, :], trow[:, :], tcl[:, :], ALU.add))
                link(nc.vector.tensor_tensor(padf[:, :], run[:, :], stride_e, ALU.add))
                nc.vector.tensor_copy(tab[:, 0:TILES], te[:, :]).then_inc(tab_ready, 1)
                nc.vector.tensor_copy(tab[:, TILES:2 * TILES], trow[:, :]).then_inc(tab_ready, 1)
                nc.vector.tensor_copy(tab[:, 2 * TILES:2 * TILES + E], padf[:, :]).then_inc(tab_ready, 1)
                dve.wait_ge(tab_ready, 3)
                link(nc.vector.tensor_scalar(shift[:, :], base_e[:, :], float(P), None, ALU.mult))
                link(nc.vector.tensor_tensor(shift[:, :], shift[:, :], stride_e, ALU.subtract))
                link(nc.vector.tensor_tensor(oht[:, :, :], oh[:, :, :, :].rearrange("p t k e -> p (t k) e"),
                                             bc(shift[:, :], 1, 2 * T), ALU.mult))
                link(nc.vector.tensor_reduce(tsh[:, :], oht[:, :, :], AX.X, ALU.add))
                link(nc.vector.tensor_tensor(tsh[:, :], tsh[:, :], slotf[:, :, :].rearrange("p t k -> p (t k)"), ALU.add))
                nc.vector.tensor_copy(yslot[:, :, :], tsh[:, :].rearrange("p (t k) -> p t k", k=2)).then_inc(yslots_ready, 1)

            dve.wait_ge(rt_in, 64)
            for b in range(B):
                maxima(b)
                normalise(b, 0)
                normalise(b, 1)
                attn_out(b)
                gat(b, 0)
                gat(b, 1)
                route(b)
            tables()

            def x_copy(n, par):
                wait(dve, h_full, 2 * n - 2)
                dve.wait_ge(x_turned, n + 1)
                nc.vector.tensor_copy(xgT[:, par].rearrange("p k n -> p (k n)"), ps[:, par, 0:D]).then_inc(xgT_ready, 1)

            def h_copy(n, par):
                wait(dve, ht_full, 2 * n - 2)
                dve.wait_ge(h_full, 2 * n + 2)
                nc.vector.tensor_copy(hs[:, par, 512:F], ps[:, 3, :]).then_inc(hs_d, 1)

            def y_add(n, par):
                wait(dve, y_stored[par], 8 * (n - par))
                dve.wait_ge(y_full, n + 1)
                e = dve.value_load(tab[0:1, bass.ds(n, 1)], min_val=0, max_val=E - 1)
                nc.vector.tensor_tensor(ys[:, par, :], ps[:, 6 + par, 0:D],
                                        b2s[:, bass.ds(e, 1), :].rearrange("p o d -> p (o d)"), ALU.add).then_inc(y_out, 1)

            def step(n, par):
                x_copy(n + 1, 1 - par)
                h_copy(n, par)
                y_add(n - 1, 1 - par)

            dve.wait_ge(b2_in, 16 * E)
            x_copy(0, 0)
            x_copy(1, 1)
            h_copy(0, 0)
            step(1, 1)
            step(2, 0)
            tiles_of(dve, step)
            step(21, 1)
            h_copy(22, 0)
            y_add(21, 1)
            y_add(22, 0)

            for half in range(2):
                dve.wait_ge(gathered[half], 16 * 8)
                for k in range(2):
                    for i in range(4 * half, 4 * half + 4):
                        ins = nc.vector.scalar_tensor_tensor(out=x2[:, i, :], in0=yg[:, i, k, :], scalar=wk2[:, i, k:k + 1],
                                                             in1=x2[:, i, :], op0=ALU.mult, op1=ALU.add)
                    link(ins)
                h4 = slice(4 * half, 4 * half + 4)
                layer_norm(2 * B + half, outs[:, h4, :], x2[:, h4, :], 4).then_inc(out_ready, 1)

        @block.tensor
        def _(pe):
            pe.wait_ge(ld_x, 64)
            for c in range(2):
                for e in range(2):
                    for k in range(2):
                        nc.tensor.matmul(ps[:, 4 * c + e, :], wq[:, k, 128 * e:128 * e + 128],
                                         xT[:, k, 512 * c:512 * c + 512], start=(k == 0), stop=(k == 1))
                for e in range(2):
                    for k in range(2):
                        ins = nc.tensor.matmul(ps[0:32, 4 * c + 2 + e, :], wk[:, k, 32 * e:32 * e + 32],
                                               xT[:, k, 512 * c:512 * c + 512], start=(k == 0), stop=(k == 1))
                ins.then_inc(proj_ready, 1)
            pe.wait_ge(rot_done, 1)
            for tt in range(T):
                for k in range(2):
                    ins = nc.tensor.matmul(ps[:, SB[0], 64 * tt:64 * tt + 64], xT[:, k, 128 * tt:128 * tt + 128],
                                           wv[:, k, :], start=(k == 0), stop=(k == 1))
            ins.then_inc(v_ready, 1)
            pe.wait_ge(consts_ready, 7)
            pe.wait_ge(v_done, 1)
            pe.wait_ge(rot_done, 4)

            def scores(b):
                pe.wait_ge(stacks_in[b], 16 * 24)
                for n in range(HKV * SLOTS):
                    g, u = n // SLOTS, n % SLOTS
                    par, gg = g % 2, g // 2
                    lo = 64 * par
                    k = b * HKV * SLOTS + n
                    if k >= 2:
                        pe.wait_ge(s_free, k - 1)
                    bank = ps[:, SB[k % 2], :]
                    if u == 0:
                        nc.tensor.matmul(bank.rearrange("p (h j) -> p h j", h=4), maskS[:, :], bc(ident_b[:, :], 1, 4),
                                         start=True, stop=False, skip_group_check=True)
                        for i in range(4):
                            ins = nc.tensor.matmul(bank[:, 128 * i:128 * i + 128],
                                                   QS[lo:lo + DATA_ROWS, b % 2, 4 * gg + i, 0:128],
                                                   KS[lo:lo + DATA_ROWS, b % 2, gg, 0:128],
                                                   start=False, stop=True, skip_group_check=True)
                    else:
                        nc.tensor.matmul(bank.rearrange("p (h j) -> p h j", h=2)[:, :, 128:256], maskS[:, :],
                                         bc(ident_b[:, :], 1, 2), start=True, stop=False, skip_group_check=True)
                        for i in range(2):
                            ins = nc.tensor.matmul(bank[:, 256 * i:256 * i + 256],
                                                   QS[lo:lo + DATA_ROWS, b % 2, 4 * gg + 2 * u - 2 + i, 128:256],
                                                   KS[lo:lo + DATA_ROWS, b % 2, gg, 0:256],
                                                   start=False, stop=True, skip_group_check=True)
                    ins.then_inc(s_full, 1)

            def misc_wait(k):
                if k >= 1:
                    pe.wait_ge(misc_free, k)

            def turn_maxima(b):
                pe.wait_ge(mparts, b + 1)
                misc_wait(MISC * b)
                dst = ps[0:64, MB, 0:S // 2].bitcast(BF16)
                for qt in range(2):
                    ins = nc.tensor.transpose(dst[:, 128 * qt:128 * qt + 128],
                                              mb[:, qt].rearrange("p a b h -> p (a b h)"), ident_b[:, :])
                ins.then_inc(misc_full, 1)

            def scores_t(b):
                pe.wait_ge(maxrows_in[b], 16 * 4)
                KR = DATA_ROWS + MAX_ROWS
                for n in range(HKV * SLOTS + SLOTS):
                    g, u = n // SLOTS, n % SLOTS
                    par, gg = g % 2, g // 2
                    lo = 64 * par
                    k = b * HKV * SLOTS + n
                    if g < HKV:
                        if k >= 2:
                            pe.wait_ge(t_free, k - 1)
                        bank = ps[:, TB[k % 2], :]
                        if u < 2:
                            nc.tensor.matmul(bank.rearrange("p (h j) -> p h j", h=2)[:, :, 0:128], maskT[:, :],
                                             bc(ident_b[:, :], 1, 2), start=True, stop=False, skip_group_check=True)
                            ins = nc.tensor.matmul(bank.rearrange("p (h j) -> p h j", h=2),
                                                   KS[lo:lo + KR, b % 2, gg, 0:128],
                                                   QS[lo:lo + KR, b % 2, 4 * gg + 2 * u:4 * gg + 2 * u + 2, :],
                                                   start=False, stop=True, skip_group_check=True)
                        else:
                            nc.tensor.matmul(bank.rearrange("p (h j) -> p h j", h=4), maskT[:, :],
                                             bc(ident_b[:, :], 1, 4), start=True, stop=False, skip_group_check=True)
                            ins = nc.tensor.matmul(bank.rearrange("p (h j) -> p h j", h=4),
                                                   KS[lo:lo + KR, b % 2, gg, 128:256],
                                                   QS[lo:lo + KR, b % 2, 4 * gg:4 * gg + 4, 128:256],
                                                   start=False, stop=True, skip_group_check=True)
                        ins.then_inc(t_full, 1)
                    if u == SLOTS - 1 and g >= 1:
                        values(b, g - 1)

            def values(b, g):
                pe.wait_ge(t_free, b * HKV * SLOTS + g * SLOTS + SLOTS)
                half = g // 4
                if g % 4 == 0:
                    if half == 0:
                        if b >= 1:
                            pe.wait_ge(x1_ready, b)
                    else:
                        pe.wait_ge(o_free, 2 * b + 1)
                o = ps[:, OB, 0:288].rearrange("p (g q i d) -> p g q i d", g=4, q=2, i=4)
                pt = PT[:, g % 2]
                for i in range(4):
                    c0 = (i % 2) * 256
                    nc.tensor.matmul(o[:, g % 4, 0, i, :], pt[:, i // 2, c0:c0 + 128], V[:, 2 * b, g, :],
                                     start=True, stop=True)
                    nc.tensor.matmul(o[:, g % 4, 1, i, :], pt[:, i // 2, c0 + 128:c0 + 256], V[:, 2 * b, g, :],
                                     start=True, stop=False)
                    ins = nc.tensor.matmul(o[:, g % 4, 1, i, :], pt[:, 2, 128 * i:128 * i + 128], V[:, 2 * b + 1, g, :],
                                           start=False, stop=True)
                ins.then_inc(pv_done, 1)

            def turn(dst, src_tile, src_k):
                for a in range(2):
                    for f in range(2):
                        ins = nc.tensor.transpose(dst[:, a * 256 + 128 * f:a * 256 + 128 * f + 128],
                                                  src_tile[:, f, 128 * a:128 * a + 128], ident[:, :])
                return ins

            def attn_proj(b):
                pe.wait_ge(o_free, 2 * b + 2)
                misc_wait(MISC * b + 1)
                turn(ps[:, MB, :], attn, 0).then_inc(misc_full, 1)
                pe.wait_ge(misc_free, MISC * b + 2)
                pe.wait_ge(ld_w, 16)
                for qt in range(2):
                    for k in range(2):
                        ins = nc.tensor.matmul(ps[:, OB, 256 * qt:256 * qt + 256], attnT[:, k, 128 * qt:128 * qt + 128],
                                               wo[:, k, :], start=(k == 0), stop=(k == 1))
                ins.then_inc(wo_ready, 1)

            def gat(b, L):
                gl = 2 * b + L
                base = MISC * b + (2 if L == 0 else 6)
                kt = 1 if L == 0 else 2
                src = (lambda k, it: ctxT[:, S * b + 128 * it:S * b + 128 * it + 128]) if L == 0 else \
                      (lambda k, it: h1T[:, k, 128 * it:128 * it + 128])
                w = (lambda k: w0[:, :]) if L == 0 else (lambda k: w1g[:, k, :])
                wa = (lambda k: wa0[:, :]) if L == 0 else (lambda k: wa1[:, k, :])
                misc_wait(base)
                for it in range(2):
                    for k in range(kt):
                        ins = nc.tensor.matmul(ps[:, MB, 256 * it:256 * it + 256], src(k, it), w(k),
                                               start=(k == 0), stop=(k == kt - 1))
                ins.then_inc(misc_full, 1)
                if gl >= 1:
                    pe.wait_ge(pt_free, gl * PTU)
                for it in range(2):
                    for k in range(kt):
                        ins = nc.tensor.matmul(ps[:, PB, 16 * it:16 * it + 16], src(k, it), wa(k),
                                               start=(k == 0), stop=(k == kt - 1))
                ins.then_inc(pt_full, 1)
                pe.wait_ge(snp_ready, gl + 1)
                pe.wait_ge(pt_free, gl * PTU + 1)
                dst = ps[0:24, PB, 0:S].bitcast(BF16).rearrange("p (s n) -> p s n", s=2)
                for s in range(2):
                    for it in range(2):
                        ins = nc.tensor.transpose(dst[:, s, 128 * it:128 * it + 128],
                                                  snp[:, it, s].rearrange("p a h -> p (a h)"), ident_b[:, :])
                ins.then_inc(pt_full, 1)
                pe.wait_ge(pt_free, gl * PTU + 2)

                def e_mm(q):
                    n = gl * 8 + q
                    it, hp = q // 4, q % 4
                    if n >= 1:
                        pe.wait_ge(e_free, n)
                    nc.tensor.matmul(ps[:, EB, :].rearrange("p (h j) -> p h j", h=2), snT[:, 0, 128 * it:128 * it + 128],
                                     delta[:, 2 * hp:2 * hp + 2, :], start=True, stop=False, skip_group_check=True)
                    for i in range(2):
                        ins = nc.tensor.matmul(ps[:, EB, 256 * i:256 * i + 256], delta[:, 2 * hp + i, 0:128], snT[:, 1, :],
                                               start=False, stop=True, skip_group_check=True)
                    ins.then_inc(e_full, 1)

                def turn_p(q):
                    pe.wait_ge(p_ready, gl * 8 + q + 1)
                    pe.wait_ge(pt_free, gl * PTU + 2 + q)
                    for i in range(2):
                        for jt in range(2):
                            c0 = 256 * i + 128 * jt
                            ins = nc.tensor.transpose(ps[:, PB, c0:c0 + 128], Pm[:, q % 2, i, 128 * jt:128 * jt + 128],
                                                      ident[:, :])
                    ins.then_inc(pt_full, 1)

                def agg(q):
                    it, hp = q // 4, q % 4
                    pe.wait_ge(pt_free, gl * PTU + 2 + q + 1)
                    if hp == 0:
                        pe.wait_ge(misc_free, base + 1 + it)
                    for i in range(2):
                        h = 2 * hp + i
                        for jt in range(2):
                            ins = nc.tensor.matmul(ps[:, MB, GO * h:GO * h + GO], PTg[:, q % 2, i, jt, :],
                                                   feat[:, jt, GO * h:GO * h + GO], start=(jt == 0), stop=(jt == 1))
                    ins.then_inc(agg_done, 1)

                for q in range(10):
                    if q < 8:
                        e_mm(q)
                    if 1 <= q <= 8:
                        turn_p(q - 1)
                    if q >= 2:
                        agg(q - 2)
                if L == 0:
                    pe.wait_ge(h_ready, 4 * b + 2)
                    pe.wait_ge(misc_free, base + 3)
                    turn(ps[:, MB, :], z, 0).then_inc(misc_full, 1)

            def router(b):
                base = MISC * b
                pe.wait_ge(x2_ready, b + 1)
                misc_wait(base + 9)
                turn(ps[:, MB, :], x2[:, 2 * b:2 * b + 2, :], 0).then_inc(misc_full, 1)
                pe.wait_ge(misc_free, base + 10)
                for i in range(2):
                    for k in range(2):
                        ins = nc.tensor.matmul(ps[:, MB, E * i:E * i + E], x2T[:, k, 128 * i:128 * i + 128], gw[:, k, :],
                                               start=(k == 0), stop=(k == 1))
                ins.then_inc(logit_ready, 1)
                pe.wait_ge(chosen_ready, b + 1)
                pe.wait_ge(misc_free, base + 11)
                nc.tensor.matmul(ps[:, MB, 0:E], before[:, :], chosen[:, 0, :], start=True, stop=True)
                nc.tensor.matmul(ps[:, MB, E:2 * E], before[:, :], chosen[:, 1, :], start=True, stop=False)
                nc.tensor.matmul(ps[:, MB, E:2 * E], ones_b[:, :], chosen[:, 0, :], start=False, stop=True)
                nc.tensor.matmul(ps[:, MB, 2 * E:3 * E], ones_b[:, :], chosen[:, 0, :], start=True, stop=False)
                nc.tensor.matmul(ps[:, MB, 2 * E:3 * E], ones_b[:, :], chosen[:, 1, :], start=False, stop=True
                                 ).then_inc(rank_ready, 1)

            pe.wait_ge(rt_in, 64)
            pe.wait_ge(ld_gat, 16 * 9)
            pe.wait_ge(wa_ready, 6)
            for b in range(B):
                scores(b)
                turn_maxima(b)
                scores_t(b)
                attn_proj(b)
                gat(b, 0)
                gat(b, 1)
                router(b)

            pe.wait_ge(tab_ready, 3)

            def turn_x(n, par):
                wait(pe, xgT_ready, n - 1)
                pe.wait_ge(xg_in[par], 8 * (n - par) + 16)
                for k in range(2):
                    ins = nc.tensor.transpose(ps[:, par, 128 * k:128 * k + 128], xg[:, par, 128 * k:128 * k + 128],
                                              ident[:, :])
                ins.then_inc(x_turned, 1)

            def expert(n):
                return pe.value_load(tab[0:1, bass.ds(n, 1)], min_val=0, max_val=E - 1)

            w1f = w1[:, :, :, :].rearrange("p e k f -> p (e k f)")
            w2flat = w2[:, :, :, :].rearrange("p e k d -> p (e k d)")

            def mm1(n, par):
                e = expert(n)
                pe.wait_ge(xgT_ready, n + 1)
                for half in range(2):
                    wait(pe, hs_d if half else hs_a, n)
                    for k in range(2):
                        ins = nc.tensor.matmul(ps[:, 2 + half, :], xgT[:, par, k, :],
                                               w1f[:, bass.ds(e * (2 * F) + (k * F + 512 * half), 512)],
                                               start=(k == 0), stop=(k == 1))
                    ins.then_inc(h_full, 1)

            def turn_h(n, par):
                for half in range(2):
                    pe.wait_ge(hs_d if half else hs_a, n + 1)
                    wait(pe, g_ready, n)
                    for k in range(4 * half, 4 * half + 4):
                        ins = nc.tensor.transpose(ps[:, 4 + half, 128 * (k % 4):128 * (k % 4) + 128],
                                                  hs[:, par, 128 * k:128 * k + 128], ident[:, :])
                    ins.then_inc(ht_full, 1)

            def mm2(n, par):
                e = expert(n)
                pe.wait_ge(g_ready, n + 1)
                wait(pe, y_out, n - 1)
                for k in range(8):
                    ins = nc.tensor.matmul(ps[:, 6 + par, 0:D], gT[:, par, k, :],
                                           w2flat[:, bass.ds(e * (8 * D) + k * D, D)], start=(k == 0), stop=(k == 7))
                ins.then_inc(y_full, 1)

            def step(n, par):
                turn_x(n + 1, 1 - par)
                mm1(n, par)
                mm2(n - 1, 1 - par)
                turn_h(n, par)

            pe.wait_ge(w1_in, 16 * E)
            pe.wait_ge(w2a_in, 16 * 2)
            pe.wait_ge(w2b_in, 16 * (E - 2))
            turn_x(0, 0)
            turn_x(1, 1)
            mm1(0, 0)
            turn_h(0, 0)
            step(1, 1)
            step(2, 0)
            tiles_of(pe, step)
            step(21, 1)
            mm1(22, 0)
            mm2(21, 1)
            turn_h(22, 0)
            mm2(22, 0)


def kernel(**inputs):
    import numpy as np
    import concourse.bacc as bacc
    from concourse import mybir as mb_
    from concourse.bass_utils import run_bass_kernel_spmd as run

    f32 = np.float32
    i = {k.replace("L0_", ""): np.asarray(v) for k, v in inputs.items()}
    wq = i["attn_Wq"].reshape(D, 4, 2, 4, 4, 2)
    wk = i["attn_Wk"].reshape(D, 4, 2, 4, 2)
    s = np.arange(S, dtype=f32)
    theta = (f32(1.0) / f32(10000.0) ** (f32(2.0) * np.arange(DK // 2, dtype=f32) / f32(DK))).astype(f32)
    ang = (s[None, :] * theta[:, None]).astype(f32)
    rope = np.stack([np.cos(ang), np.sin(ang)], 1).astype(f32)
    r = np.arange(P)
    above = np.where(r[:, None] > r[None, :], f32(-3.0e38), f32(0.0)).astype(f32)
    arrays = {
        "xT": i["x"].reshape(N, D).T, "x": i["x"].reshape(N, D), "ctxT": i["ctx_512"].reshape(N, FIN).T,
        "wq": wq.transpose(0, 5, 2, 4, 1, 3).reshape(D, 256),
        "wk": wk.transpose(0, 4, 2, 3, 1).reshape(D, 64),
        "wv": i["attn_Wv"], "wo": i["attn_Wo"],
        "w0": i["xattn_W0"].transpose(1, 0, 2).reshape(FIN, D),
        "w1g": i["xattn_W1"].transpose(1, 0, 2).reshape(D, D),
        "avec": np.stack([i["xattn_" + n].reshape(D) for n in ("a_self0", "a_neigh0", "a_self1", "a_neigh1", "b0", "b1")]),
        "ident": np.eye(P, dtype=f32),
        "cmask": np.stack([above, above.T], 1),
        "ropeq": np.tile(np.repeat(rope, 16, 0), (2, 1, 1)),
        "ropek": np.tile(np.repeat(rope, 4, 0), (2, 1, 1)),
        "umat": (r[:, None] < r[None, :]).astype(f32),
        "gw": i["ffn_gate_w"], "gb": i["ffn_gate_b"],
        "rowc": np.concatenate([np.arange(E), np.arange(E) * SLOT_ROWS, np.arange(E) * P,
                                (np.arange(E)[None, :] < np.arange(E)[:, None]).reshape(-1), np.arange(24)]).astype(f32),
        "b1": i["ffn_b1"].reshape(E, 8, P).transpose(2, 0, 1), "b2": i["ffn_b2"],
        "w1": i["ffn_w1"], "w2": i["ffn_w2"],
        "delta": np.tile(np.eye(GH, dtype=f32), (3, 1)),
    }
    nc = bacc.Bacc("TRN2", target_bir_lowering=False, num_devices=1)
    t = {}
    for k in arrays:
        arrays[k] = np.ascontiguousarray(arrays[k])
        t[k] = nc.dram_tensor("in_" + k, arrays[k].shape, mb_.dt.from_np(arrays[k].dtype), kind="ExternalInput").ap()
    out = nc.dram_tensor("out_0_dram", (N, D), F32, kind="ExternalOutput").ap()
    decoder_layer(nc, t, out)
    got = run(nc, [{"in_" + k: v for k, v in arrays.items()}], core_ids=[0])
    return got.results[0]["out_0_dram"].reshape(B, S, D)
```

```python
from contextlib import ExitStack

import concourse.bass as bass
from concourse import mybir

F32 = mybir.dt.float32
BF16 = mybir.dt.bfloat16
F16 = mybir.dt.float16
U32 = mybir.dt.uint32
I32 = mybir.dt.int32
ALU = mybir.AluOpType
ACT = mybir.ActivationFunctionType
AX = mybir.AxisListType

P = 128
B, S, D = 4, 256, 256
N = B * S
T = N // P
H, HKV, DK = 32, 8, 8
G = H // HKV
GH, GO, FIN = 8, 32, 64
E, F = 8, 1024
SCALE = float(DK) ** -0.5
MASK_VAL = -10000000000.0
EPS = 1e-5
Q_PART = (0, 0, 1, 1, 0, 2)
K_PART = (0, 1, 0, 1, 2, 0)
DATA_ROWS = 8 * len(Q_PART)
MAX_ROWS = 2
SLOTS = 3
SLOT_ROWS = N + P
TILES = 2 * N // P + E - 1
PTU = 10


def bc(ap, axis, n):
    a = ap.unsqueeze(axis)
    shape = list(a.shape)
    shape[axis] = n
    return a.to_broadcast(shape)


def misc_uses():
    uses = {}
    for b in range(B):
        for L in range(2):
            uses.update({("feat", b, L): True, ("agg", b, L, 0): False, ("agg", b, L, 1): False})
            if L == 0:
                uses[("h1", b)] = True
        uses.update({("x2", b): True, ("logits", b): False, ("ranks", b): False})
    return uses


def decoder_layer(nc, t, out):
    with ExitStack() as ctx:
        def sb(name, shape, dt=F32):
            return ctx.enter_context(nc.sbuf_tensor(name, shape, dt))

        def sem(name):
            return ctx.enter_context(nc.semaphore(name))

        ps = ctx.enter_context(nc.psum_tensor("ps", [P, 8, 512], F32))
        SB, EB, PB, OB, MB = (0, 1), (2, 3), (4, 5), 6, 7

        w1 = sb("w1", [P, E, 2, F])
        w2 = sb("w2", [P, E, 8, D])
        work = sb("work", [P, 8192])

        def carver(area):
            at = [0]

            def carve(shape, dt=F32):
                size = 1
                for n in shape[1:]:
                    size *= n
                words = size if dt in (F32, U32, I32) else size // 2
                ap = area[0:shape[0], at[0]:at[0] + words]
                at[0] += words
                assert at[0] <= area.shape[1], (at[0], shape)
                if dt is not F32:
                    ap = ap.bitcast(dt)
                names = "abcdef"[:len(shape) - 1]
                if len(shape) == 2:
                    return ap
                return ap.rearrange("p (" + " ".join(names) + ") -> p " + " ".join(names),
                                    **{n: v for n, v in zip(names[1:], shape[2:])})
            return carve

        carve = carver(w1[:, :, :, :].rearrange("p e k f -> p (e k f)"))
        cmask = carve([P, 2, P])
        umat = carve([P, P])
        ropeq = carve([P, 2, S])
        ropek = carve([32, 2, S])
        xT = carve([P, 2, N])
        wq = carve([P, 2, 256])
        wk = carve([P, 2, 64])
        wv = carve([P, 2, 64])
        avec = carve([P, 4, D])
        watmp = carve([P, D])
        rc = carve([P, 2, 512])
        rs = carve([P, 2, 512])
        rot = carve([P, 2, 512])
        qp = carve([P, 2, 3, 2, 512], BF16)
        kp = carve([32, 2, 3, 2, 512], BF16)
        carve = carver(w2[:, 2:E].rearrange("p e k f -> p (e k f)"))
        QS = carve([P, 2, 16, S], BF16)
        KS = carve([P, 2, 4, S], BF16)
        PT = carve([P, 2, SLOTS, 512])
        V = carve([P, T, HKV, DK])
        VW = carve([P, 2, 64 * 2 * HKV + 24])
        mneg = carve([P, 2, 2, 16])
        mb = carve([P, 2, 2, MAX_ROWS, 16], BF16)
        mT = carve([64, 2, S], BF16)
        carve = carver(work[:, :])
        es = carve([P, 2, 2, S])
        Pm = carve([P, 2, 2, S])
        PTg = carve([P, 2, 2, 2, P])
        Mt = carve([P, 2, S])
        feat = carve([P, 2, D])
        z = carve([P, 2, D])
        zm = carve([P, D])
        ze = carve([P, D])
        h1T = carve([P, 2, S])
        w1g = carve([P, 2, D])
        x2T = carve([P, 2, S])
        orv = carve([32, 2, S])
        attnT = carve([P, 2, S])
        wo = carve([P, 2, D])
        carve = carver(work[:, :])
        xg = carve([P, 2, D])
        xgT = carve([P, 2, 2, P])
        hs = carve([P, 2, F])
        gT = carve([P, 2, 8, P])
        ys = carve([P, 2, D])
        b2s = carve([P, E, D])
        carve = carver(w1[:, :, :, :].rearrange("p e k f -> p (e k f)"))
        yg = carve([P, T, 2, D])
        outs = carve([P, T, D])
        ident = sb("ident", [P, P])
        ident_b = sb("ident_b", [P, P], BF16)
        maskS = sb("maskS", [P, P], BF16)
        maskT = sb("maskT", [P, P], BF16)
        before = sb("before", [P, P], BF16)
        ones_b = sb("ones_b", [P, P], BF16)
        delta8 = sb("delta8", [24, GH])
        delta = sb("delta", [24, GH, S], BF16)
        x_sb = sb("x_sb", [P, 2, 2, D])
        ctxT = sb("ctxT", [FIN, N])
        w0 = sb("w0", [FIN, D])
        bvec = sb("bvec", [P, 2, D])
        wa0 = sb("wa0", [FIN, 16])
        wa1 = sb("wa1", [P, 2, 16])
        res = sb("res", [P, 2, D])
        stats = sb("stats", [P, T, 6])
        mv = sb("mv", [P, T, 2])
        vare = sb("vare", [P, T])
        rstd = sb("rstd", [P, T])
        mhalf = sb("mhalf", [P, T])
        x1 = sb("x1", [P, 2, D])
        x2 = sb("x2", [P, T, D])
        snp = sb("snp", [P, 2, 2, 3, GH], BF16)
        snr = sb("snr", [P, 2, 2, GH])
        snT = sb("snT", [24, 2, S], BF16)
        mx = sb("mx", [P, 2, 2])
        nmx = sb("nmx", [P, 2, 2])
        psums = sb("psums", [P, 2, GH])
        grv = sb("grv", [P, GH])
        gw = sb("gw", [P, 2, E])
        gb = sb("gb", [P, E])
        rowc = sb("rowc", [P, 3 * E + E * E + 24])
        iota_e, stride_e, tile_j = (rowc[:, E * i:E * i + E] for i in range(3))
        lower = rowc[:, 3 * E:3 * E + E * E].rearrange("p (a b) -> p a b", a=E)
        tau = rowc[:, 3 * E + E * E:3 * E + E * E + TILES]
        lg = sb("lg", [P, 2, E])
        lmax = sb("lmax", [P, 2])
        lsum = sb("lsum", [P, 2])
        prob = sb("prob", [P, 2, E])
        top = sb("top", [P, 2, 8])
        topi = sb("topi", [P, 2, 8], U32)
        topf = sb("topf", [P, 2, 2])
        wsum = sb("wsum", [P, 2])
        wk2 = sb("wk2", [P, T, 2])
        oh = sb("oh", [P, T, 2, E])
        chosen = sb("chosen", [P, 2, E], BF16)
        run = sb("run", [P, E])
        pos = sb("pos", [P, 2, E])
        ohp = sb("ohp", [P, 2, 2, E])
        slotf = sb("slotf", [P, T, 2])
        shift = sb("shift", [P, E])
        tsh = sb("tsh", [P, 2 * T])
        oht = sb("oht", [P, T * 2, E])
        yslot = sb("yslot", [P, T, 2], I32)
        slot = sb("slot", [P, T, 2], I32)
        big = sb("big", [P, TILES, E])
        big2 = sb("big2", [P, TILES, E])
        tiles_e = sb("tiles_e", [P, E])
        base_e = sb("base_e", [P, E])
        end_e = sb("end_e", [P, E])
        tcl = sb("tcl", [P, TILES])
        te = sb("te", [P, TILES])
        tb = sb("tb", [P, TILES])
        trow = sb("trow", [P, TILES])
        last = sb("last", [P, 1])
        tab = sb("tab", [P, 2 * TILES + E], I32)
        padf = sb("padf", [P, E])
        zero = sb("zero", [P, D])
        b1s = sb("b1s", [P, E, 8])
        b1t = sb("b1t", [P, 2, 8])

        qd = nc.dram_tensor("q_parts", (2, 2, 3, 8, 16, 512), BF16, kind="Internal").ap()
        kd = nc.dram_tensor("k_parts", (2, 2, 3, 8, 4, 512), BF16, kind="Internal").ap()
        xd = nc.dram_tensor("x_rows", (E * SLOT_ROWS, D), F32, kind="Internal").ap()
        yd = nc.dram_tensor("y_rows", (TILES * P, D), F32, kind="Internal").ap()

        ld_const, ld_x, ld_w, ld_gat = (sem(n) for n in ("ld_const", "ld_x", "ld_w", "ld_gat"))
        consts_ready = sem("consts_ready")
        ones_ready = sem("ones_ready")
        proj_ready = sem("proj_ready")
        v_ready = sem("v_ready")
        v_done = sem("v_done")
        vw_ready = sem("vw_ready")
        rot_done = sem("rot_done")
        part_a = sem("part_a")
        rem_a = sem("rem_a")
        parts_out = [sem(f"parts_out{c}") for c in range(2)]
        stacks_in = [sem(f"stacks_in{b}") for b in range(B)]
        maxrows_in = [sem(f"maxrows_in{b}") for b in range(B)]
        s_full, s_free = sem("s_full"), sem("s_free")
        mparts = sem("mparts")
        mt_full, mt_free = sem("mt_full"), sem("mt_free")
        misc_full, misc_free = sem("misc_full"), sem("misc_free")
        t_full, t_free = sem("t_full"), sem("t_free")
        pv_done = sem("pv_done")
        o_full, o_free = sem("o_full"), sem("o_free")
        wo_ready, x1_ready = sem("wo_ready"), sem("x1_ready")
        var_ready, rstd_ready = sem("var_ready"), sem("rstd_ready")
        wa_ready = sem("wa_ready")
        pt_full, pt_free = sem("pt_full"), sem("pt_free")
        snp_ready = sem("snp_ready")
        e_full, e_free, e_fifth = sem("e_full"), sem("e_free"), sem("e_fifth")
        masked = sem("masked")
        p_ready = sem("p_ready")
        agg_done = sem("agg_done")
        zneg, zexp = sem("zneg"), sem("zexp")
        h_ready = sem("h_ready")
        x2_ready = sem("x2_ready")
        dve_step, act_step, pool_step = sem("dve_step"), sem("act_step"), sem("pool_step")
        stored = sem("stored")
        w1_in, w2a_in, w2b_in, rt_in = sem("w1_in"), sem("w2a_in"), sem("w2b_in"), sem("rt_in")
        x_in1 = [sem(f"x_in1_{i}") for i in range(2)]
        logit_ready, lexp_in, lexp = sem("logit_ready"), sem("lexp_in"), sem("lexp")
        chosen_ready, rank_ready = sem("chosen_ready"), sem("rank_ready")
        slots_ready, scattered = sem("slots_ready"), sem("scattered")
        yslots_ready = sem("yslots_ready")
        tab_ready, padded = sem("tab_ready"), sem("padded")
        xg_in, x_turned, xgT_ready = [sem(f"xg_in{i}") for i in range(2)], sem("x_turned"), sem("xgT_ready")
        h_full, hs_a, hs_d, ht_full = sem("h_full"), sem("hs_a"), sem("hs_d"), sem("ht_full")
        b1_ready, g_ready, y_full, y_out = (sem(n) for n in ("b1_ready", "g_ready", "y_full", "y_out"))
        y_stored = [sem(f"y_stored{i}") for i in range(2)]
        b2_in = sem("b2_in")
        gathered = [sem(f"gathered{i}") for i in range(2)]
        zero_ready = sem("zero_ready")
        out_ready = sem("out_ready")

        uses = misc_uses()

        def use(*name):
            return list(uses).index(name)

        def turned(*name):
            return sum(list(uses.values())[:use(*name)])

        def wait(eng, sm, value):
            if not isinstance(value, int) or value > 0:
                eng.wait_ge(sm, value)

        def tiles_of(eng, step):
            with eng.Fori(1, 10) as i:
                step(2 * i + 1, 1)
                step(2 * i + 2, 0)

        block = ctx.enter_context(nc.Block())
        LN_OPS = 2

        @block.sync
        def _(sp):
            sp.dma_start(xT[:, :, :], t["xT"].rearrange("(k p) n -> p k n", p=P)).then_inc(ld_x, 16)
            sp.dma_start(wq[:, :, :], t["wq"].rearrange("(k p) n -> p k n", p=P)).then_inc(ld_x, 16)
            sp.dma_start(wk[:, :, :], t["wk"].rearrange("(k p) n -> p k n", p=P)).then_inc(ld_x, 16)
            sp.dma_start(wv[:, :, :], t["wv"].rearrange("(k p) n -> p k n", p=P)).then_inc(ld_x, 16)
            x_tok = t["x"].rearrange("(b t p) d -> b p t d", b=B, p=P)
            for b in range(2):
                sp.dma_start(x_sb[:, b], x_tok[b]).then_inc(x_in1[b], 16)
            sp.dma_start(wo[:, :, :], t["wo"].rearrange("(k p) n -> p k n", p=P)).then_inc(ld_w, 16)
            sp.dma_start(ctxT[:, :], t["ctxT"]).then_inc(ld_gat, 16)
            sp.dma_start(w0[:, :], t["w0"]).then_inc(ld_gat, 16)
            sp.dma_start(w1g[:, :, :], t["w1g"].rearrange("(k p) n -> p k n", p=P)).then_inc(ld_gat, 16)
            sp.dma_start(bvec[:, 0, :], t["avec"][4, :].partition_broadcast(P)).then_inc(ld_gat, 16)
            sp.dma_start(bvec[:, 1, :], t["avec"][5, :].partition_broadcast(P)).then_inc(ld_gat, 16)
            sp.dma_start(gw[:, :, :], t["gw"].rearrange("(k p) n -> p k n", p=P)).then_inc(rt_in, 16)
            sp.dma_start(gb[:, :], t["gb"].partition_broadcast(P)).then_inc(rt_in, 16)
            sp.dma_start(rowc[:, :], t["rowc"].partition_broadcast(P)).then_inc(rt_in, 16)
            sp.dma_start(b1s[:, :, :], t["b1"]).then_inc(rt_in, 16)
            for i in range(4):
                sp.dma_start(avec[:, i, :], t["avec"][i, :].partition_broadcast(P)).then_inc(ld_gat, 16)

            def parts(c):
                sp.wait_ge(rem_a, 4 * (c + 1))
                sp.wait_ge(part_a, 4 * (c + 1))
                for par in range(2):
                    sp.dma_start(qd[c, par].rearrange("a (e p) h n -> (p h) (a e) n", e=2),
                                 qp[64 * par:64 * par + 64, c].rearrange("p a e n -> p (a e) n")
                                 ).then_inc(parts_out[c], 16)
                    sp.dma_start(kd[c, par].rearrange("a (e p) h n -> (p h) (a e) n", e=2),
                                 kp[16 * par:16 * par + 16, c].rearrange("p a e n -> p (a e) n")
                                 ).then_inc(parts_out[c], 16)

            def stacks(b):
                c, half = b // 2, b % 2
                sp.wait_ge(parts_out[c], 4 * 16)
                if b >= 2:
                    sp.wait_ge(t_full, HKV * SLOTS * (b - 1))
                tok = slice(S * half, S * half + S)
                for j in range(len(Q_PART)):
                    for par in range(2):
                        rows = slice(64 * par + 8 * j, 64 * par + 8 * j + 8)
                        sp.dma_start(QS[rows, b % 2, :, :], qd[c, par, Q_PART[j], :, :, tok]
                                     ).then_inc(stacks_in[b], 16)
                        sp.dma_start(KS[rows, b % 2, :, :], kd[c, par, K_PART[j], :, :, tok]
                                     ).then_inc(stacks_in[b], 16)

            def max_rows(b):
                sp.wait_ge(mt_free, b + 1)
                for par in range(2):
                    for part in range(MAX_ROWS):
                        r = 64 * par + DATA_ROWS + part
                        q0 = 32 * par + 16 * part
                        sp.dma_start(QS[r:r + 1, b % 2, :, :], mT[q0:q0 + 16, b % 2, :]).then_inc(maxrows_in[b], 16)

            w1_rows = t["w1"].rearrange("e (k p) f -> e p k f", p=P)
            w2_rows = t["w2"].rearrange("e (k p) d -> e p k d", p=P)
            sp.wait_ge(ones_ready, 1)
            parts(0)
            stacks(0)
            stacks(1)
            parts(1)
            sp.wait_ge(parts_out[1], 4 * 16)
            for e in range(2):
                sp.dma_start(w2[:, e], w2_rows[e]).then_inc(w2a_in, 16)
            max_rows(0)
            sp.wait_ge(v_ready, 1)
            sp.wait_ge(wa_ready, 6)
            sp.wait_ge(consts_ready, 5)
            for e in range(E):
                sp.dma_start(w1[:, e], w1_rows[e]).then_inc(w1_in, 16)
            stacks(2)
            max_rows(1)
            stacks(3)
            max_rows(2)
            for b in range(2, B):
                sp.wait_ge(x1_ready, b - 1)
                sp.dma_start(x_sb[:, b % 2], x_tok[b]).then_inc(x_in1[b % 2], 16)
            max_rows(3)
            sp.wait_ge(x1_ready, B)
            for e in range(2, E):
                sp.dma_start(w2[:, e], w2_rows[e]).then_inc(w2b_in, 16)
            sp.wait_ge(tab_ready, 3)
            sp.wait_ge(zero_ready, 1)
            for e in range(E):
                row = sp.value_load(tab[0:1, 2 * TILES + e:2 * TILES + e + 1], min_val=0, max_val=E * SLOT_ROWS - P)
                sp.dma_start(xd[bass.ds(row, P), :], zero[:, :]).then_inc(padded, 16)
            sp.wait_ge(x2_ready, B)
            for e in range(E):
                sp.dma_start(b2s[:, e, :], t["b2"][e, :].partition_broadcast(P)).then_inc(b2_in, 16)
            sp.wait_ge(scattered, 16 * 4 * B)
            sp.wait_ge(padded, 16 * E)

            def tile_row(n):
                return sp.value_load(tab[0:1, bass.ds(n + TILES, 1)], min_val=0, max_val=E * SLOT_ROWS - P)

            def load_tile(n, par):
                wait(sp, x_turned, n - 1)
                sp.dma_start(xg[:, par, :], xd[bass.ds(tile_row(n), P), :]).then_inc(xg_in[par], 16)

            def store_tile(n, par):
                sp.wait_ge(y_out, n + 1)
                sp.dma_start(yd[bass.ds(n * P, P), :], ys[:, par, :]).then_inc(y_stored[par], 16)

            def step(n, par):
                load_tile(n + 2, par)
                store_tile(n - 1, 1 - par)

            load_tile(0, 0)
            load_tile(1, 1)
            load_tile(2, 0)
            step(1, 1)
            step(2, 0)
            with sp.Fori(1, 9) as i:
                step(2 * i + 1, 1)
                step(2 * i + 2, 0)
            step(19, 1)
            step(20, 0)
            store_tile(20, 0)
            store_tile(21, 1)
            store_tile(22, 0)
            out_rows = out.rearrange("(t p) d -> p t d", p=P)
            for half in range(2):
                sp.wait_ge(out_ready, half + 1)
                sp.dma_start(out_rows[:, 4 * half:4 * half + 4, :], outs[:, 4 * half:4 * half + 4, :]).then_inc(stored, 16)
            sp.wait_ge(stored, 32)

        @block.gpsimd
        def _(pool):
            nc.gpsimd.memset(KS[:, :, :, :], 1.0).then_inc(ones_ready, 1)
            nc.gpsimd.memset(VW[:, :, :], 0.0).then_inc(ones_ready, 1)
            blocks = [VW[:, par, 0:64 * 2 * HKV].rearrange("p (n c) -> p n c", c=64) for par in range(2)]
            pool.wait_ge(ones_ready, 2)
            for par in range(2):
                nc.gpsimd.memset(blocks[par][:, :, 56:64], 1.0).then_inc(vw_ready, 1)
            nc.gpsimd.memset(mhalf[:, :], -0.5).then_inc(pool_step, 1)
            pool.wait_ge(ld_const, 16 * 6)
            nc.gpsimd.tensor_copy(ident_b[:, :], ident[:, :]).then_inc(consts_ready, 1)
            nc.gpsimd.tensor_copy(maskS[:, :], cmask[:, 0, :]).then_inc(consts_ready, 1)
            nc.gpsimd.tensor_copy(maskT[:, :], cmask[:, 1, :]).then_inc(consts_ready, 1)
            nc.gpsimd.tensor_copy(before[:, :], umat[:, :]).then_inc(consts_ready, 1)
            nc.gpsimd.tensor_copy(delta[:, :, :], bc(delta8[:, :], 2, S)).then_inc(consts_ready, 1)
            nc.gpsimd.memset(ones_b[:, :], 1.0).then_inc(consts_ready, 1)
            nc.gpsimd.memset(run[:, :], 0.0).then_inc(consts_ready, 1)
            nc.gpsimd.memset(zero[:, :], 0.0).then_inc(zero_ready, 1)
            steps = [1]

            def inverse_root(k, n):
                pool.wait_ge(var_ready, k + 1)
                nc.gpsimd.tensor_scalar(vare[:, 0:n], mv[:, 0:n, 1], EPS, None, ALU.add).then_inc(pool_step, 1)
                steps[0] += 1
                pool.wait_ge(pool_step, steps[0])
                nc.gpsimd.tensor_tensor(rstd[:, 0:n], vare[:, 0:n], mhalf[:, 0:n], ALU.pow).then_inc(rstd_ready, 1)

            def windows(b):
                if b >= 2:
                    pool.wait_ge(pv_done, HKV * (b - 1))
                nc.gpsimd.tensor_copy(blocks[b % 2][:, :, 24:32],
                                      V[:, 2 * b:2 * b + 2].rearrange("p t g d -> p (t g) d")).then_inc(vw_ready, 1)

            pool.wait_ge(v_done, 1)
            windows(0)
            inverse_root(0, 2)
            windows(1)
            for b in range(B):
                if b + 2 < B:
                    windows(b + 2)
                inverse_root(2 * b + 1, 2)
                if b + 1 < B:
                    inverse_root(2 * b + 2, 2)
                pool.wait_ge(slots_ready, b + 1)
                for i in range(2):
                    for k in range(2):
                        nc.gpsimd.indirect_dma_start(
                            out=xd, out_offset=bass.IndirectOffsetOnAxis(ap=slot[:, 2 * b + i, k:k + 1], axis=0),
                            in_=x2[:, 2 * b + i, :], in_offset=None).then_inc(scattered, 16)

            def bias_tile(n, par):
                wait(pool, g_ready, n - 1)
                e = pool.value_load(tab[0:1, bass.ds(n, 1)], min_val=0, max_val=E - 1)
                nc.gpsimd.tensor_copy(b1t[:, par, :], b1s[:, bass.ds(e, 1), :].rearrange("p o k -> p (o k)")
                                      ).then_inc(b1_ready, 1)

            pool.wait_ge(tab_ready, 3)
            pool.wait_ge(rt_in, 64)
            for n in range(3):
                bias_tile(n, n % 2)
            tiles_of(pool, bias_tile)
            bias_tile(21, 1)
            bias_tile(22, 0)
            pool.wait_ge(y_stored[0], 8 * (TILES + 1))
            pool.wait_ge(y_stored[1], 8 * (TILES - 1))
            pool.wait_ge(y_full, TILES)
            pool.wait_ge(yslots_ready, 1)
            for i in range(T):
                for k in range(2):
                    nc.gpsimd.indirect_dma_start(
                        out=yg[:, i, k, :], out_offset=None, in_=yd,
                        in_offset=bass.IndirectOffsetOnAxis(ap=yslot[:, i, k:k + 1], axis=0)).then_inc(gathered[i // 4], 16)
            inverse_root(2 * B, 4)
            inverse_root(2 * B + 1, 4)

        @block.scalar
        def _(act):
            act.dma_start(ident[:, :], t["ident"]).then_inc(ld_const, 16)
            act.dma_start(cmask[:, :, :], t["cmask"]).then_inc(ld_const, 16)
            act.dma_start(ropeq[:, :, :], t["ropeq"]).then_inc(ld_const, 16)
            act.dma_start(ropek[:, :, :], t["ropek"]).then_inc(ld_const, 16)
            act.dma_start(delta8[:, :], t["delta"]).then_inc(ld_const, 16)
            act.dma_start(umat[:, :], t["umat"]).then_inc(ld_const, 16)

            for c in range(2):
                for u, dst in ((2 * c, qp[:, c]), (2 * c + 1, kp[:, c])):
                    rows = P if u % 2 == 0 else 32
                    src = rot[0:rows]
                    act.wait_ge(rot_done, u + 1)
                    nc.scalar.activation(dst[:, 0], src, ACT.Copy).then_inc(part_a, 1)
                    act.wait_ge(rem_a, 2 * u + 1)
                    nc.scalar.activation(dst[:, 1], src, ACT.Copy).then_inc(part_a, 1)
            act.wait_ge(ones_ready, 1)
            act.wait_ge(v_ready, 1)
            nc.scalar.activation(V[:, :, :, :], ps[:, SB[0], :].rearrange("p (t g d) -> p t g d", t=T, g=HKV),
                                 ACT.Copy).then_inc(v_done, 1)

            def exps(b, g):
                for u in range(SLOTS):
                    k = (b * HKV + g) * SLOTS + u
                    act.wait_ge(t_full, k + 1)
                    if b * HKV + g >= 2:
                        act.wait_ge(pv_done, b * HKV + g - 1)
                    nc.scalar.activation(PT[:, g % 2, u, :], ps[:, SB[k % 2], :], ACT.Exp,
                                         scale=SCALE).then_inc(t_free, 1)

            def copy_maxima(b):
                act.wait_ge(mt_full, b + 1)
                nc.scalar.activation(mT[:, b % 2, :], ps[0:64, OB, 0:S // 2].bitcast(BF16), ACT.Copy).then_inc(mt_free, 1)

            def misc_copy(dst, src, *name):
                act.wait_ge(misc_full, turned(*name) + 1)
                nc.scalar.activation(dst, src, ACT.Copy).then_inc(misc_free, 1)

            misc = ps[:, MB, :].rearrange("p (a d) -> p a d", a=2)

            def slope(gl, q):
                n = gl * 8 + q
                act.wait_ge(e_full, n + 1)
                if n >= 2:
                    act.wait_ge(p_ready, n - 1)
                nc.scalar.activation(es[:, q % 2].rearrange("p a j -> p (a j)"), ps[:, EB[q % 2], :], ACT.Copy,
                                     scale=0.2).then_inc(e_fifth, 1)

            def gexp(gl, q):
                n = gl * 8 + q
                it, hp = q // 4, q % 4
                act.wait_ge(masked, n + 1)
                if n >= 2:
                    m = n - 2
                    act.wait_ge(pt_full, (m // 8) * PTU + 2 + m % 8 + 1)
                for i in range(2):
                    ins = nc.scalar.activation(Pm[:, q % 2, i, :], es[:, q % 2, i, :], ACT.Exp,
                                               bias=nmx[:, q % 2, i:i + 1],
                                               accum_out=psums[:, it, 2 * hp + i:2 * hp + i + 1])
                ins.then_inc(p_ready, 1)

            def gat(b, L):
                gl = 2 * b + L
                misc_copy(feat[:, :, :], misc, "feat", b, L)
                for q in range(9):
                    if q < 8:
                        slope(gl, q)
                    if q == 7:
                        elu_exp(gl, 0)
                    if q >= 1:
                        gexp(gl, q - 1)
                    if L == 1 and b + 1 < B and q < HKV:
                        exps(b + 1, q)
                if L == 0 and b + 1 < B:
                    copy_maxima(b + 1)
                elu_exp(gl, 1)
                if L == 0:
                    misc_copy(h1T[:, :, :], misc, "h1", b)

            def elu_exp(gl, it):
                act.wait_ge(zneg, 2 * gl + it + 1)
                nc.scalar.activation(ze[:, :], zm[:, :], ACT.Exp).then_inc(zexp, 1)

            copy_maxima(0)
            for g in range(HKV):
                exps(0, g)
            for b in range(B):
                gat(b, 0)
                gat(b, 1)
                misc_copy(x2T[:, :, :], misc, "x2", b)
                act.wait_ge(lexp_in, b + 1)
                nc.scalar.activation(prob[:, :, :], lg[:, :, :], ACT.Exp).then_inc(lexp, 1)

            def gelu_tile(n, par):
                wait(act, ht_full, 2 * n - 2)
                act.wait_ge(h_full, 2 * n + 1)
                nc.scalar.activation(hs[:, par, 0:512], ps[:, 2, :], ACT.Copy).then_inc(hs_a, 1)
                wait(act, y_full, n - 1)
                act.wait_ge(b1_ready, n + 1)
                for k in range(8):
                    if k % 4 == 0:
                        act.wait_ge(ht_full, 2 * n + 1 + k // 4)
                    ins = nc.scalar.activation(gT[:, par, k, :], ps[:, 4 + k // 4, 128 * (k % 4):128 * (k % 4) + 128],
                                               ACT.Gelu_apprx_tanh, bias=b1t[:, par, k:k + 1])
                ins.then_inc(g_ready, 1)

            for n in range(3):
                gelu_tile(n, n % 2)
            tiles_of(act, gelu_tile)
            gelu_tile(21, 1)
            gelu_tile(22, 0)

        @block.vector
        def _(dve):
            chain = [0]

            def link(ins):
                chain[0] += 1
                ins.then_inc(dve_step, 1)
                dve.wait_ge(dve_step, chain[0])

            dve.wait_ge(ld_const, 16 * 6)
            for c in range(2):
                dve.wait_ge(proj_ready, c + 1)
                for kind in range(2):
                    u = 2 * c + kind
                    rows = P if kind == 0 else 32
                    bank = 4 * c + 2 * kind
                    table = ropeq if kind == 0 else ropek
                    dst = qp[:, c] if kind == 0 else kp[:, c]
                    src = ps[0:rows, bank:bank + 2, :].rearrange("p e (b n) -> p (e b) n", b=2)
                    cos, sin = (bc(table[0:rows, i, :], 1, 4) for i in range(2))
                    link(nc.vector.tensor_tensor(rc[0:rows].rearrange("p e (b n) -> p (e b) n", b=2), src, cos, ALU.mult))
                    link(nc.vector.tensor_tensor(rs[0:rows].rearrange("p e (b n) -> p (e b) n", b=2), src, sin, ALU.mult))
                    if u >= 1:
                        dve.wait_ge(part_a, 2 * u)
                    nc.vector.tensor_tensor(rot[0:rows, 0, :], rc[0:rows, 0, :], rs[0:rows, 1, :], ALU.subtract)
                    nc.vector.tensor_tensor(rot[0:rows, 1, :], rs[0:rows, 0, :], rc[0:rows, 1, :], ALU.add
                                            ).then_inc(rot_done, 1)
                    dve.wait_ge(part_a, 2 * u + 1)
                    nc.vector.tensor_tensor(rot[0:rows], rot[0:rows], dst[:, 0], ALU.subtract).then_inc(rem_a, 1)
                    dve.wait_ge(part_a, 2 * u + 2)
                    nc.vector.tensor_tensor(dst[:, 2], rot[0:rows], dst[:, 1], ALU.subtract).then_inc(rem_a, 1)

            dve.wait_ge(ld_gat, 16 * 9)
            for L in range(2):
                for k in range(1 if L == 0 else 2):
                    rows = FIN if L == 0 else P
                    w = w0[:, :] if L == 0 else w1g[:, k, :]
                    for i in range(2):
                        o = wa0[:, 8 * i:8 * i + 8] if L == 0 else wa1[:, k, 8 * i:8 * i + 8]
                        nth = 2 * (L + k) + i
                        if nth:
                            dve.wait_ge(wa_ready, nth)
                        link(nc.vector.tensor_tensor(watmp[0:rows, :], w, avec[0:rows, 2 * L + i, :], ALU.mult))
                        nc.vector.tensor_reduce(o, watmp[0:rows, :].rearrange("p (h o) -> p h o", h=GH), AX.X, ALU.add
                                                ).then_inc(wa_ready, 1)

            def maxima(b, g):
                par, gg = g % 2, g // 2
                for u in range(SLOTS):
                    k = (b * HKV + g) * SLOTS + u
                    dve.wait_ge(s_full, k + 1)
                    if u == 0:
                        o, w = mneg[:, 0, par, 4 * gg:4 * gg + 4], 4
                    else:
                        o, w = mneg[:, 1, par, 4 * gg + 2 * u - 2:4 * gg + 2 * u], 2
                    nc.vector.tensor_reduce(o, ps[:, SB[k % 2], :].rearrange("p (h j) -> p h j", h=w), AX.X,
                                            ALU.max, negate=True).then_inc(s_free, 1)

            def maxima_parts(b):
                dve.wait_ge(s_free, (b + 1) * HKV * SLOTS)
                if b >= 1:
                    dve.wait_ge(mt_full, b)
                link(nc.vector.tensor_copy(mb[:, :, :, 0, :], mneg[:, :, :, :]))
                nc.vector.tensor_tensor(mb[:, :, :, 1, :], mneg[:, :, :, :], mb[:, :, :, 0, :], ALU.subtract
                                        ).then_inc(mparts, 1)

            def normalise(b, g):
                dve.wait_ge(pv_done, HKV * b + g + 1)
                lo = 64 * (g % 2)
                link(nc.vector.reciprocal(orv[:, g % 2, :], ps[lo + 32:lo + 64, OB, 0:S]))
                nc.vector.tensor_tensor(attnT[32 * (g % 4):32 * (g % 4) + 32, g // 4, :], ps[lo:lo + 32, OB, 0:S],
                                        orv[:, g % 2, :], ALU.mult).then_inc(o_free, 1)

            def layer_norm(k, dst, src=None, n=2):
                src = res if src is None else src
                for i in range(n):
                    nc.vector.bn_stats(stats[:, i, :], src[:, i, :]).then_inc(dve_step, 1)
                    chain[0] += 1
                dve.wait_ge(dve_step, chain[0])
                if k >= 1:
                    dve.wait_ge(rstd_ready, k)
                for i in range(n):
                    ins = nc.vector.bn_aggr(mv[:, i, :], stats[:, i, :])
                ins.then_inc(var_ready, 1)
                dve.wait_ge(rstd_ready, k + 1)
                for i in range(n):
                    ins = nc.vector.tensor_scalar(dst[:, i, :], src[:, i, :], mv[:, i, 0:1], rstd[:, i:i + 1],
                                                  ALU.subtract, ALU.mult)
                return ins

            def attn_out(b):
                dve.wait_ge(wo_ready, b + 1)
                dve.wait_ge(x_in1[b % 2], 16 * (b // 2) + 16)
                link(nc.vector.tensor_tensor(res[:, :, :], ps[:, OB, :].rearrange("p (a d) -> p a d", a=2),
                                             x_sb[:, b % 2], ALU.add))
                layer_norm(2 * b, x1).then_inc(x1_ready, 1)
                dve.wait_ge(x1_ready, b + 1)
                link(nc.vector.tensor_scalar(Mt[:, :, :], x1[:, :, :], -1.0, 1.0, ALU.mult, ALU.add))
                link(nc.vector.tensor_scalar(Mt[:, :, :], Mt[:, :, :], MASK_VAL, None, ALU.mult))

            def gat(b, L):
                gl = 2 * b + L
                dve.wait_ge(pt_full, gl * PTU + 1)
                sn = ps[:, PB[0], 0:32].rearrange("p (t s h) -> p t s h", t=2, s=2)
                if gl >= 1:
                    dve.wait_ge(pt_full, (gl - 1) * PTU + 2)
                link(nc.vector.tensor_copy(snp[:, :, :, 0, :], sn))
                nc.vector.tensor_tensor(snr[:, :, :, :], sn, snp[:, :, :, 0, :], ALU.subtract).then_inc(pt_free, 1)
                dve.wait_ge(pt_free, gl * PTU + 1)
                link(nc.vector.tensor_copy(snp[:, :, :, 1, :], snr[:, :, :, :]))
                nc.vector.tensor_tensor(snp[:, :, :, 2, :], snr[:, :, :, :], snp[:, :, :, 1, :], ALU.subtract
                                        ).then_inc(snp_ready, 1)
                dve.wait_ge(pt_full, gl * PTU + 2)
                if gl >= 1:
                    dve.wait_ge(e_full, gl * 8)
                nc.vector.tensor_copy(snT[:, :, :], ps[0:24, PB[1], 0:S].bitcast(BF16).rearrange("p (s n) -> p s n", s=2)
                                      ).then_inc(pt_free, 1)

                def mask_max(q):
                    n = gl * 8 + q
                    it = q // 4
                    dve.wait_ge(e_fifth, n + 1)
                    ee = es[:, q % 2].rearrange("p a j -> p (a j)")
                    nc.vector.tensor_tensor(ee, ps[:, EB[q % 2], :], ee, ALU.max).then_inc(e_free, 1)
                    dve.wait_ge(e_free, n + 1)
                    if n >= 2:
                        dve.wait_ge(p_ready, n - 1)
                    for i in range(2):
                        ins = nc.vector.tensor_tensor_reduce(
                            out=es[:, q % 2, i, :], in0=es[:, q % 2, i, :], in1=Mt[:, it, :], scale=1.0,
                            scalar=-3.0e38, op0=ALU.add, op1=ALU.max, accum_out=mx[:, q % 2, i:i + 1])
                    link(ins)
                    nc.vector.tensor_scalar(nmx[:, q % 2, :], mx[:, q % 2, :], -1.0, None, ALU.mult).then_inc(masked, 1)

                def pt_copy(q):
                    n = gl * 8 + q
                    dve.wait_ge(pt_full, gl * PTU + 2 + q + 1)
                    if n >= 2:
                        dve.wait_ge(agg_done, n - 1)
                    nc.vector.tensor_copy(PTg[:, q % 2].rearrange("p h j i -> p (h j i)"), ps[:, PB[q % 2], :]).then_inc(pt_free, 1)

                def elu_in(it):
                    dve.wait_ge(agg_done, 8 * gl + 4 * it + 4)
                    link(nc.vector.reciprocal(grv[:, :], psums[:, it, :]))
                    nc.vector.tensor_tensor(z[:, it, :].rearrange("p (h o) -> p h o", h=GH),
                                            ps[:, MB, 0:D].rearrange("p (h o) -> p h o", h=GH),
                                            bc(grv[:, :], 2, GO), ALU.mult).then_inc(misc_free, 1)
                    dve.wait_ge(misc_free, use("agg", b, L, it) + 1)
                    link(nc.vector.tensor_tensor(z[:, it, :], z[:, it, :], bvec[:, L, :], ALU.add))
                    nc.vector.tensor_scalar(zm[:, :], z[:, it, :], 0.0, None, ALU.min).then_inc(zneg, 1)

                def elu_out(it):
                    dve.wait_ge(zexp, 2 * gl + it + 1)
                    nc.vector.scalar_tensor_tensor(out=z[:, it, :], in0=ze[:, :], scalar=-1.0, in1=z[:, it, :],
                                                   op0=ALU.add, op1=ALU.max).then_inc(h_ready, 1)

                for q in range(10):
                    if q == 7:
                        elu_in(0)
                    if q < 8:
                        mask_max(q)
                    if q == 7:
                        elu_out(0)
                    if q >= 2:
                        pt_copy(q - 2)
                    if b + 1 < B and L == 0:
                        if q < HKV:
                            maxima(b + 1, q)
                        elif q == HKV:
                            maxima_parts(b + 1)
                    if b + 1 < B and L == 1 and q >= 2:
                        normalise(b + 1, q - 2)
                elu_in(1)
                elu_out(1)
                if L == 1:
                    dve.wait_ge(h_ready, 4 * b + 4)
                    link(nc.vector.tensor_tensor(res[:, :, :], z[:, :, :], x1[:, :, :], ALU.add))
                    layer_norm(2 * b + 1, x2[:, 2 * b:2 * b + 2, :]).then_inc(x2_ready, 1)
                    dve.wait_ge(x2_ready, b + 1)

            def route(b):
                dve.wait_ge(logit_ready, b + 1)
                nc.vector.tensor_tensor(lg[:, :, :], ps[:, MB, 0:2 * E].rearrange("p (t e) -> p t e", t=2),
                                        bc(gb[:, :], 1, 2), ALU.add).then_inc(misc_free, 1)
                dve.wait_ge(misc_free, use("logits", b) + 1)
                link(nc.vector.tensor_reduce(lmax[:, :], lg[:, :, :], AX.X, ALU.max))
                link(nc.vector.tensor_tensor(lg[:, :, :], lg[:, :, :], bc(lmax[:, :], 2, E), ALU.subtract))
                nc.vector.tensor_copy(lmax[:, :], lmax[:, :]).then_inc(lexp_in, 1)
                dve.wait_ge(lexp, b + 1)
                link(nc.vector.tensor_reduce(lsum[:, :], prob[:, :, :], AX.X, ALU.add))
                link(nc.vector.reciprocal(lsum[:, :], lsum[:, :]))
                link(nc.vector.tensor_tensor(prob[:, :, :], prob[:, :, :], bc(lsum[:, :], 2, E), ALU.mult))
                for i in range(2):
                    link(nc.vector.max(top[:, i, :], prob[:, i, :]))
                    link(nc.vector.max_index(topi[:, i, :], top[:, i, :], prob[:, i, :]))
                link(nc.vector.tensor_copy(topf[:, :, :], topi[:, :, 0:2]))
                link(nc.vector.tensor_tensor(wsum[:, :], top[:, :, 0], top[:, :, 1], ALU.add))
                link(nc.vector.reciprocal(wsum[:, :], wsum[:, :]))
                link(nc.vector.tensor_tensor(wk2[:, 2 * b:2 * b + 2, :], top[:, :, 0:2], bc(wsum[:, :], 2, 2), ALU.mult))
                for i in range(2):
                    link(nc.vector.tensor_tensor(oh[:, 2 * b + i], bc(iota_e, 1, 2), bc(topf[:, i, :], 2, E), ALU.is_equal))
                nc.vector.tensor_tensor(chosen[:, :, :], oh[:, 2 * b:2 * b + 2, 0, :], oh[:, 2 * b:2 * b + 2, 1, :], ALU.add).then_inc(chosen_ready, 1)
                dve.wait_ge(rank_ready, b + 1)
                link(nc.vector.tensor_tensor(pos[:, :, :], ps[:, MB, 0:2 * E].rearrange("p (t e) -> p t e", t=2),
                                             bc(run[:, :], 1, 2), ALU.add))
                nc.vector.tensor_tensor(run[:, :], run[:, :], ps[:, MB, 2 * E:3 * E], ALU.add).then_inc(misc_free, 1)
                link(nc.vector.tensor_tensor(pos[:, :, :], pos[:, :, :], bc(stride_e, 1, 2), ALU.add))
                for i in range(2):
                    link(nc.vector.tensor_tensor(ohp[:, i], oh[:, 2 * b + i], bc(pos[:, i, :], 1, 2), ALU.mult))
                link(nc.vector.tensor_reduce(slotf[:, 2 * b:2 * b + 2, :], ohp[:, :, :, :], AX.X, ALU.add))
                nc.vector.tensor_copy(slot[:, 2 * b:2 * b + 2, :], slotf[:, 2 * b:2 * b + 2, :]).then_inc(slots_ready, 1)
                dve.wait_ge(slots_ready, b + 1)
                dve.wait_ge(misc_free, use("ranks", b) + 1)

            def tables():
                link(nc.vector.tensor_tensor(big[:, 0:E, :], bc(run[:, :], 2, E), bc(tile_j, 1, E), ALU.is_gt))
                link(nc.vector.tensor_reduce(tiles_e[:, :], big[:, 0:E, :], AX.X, ALU.add))
                link(nc.vector.tensor_tensor(big[:, 0:E, :], lower, bc(tiles_e[:, :], 1, E), ALU.mult))
                link(nc.vector.tensor_reduce(base_e[:, :], big[:, 0:E, :], AX.X, ALU.add))
                link(nc.vector.tensor_tensor(end_e[:, :], base_e[:, :], tiles_e[:, :], ALU.add))
                link(nc.vector.tensor_scalar(last[:, :], end_e[:, E - 1:E], -1.0, None, ALU.add))
                link(nc.vector.tensor_scalar(tcl[:, :], tau, last[:, 0:1], None, ALU.min))
                link(nc.vector.tensor_tensor(big[:, :, :], bc(tcl[:, :], 2, E), bc(end_e[:, :], 1, TILES), ALU.is_ge))
                link(nc.vector.tensor_reduce(te[:, :], big[:, :, :], AX.X, ALU.add))
                link(nc.vector.tensor_tensor(big2[:, :, :], big[:, :, :], bc(tiles_e[:, :], 1, TILES), ALU.mult))
                link(nc.vector.tensor_reduce(tb[:, :], big2[:, :, :], AX.X, ALU.add))
                link(nc.vector.tensor_tensor(trow[:, :], tcl[:, :], tb[:, :], ALU.subtract))
                link(nc.vector.tensor_scalar(trow[:, :], trow[:, :], float(P), None, ALU.mult))
                link(nc.vector.tensor_scalar(tcl[:, :], te[:, :], float(SLOT_ROWS), None, ALU.mult))
                link(nc.vector.tensor_tensor(trow[:, :], trow[:, :], tcl[:, :], ALU.add))
                link(nc.vector.tensor_tensor(padf[:, :], run[:, :], stride_e, ALU.add))
                nc.vector.tensor_copy(tab[:, 0:TILES], te[:, :]).then_inc(tab_ready, 1)
                nc.vector.tensor_copy(tab[:, TILES:2 * TILES], trow[:, :]).then_inc(tab_ready, 1)
                nc.vector.tensor_copy(tab[:, 2 * TILES:2 * TILES + E], padf[:, :]).then_inc(tab_ready, 1)
                dve.wait_ge(tab_ready, 3)
                link(nc.vector.tensor_scalar(shift[:, :], base_e[:, :], float(P), None, ALU.mult))
                link(nc.vector.tensor_tensor(shift[:, :], shift[:, :], stride_e, ALU.subtract))
                link(nc.vector.tensor_tensor(oht[:, :, :], oh[:, :, :, :].rearrange("p t k e -> p (t k) e"),
                                             bc(shift[:, :], 1, 2 * T), ALU.mult))
                link(nc.vector.tensor_reduce(tsh[:, :], oht[:, :, :], AX.X, ALU.add))
                link(nc.vector.tensor_tensor(tsh[:, :], tsh[:, :], slotf[:, :, :].rearrange("p t k -> p (t k)"), ALU.add))
                nc.vector.tensor_copy(yslot[:, :, :], tsh[:, :].rearrange("p (t k) -> p t k", k=2)).then_inc(yslots_ready, 1)

            dve.wait_ge(rt_in, 64)
            for g in range(HKV):
                maxima(0, g)
            maxima_parts(0)
            for g in range(HKV):
                normalise(0, g)
            attn_out(0)
            for b in range(B):
                gat(b, 0)
                gat(b, 1)
                if b + 1 < B:
                    attn_out(b + 1)
                route(b)
            tables()

            def x_copy(n, par):
                wait(dve, h_full, 2 * n - 2)
                dve.wait_ge(x_turned, n + 1)
                nc.vector.tensor_copy(xgT[:, par].rearrange("p k n -> p (k n)"), ps[:, par, 0:D]).then_inc(xgT_ready, 1)

            def h_copy(n, par):
                wait(dve, ht_full, 2 * n - 2)
                dve.wait_ge(h_full, 2 * n + 2)
                nc.vector.tensor_copy(hs[:, par, 512:F], ps[:, 3, :]).then_inc(hs_d, 1)

            def y_add(n, par):
                wait(dve, y_stored[par], 8 * (n - par))
                dve.wait_ge(y_full, n + 1)
                e = dve.value_load(tab[0:1, bass.ds(n, 1)], min_val=0, max_val=E - 1)
                nc.vector.tensor_tensor(ys[:, par, :], ps[:, 6 + par, 0:D],
                                        b2s[:, bass.ds(e, 1), :].rearrange("p o d -> p (o d)"), ALU.add).then_inc(y_out, 1)

            def step(n, par):
                x_copy(n + 1, 1 - par)
                h_copy(n, par)
                y_add(n - 1, 1 - par)

            dve.wait_ge(b2_in, 16 * E)
            x_copy(0, 0)
            x_copy(1, 1)
            h_copy(0, 0)
            step(1, 1)
            step(2, 0)
            tiles_of(dve, step)
            step(21, 1)
            h_copy(22, 0)
            y_add(21, 1)
            y_add(22, 0)

            for half in range(2):
                dve.wait_ge(gathered[half], 16 * 8)
                for k in range(2):
                    for i in range(4 * half, 4 * half + 4):
                        ins = nc.vector.scalar_tensor_tensor(out=x2[:, i, :], in0=yg[:, i, k, :], scalar=wk2[:, i, k:k + 1],
                                                             in1=x2[:, i, :], op0=ALU.mult, op1=ALU.add)
                    link(ins)
                h4 = slice(4 * half, 4 * half + 4)
                layer_norm(2 * B + half, outs[:, h4, :], x2[:, h4, :], 4).then_inc(out_ready, 1)

        @block.tensor
        def _(pe):
            pe.wait_ge(ld_x, 64)
            for c in range(2):
                for e in range(2):
                    for k in range(2):
                        nc.tensor.matmul(ps[:, 4 * c + e, :], wq[:, k, 128 * e:128 * e + 128],
                                         xT[:, k, 512 * c:512 * c + 512], start=(k == 0), stop=(k == 1))
                for e in range(2):
                    for k in range(2):
                        ins = nc.tensor.matmul(ps[0:32, 4 * c + 2 + e, :], wk[:, k, 32 * e:32 * e + 32],
                                               xT[:, k, 512 * c:512 * c + 512], start=(k == 0), stop=(k == 1))
                ins.then_inc(proj_ready, 1)
            pe.wait_ge(rot_done, 1)
            for tt in range(T):
                for k in range(2):
                    ins = nc.tensor.matmul(ps[:, SB[0], 64 * tt:64 * tt + 64], xT[:, k, 128 * tt:128 * tt + 128],
                                           wv[:, k, :], start=(k == 0), stop=(k == 1))
            ins.then_inc(v_ready, 1)
            pe.wait_ge(consts_ready, 7)
            pe.wait_ge(v_done, 1)
            pe.wait_ge(rot_done, 4)

            def scores(b, g, units=range(SLOTS)):
                par, gg = g % 2, g // 2
                lo = 64 * par
                if g == 0 and 0 in units:
                    pe.wait_ge(stacks_in[b], 16 * 24)
                    wait(pe, t_free, b * HKV * SLOTS)
                for u in units:
                    k = (b * HKV + g) * SLOTS + u
                    if k >= 2:
                        pe.wait_ge(s_free, k - 1)
                    bank = ps[:, SB[k % 2], :]
                    if u == 0:
                        nc.tensor.matmul(bank.rearrange("p (h j) -> p h j", h=4), maskS[:, :], bc(ident_b[:, :], 1, 4),
                                         start=True, stop=False, skip_group_check=True)
                        for i in range(4):
                            ins = nc.tensor.matmul(bank[:, 128 * i:128 * i + 128],
                                                   QS[lo:lo + DATA_ROWS, b % 2, 4 * gg + i, 0:128],
                                                   KS[lo:lo + DATA_ROWS, b % 2, gg, 0:128],
                                                   start=False, stop=True, skip_group_check=True)
                    else:
                        nc.tensor.matmul(bank.rearrange("p (h j) -> p h j", h=2)[:, :, 128:256], maskS[:, :],
                                         bc(ident_b[:, :], 1, 2), start=True, stop=False, skip_group_check=True)
                        for i in range(2):
                            ins = nc.tensor.matmul(bank[:, 256 * i:256 * i + 256],
                                                   QS[lo:lo + DATA_ROWS, b % 2, 4 * gg + 2 * u - 2 + i, 128:256],
                                                   KS[lo:lo + DATA_ROWS, b % 2, gg, 0:256],
                                                   start=False, stop=True, skip_group_check=True)
                    ins.then_inc(s_full, 1)

            def turn_maxima(b):
                pe.wait_ge(mparts, b + 1)
                wait(pe, x1_ready, b)
                dst = ps[0:64, OB, 0:S // 2].bitcast(BF16)
                for qt in range(2):
                    ins = nc.tensor.transpose(dst[:, 128 * qt:128 * qt + 128],
                                              mb[:, qt].rearrange("p a b h -> p (a b h)"), ident_b[:, :])
                ins.then_inc(mt_full, 1)

            def scores_t(b, g, units=range(SLOTS)):
                KR = DATA_ROWS + MAX_ROWS
                par, gg = g % 2, g // 2
                lo = 64 * par
                if g == 0 and 0 in units:
                    pe.wait_ge(maxrows_in[b], 16 * 4)
                    pe.wait_ge(s_free, (b + 1) * HKV * SLOTS)
                for u in units:
                    k = (b * HKV + g) * SLOTS + u
                    if k >= 2:
                        pe.wait_ge(t_free, k - 1)
                    bank = ps[:, SB[k % 2], :]
                    if u < 2:
                        nc.tensor.matmul(bank.rearrange("p (h j) -> p h j", h=2)[:, :, 0:128], maskT[:, :],
                                         bc(ident_b[:, :], 1, 2), start=True, stop=False, skip_group_check=True)
                        ins = nc.tensor.matmul(bank.rearrange("p (h j) -> p h j", h=2),
                                               KS[lo:lo + KR, b % 2, gg, 0:128],
                                               QS[lo:lo + KR, b % 2, 4 * gg + 2 * u:4 * gg + 2 * u + 2, :],
                                               start=False, stop=True, skip_group_check=True)
                    else:
                        nc.tensor.matmul(bank.rearrange("p (h j) -> p h j", h=4), maskT[:, :],
                                         bc(ident_b[:, :], 1, 4), start=True, stop=False, skip_group_check=True)
                        ins = nc.tensor.matmul(bank.rearrange("p (h j) -> p h j", h=4),
                                               KS[lo:lo + KR, b % 2, gg, 128:256],
                                               QS[lo:lo + KR, b % 2, 4 * gg:4 * gg + 4, 128:256],
                                               start=False, stop=True, skip_group_check=True)
                    ins.then_inc(t_full, 1)

            def values(b, g):
                pe.wait_ge(t_free, (b * HKV + g + 1) * SLOTS)
                if g == 0:
                    pe.wait_ge(vw_ready, 2 + b + 1)
                    pe.wait_ge(mt_free, b + 1)
                if g >= 2:
                    pe.wait_ge(o_free, b * HKV + g - 1)
                o = ps[64 * (g % 2):64 * (g % 2) + 64, OB, 0:S]
                for i in range(4):
                    for kt in range(2):
                        at = 64 * (kt * HKV + g) + 24 - 8 * i
                        pt = PT[:, g % 2, i // 2, S * (i % 2):S * (i % 2) + S] if kt == 0 else \
                            PT[:, g % 2, 2, P * i:P * i + P]
                        ins = nc.tensor.matmul(o[:, P * kt:S], VW[:, b % 2, at:at + 64], pt,
                                               start=(i == 0 and kt == 0), stop=(i == 3 and kt == 1),
                                               skip_group_check=True)
                ins.then_inc(pv_done, 1)

            def turn(dst, src_tile):
                for a in range(2):
                    for f in range(2):
                        ins = nc.tensor.transpose(dst[:, a * 256 + 128 * f:a * 256 + 128 * f + 128],
                                                  src_tile[:, f, 128 * a:128 * a + 128], ident[:, :])
                return ins

            def attn_proj(b):
                pe.wait_ge(o_free, HKV * (b + 1))
                pe.wait_ge(ld_w, 16)
                for qt in range(2):
                    for k in range(2):
                        ins = nc.tensor.matmul(ps[:, OB, 256 * qt:256 * qt + 256], attnT[:, k, 128 * qt:128 * qt + 128],
                                               wo[:, k, :], start=(k == 0), stop=(k == 1))
                ins.then_inc(wo_ready, 1)

            def gat(b, L):
                gl = 2 * b + L
                kt = 1 if L == 0 else 2
                src = (lambda k, it: ctxT[:, S * b + 128 * it:S * b + 128 * it + 128]) if L == 0 else \
                      (lambda k, it: h1T[:, k, 128 * it:128 * it + 128])
                w = (lambda k: w0[:, :]) if L == 0 else (lambda k: w1g[:, k, :])
                wa = (lambda k: wa0[:, :]) if L == 0 else (lambda k: wa1[:, k, :])
                wait(pe, misc_free, use("feat", b, L))
                for it in range(2):
                    for k in range(kt):
                        ins = nc.tensor.matmul(ps[:, MB, 256 * it:256 * it + 256], src(k, it), w(k),
                                               start=(k == 0), stop=(k == kt - 1))
                ins.then_inc(misc_full, 1)
                if gl >= 1:
                    pe.wait_ge(pt_free, gl * PTU)
                for it in range(2):
                    for k in range(kt):
                        ins = nc.tensor.matmul(ps[:, PB[0], 16 * it:16 * it + 16], src(k, it), wa(k),
                                               start=(k == 0), stop=(k == kt - 1))
                ins.then_inc(pt_full, 1)
                pe.wait_ge(snp_ready, gl + 1)
                pe.wait_ge(pt_free, gl * PTU + 1)
                dst = ps[0:24, PB[1], 0:S].bitcast(BF16).rearrange("p (s n) -> p s n", s=2)
                for s in range(2):
                    for it in range(2):
                        ins = nc.tensor.transpose(dst[:, s, 128 * it:128 * it + 128],
                                                  snp[:, it, s].rearrange("p a h -> p (a h)"), ident_b[:, :])
                ins.then_inc(pt_full, 1)
                pe.wait_ge(pt_free, gl * PTU + 2)

                def e_mm(q):
                    n = gl * 8 + q
                    it, hp = q // 4, q % 4
                    if n >= 2:
                        pe.wait_ge(e_free, n - 1)
                    nc.tensor.matmul(ps[:, EB[q % 2], :].rearrange("p (h j) -> p h j", h=2), snT[:, 0, 128 * it:128 * it + 128],
                                     delta[:, 2 * hp:2 * hp + 2, :], start=True, stop=False, skip_group_check=True)
                    for i in range(2):
                        ins = nc.tensor.matmul(ps[:, EB[q % 2], 256 * i:256 * i + 256], delta[:, 2 * hp + i, 0:128], snT[:, 1, :],
                                               start=False, stop=True, skip_group_check=True)
                    ins.then_inc(e_full, 1)

                def turn_p(q):
                    pe.wait_ge(p_ready, gl * 8 + q + 1)
                    pe.wait_ge(pt_free, gl * PTU + 1 + q)
                    for i in range(2):
                        for jt in range(2):
                            c0 = 256 * i + 128 * jt
                            ins = nc.tensor.transpose(ps[:, PB[q % 2], c0:c0 + 128], Pm[:, q % 2, i, 128 * jt:128 * jt + 128],
                                                      ident[:, :])
                    ins.then_inc(pt_full, 1)

                def agg(q):
                    it, hp = q // 4, q % 4
                    pe.wait_ge(pt_free, gl * PTU + 2 + q + 1)
                    if hp == 0:
                        pe.wait_ge(misc_free, use("agg", b, L, it))
                    for i in range(2):
                        h = 2 * hp + i
                        for jt in range(2):
                            ins = nc.tensor.matmul(ps[:, MB, GO * h:GO * h + GO], PTg[:, q % 2, i, jt, :],
                                                   feat[:, jt, GO * h:GO * h + GO], start=(jt == 0), stop=(jt == 1))
                    ins.then_inc(agg_done, 1)

                nxt = b + 1
                for q in range(11):
                    if q < 8:
                        e_mm(q)
                    if nxt < B and q < HKV:
                        (scores if L == 0 else scores_t)(nxt, q, range(2))
                    if 2 <= q <= 9:
                        turn_p(q - 2)
                    if nxt < B and L == 1 and 1 <= q <= HKV:
                        values(nxt, q - 1)
                    if nxt < B and q < HKV:
                        (scores if L == 0 else scores_t)(nxt, q, range(2, SLOTS))
                    if q >= 3:
                        agg(q - 3)
                    if nxt < B and L == 0 and q == 9:
                        turn_maxima(nxt)
                if L == 0:
                    pe.wait_ge(h_ready, 4 * b + 2)
                    pe.wait_ge(misc_free, use("h1", b))
                    turn(ps[:, MB, :], z).then_inc(misc_full, 1)

            def router(b):
                pe.wait_ge(x2_ready, b + 1)
                pe.wait_ge(misc_free, use("x2", b))
                turn(ps[:, MB, :], x2[:, 2 * b:2 * b + 2, :]).then_inc(misc_full, 1)
                pe.wait_ge(misc_free, use("logits", b))
                for i in range(2):
                    for k in range(2):
                        ins = nc.tensor.matmul(ps[:, MB, E * i:E * i + E], x2T[:, k, 128 * i:128 * i + 128], gw[:, k, :],
                                               start=(k == 0), stop=(k == 1))
                ins.then_inc(logit_ready, 1)
                pe.wait_ge(chosen_ready, b + 1)
                pe.wait_ge(misc_free, use("ranks", b))
                nc.tensor.matmul(ps[:, MB, 0:E], before[:, :], chosen[:, 0, :], start=True, stop=True)
                nc.tensor.matmul(ps[:, MB, E:2 * E], before[:, :], chosen[:, 1, :], start=True, stop=False)
                nc.tensor.matmul(ps[:, MB, E:2 * E], ones_b[:, :], chosen[:, 0, :], start=False, stop=True)
                nc.tensor.matmul(ps[:, MB, 2 * E:3 * E], ones_b[:, :], chosen[:, 0, :], start=True, stop=False)
                nc.tensor.matmul(ps[:, MB, 2 * E:3 * E], ones_b[:, :], chosen[:, 1, :], start=False, stop=True
                                 ).then_inc(rank_ready, 1)

            pe.wait_ge(rt_in, 64)
            pe.wait_ge(ld_gat, 16 * 9)
            pe.wait_ge(wa_ready, 6)
            for g in range(HKV):
                scores(0, g)
            turn_maxima(0)
            for g in range(HKV + 1):
                if g < HKV:
                    scores_t(0, g)
                if g >= 1:
                    values(0, g - 1)
            attn_proj(0)
            for b in range(B):
                gat(b, 0)
                gat(b, 1)
                if b + 1 < B:
                    attn_proj(b + 1)
                router(b)

            pe.wait_ge(tab_ready, 3)

            def turn_x(n, par):
                wait(pe, xgT_ready, n - 1)
                pe.wait_ge(xg_in[par], 8 * (n - par) + 16)
                for k in range(2):
                    ins = nc.tensor.transpose(ps[:, par, 128 * k:128 * k + 128], xg[:, par, 128 * k:128 * k + 128],
                                              ident[:, :])
                ins.then_inc(x_turned, 1)

            def expert(n):
                return pe.value_load(tab[0:1, bass.ds(n, 1)], min_val=0, max_val=E - 1)

            w1f = w1[:, :, :, :].rearrange("p e k f -> p (e k f)")
            w2flat = w2[:, :, :, :].rearrange("p e k d -> p (e k d)")

            def mm1(n, par):
                e = expert(n)
                pe.wait_ge(xgT_ready, n + 1)
                for half in range(2):
                    wait(pe, hs_d if half else hs_a, n)
                    for k in range(2):
                        ins = nc.tensor.matmul(ps[:, 2 + half, :], xgT[:, par, k, :],
                                               w1f[:, bass.ds(e * (2 * F) + (k * F + 512 * half), 512)],
                                               start=(k == 0), stop=(k == 1))
                    ins.then_inc(h_full, 1)

            def turn_h(n, par):
                for half in range(2):
                    pe.wait_ge(hs_d if half else hs_a, n + 1)
                    wait(pe, g_ready, n)
                    for k in range(4 * half, 4 * half + 4):
                        ins = nc.tensor.transpose(ps[:, 4 + half, 128 * (k % 4):128 * (k % 4) + 128],
                                                  hs[:, par, 128 * k:128 * k + 128], ident[:, :])
                    ins.then_inc(ht_full, 1)

            def mm2(n, par):
                e = expert(n)
                pe.wait_ge(g_ready, n + 1)
                wait(pe, y_out, n - 1)
                for k in range(8):
                    ins = nc.tensor.matmul(ps[:, 6 + par, 0:D], gT[:, par, k, :],
                                           w2flat[:, bass.ds(e * (8 * D) + k * D, D)], start=(k == 0), stop=(k == 7))
                ins.then_inc(y_full, 1)

            def step(n, par):
                turn_x(n + 1, 1 - par)
                mm1(n, par)
                mm2(n - 1, 1 - par)
                turn_h(n, par)

            pe.wait_ge(w1_in, 16 * E)
            pe.wait_ge(w2a_in, 16 * 2)
            pe.wait_ge(w2b_in, 16 * (E - 2))
            turn_x(0, 0)
            turn_x(1, 1)
            mm1(0, 0)
            turn_h(0, 0)
            step(1, 1)
            step(2, 0)
            tiles_of(pe, step)
            step(21, 1)
            mm1(22, 0)
            mm2(21, 1)
            turn_h(22, 0)
            mm2(22, 0)


def kernel(**inputs):
    import numpy as np
    import concourse.bacc as bacc
    from concourse import mybir as mb_
    from concourse.bass_utils import run_bass_kernel_spmd as run

    f32 = np.float32
    i = {k.replace("L0_", ""): np.asarray(v) for k, v in inputs.items()}
    wq = i["attn_Wq"].reshape(D, 4, 2, 4, 4, 2)
    wk = i["attn_Wk"].reshape(D, 4, 2, 4, 2)
    s = np.arange(S, dtype=f32)
    theta = (f32(1.0) / f32(10000.0) ** (f32(2.0) * np.arange(DK // 2, dtype=f32) / f32(DK))).astype(f32)
    ang = (s[None, :] * theta[:, None]).astype(f32)
    rope = np.stack([np.cos(ang), np.sin(ang)], 1).astype(f32)
    r = np.arange(P)
    above = np.where(r[:, None] > r[None, :], f32(-3.0e38), f32(0.0)).astype(f32)
    arrays = {
        "xT": i["x"].reshape(N, D).T, "x": i["x"].reshape(N, D), "ctxT": i["ctx_512"].reshape(N, FIN).T,
        "wq": wq.transpose(0, 5, 2, 4, 1, 3).reshape(D, 256),
        "wk": wk.transpose(0, 4, 2, 3, 1).reshape(D, 64),
        "wv": i["attn_Wv"], "wo": i["attn_Wo"],
        "w0": i["xattn_W0"].transpose(1, 0, 2).reshape(FIN, D),
        "w1g": i["xattn_W1"].transpose(1, 0, 2).reshape(D, D),
        "avec": np.stack([i["xattn_" + n].reshape(D) for n in ("a_self0", "a_neigh0", "a_self1", "a_neigh1", "b0", "b1")]),
        "ident": np.eye(P, dtype=f32),
        "cmask": np.stack([above, above.T], 1),
        "ropeq": np.tile(np.repeat(rope, 16, 0), (2, 1, 1)),
        "ropek": np.tile(np.repeat(rope, 4, 0), (2, 1, 1)),
        "umat": (r[:, None] < r[None, :]).astype(f32),
        "gw": i["ffn_gate_w"], "gb": i["ffn_gate_b"],
        "rowc": np.concatenate([np.arange(E), np.arange(E) * SLOT_ROWS, np.arange(E) * P,
                                (np.arange(E)[None, :] < np.arange(E)[:, None]).reshape(-1), np.arange(24)]).astype(f32),
        "b1": i["ffn_b1"].reshape(E, 8, P).transpose(2, 0, 1), "b2": i["ffn_b2"],
        "w1": i["ffn_w1"], "w2": i["ffn_w2"],
        "delta": np.tile(np.eye(GH, dtype=f32), (3, 1)),
    }
    nc = bacc.Bacc("TRN2", target_bir_lowering=False, num_devices=1)
    t = {}
    for k in arrays:
        arrays[k] = np.ascontiguousarray(arrays[k])
        t[k] = nc.dram_tensor("in_" + k, arrays[k].shape, mb_.dt.from_np(arrays[k].dtype), kind="ExternalInput").ap()
    out = nc.dram_tensor("out_0_dram", (N, D), F32, kind="ExternalOutput").ap()
    decoder_layer(nc, t, out)
    got = run(nc, [{"in_" + k: v for k, v in arrays.items()}], core_ids=[0])
    return got.results[0]["out_0_dram"].reshape(B, S, D)
```

```python
from contextlib import ExitStack

import concourse.bass as bass
from concourse import mybir

F32 = mybir.dt.float32
BF16 = mybir.dt.bfloat16
F16 = mybir.dt.float16
U32 = mybir.dt.uint32
I32 = mybir.dt.int32
ALU = mybir.AluOpType
ACT = mybir.ActivationFunctionType
AX = mybir.AxisListType

P = 128
B, S, D = 4, 256, 256
N = B * S
T = N // P
H, HKV, DK = 32, 8, 8
G = H // HKV
GH, GO, FIN = 8, 32, 64
E, F = 8, 1024
SCALE = float(DK) ** -0.5
MASK_VAL = -10000000000.0
EPS = 1e-5
Q_PART = (0, 0, 0, 1, 1, 2)
K_PART = (0, 1, 2, 0, 1, 0)
DATA_ROWS = 8 * len(Q_PART)
MAX_ROWS = 2
SLOTS = 3
SLOT_ROWS = N + P
TILES = 2 * N // P + E - 1
UP = 64.0
W1_STEPS = dict(zip([(0, 0, 1), (0, 0, 3), (0, 0, 5), (1, 0, 2), (1, 0, 6), (2, 0, 2), (2, 0, 6), (3, 0, 0)], range(E)))
W2_STEPS = {(B - 1, L, q): 3 * L + (q - 3) // 2 for L in range(2) for q in (3, 5, 7)}
ROW = D + 2
AHEAD = 2
PTU = 10


def bc(ap, axis, n):
    a = ap.unsqueeze(axis)
    shape = list(a.shape)
    shape[axis] = n
    return a.to_broadcast(shape)


def misc_uses():
    uses = {}
    for b in range(B):
        for L in range(2):
            uses.update({("feat", b, L): True, ("agg", b, L, 0): False, ("agg", b, L, 1): False})
            if L == 0:
                uses[("h1", b)] = True
    return uses


def decoder_layer(nc, t, out):
    with ExitStack() as ctx:
        def sb(name, shape, dt=F32):
            return ctx.enter_context(nc.sbuf_tensor(name, shape, dt))

        def sem(name):
            return ctx.enter_context(nc.semaphore(name))

        ps = ctx.enter_context(nc.psum_tensor("ps", [P, 8, 512], F32))
        SB, EB, PB, OB, MB = (0, 1), (2, 3), (4, 5), 6, 7
        PROJ = (4, 2)

        w1 = sb("w1", [P, E, 2, F])
        w2 = sb("w2", [P, E, 8, D])
        work = sb("work", [P, 8192])

        def carver(area):
            at = [0]

            def carve(shape, dt=F32):
                size = 1
                for n in shape[1:]:
                    size *= n
                words = size if dt in (F32, U32, I32) else size // 2
                ap = area[0:shape[0], at[0]:at[0] + words]
                at[0] += words
                assert at[0] <= area.shape[1], (at[0], shape)
                if dt is not F32:
                    ap = ap.bitcast(dt)
                names = "abcdef"[:len(shape) - 1]
                if len(shape) == 2:
                    return ap
                return ap.rearrange("p (" + " ".join(names) + ") -> p " + " ".join(names),
                                    **{n: v for n, v in zip(names[1:], shape[2:])})
            return carve

        carve = carver(w1[:, :, :, :].rearrange("p e k f -> p (e k f)"))
        cmask = carve([P, 2, P])
        umat = carve([P, P])
        ropeq = carve([P, 2, S])
        ropek = carve([32, 2, S])
        xT = carve([P, 2, N])
        wq = carve([P, 2, 256])
        wk = carve([P, 2, 64])
        wv = carve([P, 2, 64])
        avec = carve([P, 4, D])
        watmp = carve([P, D])
        rc = carve([P, 2, 2, S])
        rs = carve([P, 2, 2, S])
        rot = carve([P, 2, 2, S])
        qp = carve([P, B, 3, 2, S], BF16)
        kp = carve([32, B, 3, 2, S], BF16)
        carve = carver(w2[:, 2:E].rearrange("p e k f -> p (e k f)"))
        QS = carve([P, 2, 16, S], BF16)
        KS = carve([P, 2, 4, S], BF16)
        PT = carve([P, 2, SLOTS, 512])
        V = carve([P, T, HKV, DK])
        VW = carve([P, 2, 64 * 2 * HKV + 24])
        x_sb = carve([P, 2, 2, D])
        mneg = carve([P, 2, 2, 16])
        mb = carve([P, 2, 2, MAX_ROWS, 16], BF16)
        mT = carve([64, 2, S], BF16)
        carve = carver(work[:, :])
        es = carve([P, 2, 2, S])
        Pm = carve([P, 2, 2, S])
        PTg = carve([P, 2, 2, 2, P])
        Mt = carve([P, 2, S])
        feat = carve([P, 2, D])
        z = carve([P, 2, D])
        zm = carve([P, D])
        ze = carve([P, D])
        h1T = carve([P, 2, S])
        w1g = carve([P, 2, D])
        orv = carve([32, 2, S])
        attnT = carve([P, 2, S])
        wo = carve([P, 2, D])
        x2T = carve([P, 2, S])
        carve = carver(work[:, :])
        xg = carve([P, 2, ROW])
        xp = carve([P, 2, 2, 2, P], F16)
        hid = carve([P, F])
        gp = carve([P, 2, 2, F], F16)
        gT = carve([P, 2, 8, 2, P], F16)
        ys = carve([P, 2, D])
        sel1 = carve([16, 2, P], F16)
        sel2 = carve([16, 2, P], F16)
        brow = carve([16, F + D], F16)
        raw67 = work[:, 1028:1028 + 4096].rearrange("p (e k d) -> p e k d", e=2, k=8)
        braw = work[0:16, 5124:5124 + F + D]
        W1f = w1[:, :, :, :].rearrange("p e k f -> p (e k f)").bitcast(F16)
        W1 = W1f.rearrange("p (e k s f) -> p e k s f", e=E, k=2, s=2)
        W2f = w2[:, :, :, :].rearrange("p e k d -> p (e k d)").bitcast(F16)
        W2 = W2f.rearrange("p (e k s d) -> p e k s d", e=E, k=8, s=2)
        w1raw = w2[:, 0:2].rearrange("p e k d -> p e (k d)").rearrange("p e (k f) -> p e k f", k=2)

        def w2raw(e):
            return w2[:, e + 2] if e < E - 2 else raw67[:, e - (E - 2)]

        carve = carver(w1[:, :, :, :].rearrange("p e k f -> p (e k f)"))
        yg = carve([P, T, 2, D])
        outs = carve([P, T, D])
        ident = sb("ident", [P, P])
        ident_b = sb("ident_b", [P, P], BF16)
        maskS = sb("maskS", [P, P], BF16)
        maskT = sb("maskT", [P, P], BF16)
        before = sb("before", [P, P], BF16)
        ones_b = sb("ones_b", [P, P], BF16)
        delta8 = sb("delta8", [24, GH])
        delta = sb("delta", [24, GH, S], BF16)
        ctxT = sb("ctxT", [FIN, N])
        w0 = sb("w0", [FIN, D])
        bvec = sb("bvec", [P, 2, D])
        wa0 = sb("wa0", [FIN, 16])
        wa1 = sb("wa1", [P, 2, 16])
        res = sb("res", [P, 2, 2, D])
        stats = sb("stats", [P, T, 6])
        mv = sb("mv", [P, T, 2])
        vare = sb("vare", [P, T])
        rstd = sb("rstd", [P, T])
        mhalf = sb("mhalf", [P, T])
        x1 = sb("x1", [P, 2, 2, D])
        x2e = sb("x2e", [P, T, ROW])
        x2 = x2e[:, :, 0:D]
        ids = sb("ids", [P, T + 1])
        differs = sb("differs", [P, 1])
        dest_in = sb("dest_in", [P, 2])
        dest = sb("dest", [P, 2], I32)
        snp = sb("snp", [P, 2, 2, 3, GH], BF16)
        snr = sb("snr", [P, 2, 2, GH])
        snT = sb("snT", [24, 2, S], BF16)
        mx = sb("mx", [P, 2, 2])
        nmx = sb("nmx", [P, 2, 2])
        psums = sb("psums", [P, 2, GH])
        grv = sb("grv", [P, GH])
        gw = sb("gw", [P, 2, E])
        gb = sb("gb", [P, E])
        rowc = sb("rowc", [P, 3 * E + E * E + 24])
        iota_e, stride_e, tile_j = (rowc[:, E * i:E * i + E] for i in range(3))
        lower = rowc[:, 3 * E:3 * E + E * E].rearrange("p (a b) -> p a b", a=E)
        tau = rowc[:, 3 * E + E * E:3 * E + E * E + TILES]
        lg = sb("lg", [P, 2, E])
        lmax = sb("lmax", [P, 2])
        lsum = sb("lsum", [P, 2])
        prob = sb("prob", [P, 2, E])
        top = sb("top", [P, 2, 8])
        topi = sb("topi", [P, 2, 8], U32)
        topf = sb("topf", [P, 2, 2])
        wsum = sb("wsum", [P, 2])
        wk2 = sb("wk2", [P, T, 2])
        oh = sb("oh", [P, T, 2, E])
        chosen = sb("chosen", [P, 2, E], BF16)
        run = sb("run", [P, E])
        pos = sb("pos", [P, 2, E])
        ohp = sb("ohp", [P, 2, 2, E])
        slotf = sb("slotf", [P, T, 2])
        slot = sb("slot", [P, T, 2], I32)
        big = sb("big", [P, TILES, E])
        big2 = sb("big2", [P, TILES, E])
        tiles_e = sb("tiles_e", [P, E])
        base_e = sb("base_e", [P, E])
        end_e = sb("end_e", [P, E])
        tcl = sb("tcl", [P, TILES])
        te = sb("te", [P, TILES])
        tb = sb("tb", [P, TILES])
        trow = sb("trow", [P, TILES])
        last = sb("last", [P, 1])
        tab = sb("tab", [P, 2 * TILES + E], I32)
        padf = sb("padf", [P, E])
        zero = sb("zero", [P, ROW])
        selc = sb("selc", [16, E + 1])
        ident_h = sb("ident_h", [P, P], F16)

        qd = nc.dram_tensor("q_parts", (B, 2, 3, 8, 16, S), BF16, kind="Internal").ap()
        kd = nc.dram_tensor("k_parts", (B, 2, 3, 8, 4, S), BF16, kind="Internal").ap()
        xd = nc.dram_tensor("x_rows", (E * SLOT_ROWS, ROW), F32, kind="Internal").ap()
        yd = nc.dram_tensor("y_rows", (3 * N + P, D), F32, kind="Internal").ap()

        ld_x0 = sem("ld_x0")
        ld_const, ld_x, ld_w, ld_gat = (sem(n) for n in ("ld_const", "ld_x", "ld_w", "ld_gat"))
        consts_ready = sem("consts_ready")
        ones_ready = sem("ones_ready")
        proj_ready = sem("proj_ready")
        v_ready = sem("v_ready")
        v_done = sem("v_done")
        vw_ready = sem("vw_ready")
        rot_done = sem("rot_done")
        part_a = sem("part_a")
        rem_a = sem("rem_a")
        parts_out = [sem(f"parts_out{c}") for c in range(B)]
        stacks_in = [sem(f"stacks_in{b}") for b in range(B)]
        maxrows_in = [sem(f"maxrows_in{b}") for b in range(B)]
        s_full, s_free = sem("s_full"), sem("s_free")
        mparts = sem("mparts")
        mt_full, mt_free = sem("mt_full"), sem("mt_free")
        misc_full, misc_free = sem("misc_full"), sem("misc_free")
        t_full, t_free = sem("t_full"), sem("t_free")
        pv_done = sem("pv_done")
        o_full, o_free = sem("o_full"), sem("o_free")
        wo_ready, x1_ready = sem("wo_ready"), sem("x1_ready")
        var_ready, rstd_ready = sem("var_ready"), sem("rstd_ready")
        wa_ready = sem("wa_ready")
        pt_full, pt_free = sem("pt_full"), sem("pt_free")
        snp_ready = sem("snp_ready")
        e_full, e_free, e_fifth = sem("e_full"), sem("e_free"), sem("e_fifth")
        masked = sem("masked")
        p_ready = sem("p_ready")
        agg_done = sem("agg_done")
        zneg, zexp = sem("zneg"), sem("zexp")
        h_ready = sem("h_ready")
        x2_ready = sem("x2_ready")
        dve_step, act_step, pool_step = sem("dve_step"), sem("act_step"), sem("pool_step")
        stored = sem("stored")
        w1_in = [sem(f"w1_in{i}") for i in range(2)]
        w2_in = [sem(f"w2_in{e}") for e in range(E)]
        w1_high, w1_split, w2_high, w2_low = (sem(n) for n in ("w1_high", "w1_split", "w2_high", "w2_low"))
        rt_in, braw_in, bhigh, brow_ready = sem("rt_in"), sem("braw_in"), sem("bhigh"), sem("brow_ready")
        x_in1 = [sem(f"x_in1_{i}") for i in range(2)]
        x2_turned, x2T_ready, logits_read, ranks_read = (sem(n) for n in ("x2_turned", "x2T_ready", "logits_read", "ranks_read"))
        logit_ready, lexp_in, lexp = sem("logit_ready"), sem("lexp_in"), sem("lexp")
        chosen_ready, rank_ready = sem("chosen_ready"), sem("rank_ready")
        slots_ready, scattered = sem("slots_ready"), sem("scattered")
        ids_ready, dest_step, dest_made, dest_ready = (sem(n) for n in ("ids_ready", "dest_step", "dest_made", "dest_ready"))
        tab_ready, padded = sem("tab_ready"), sem("padded")
        xg_in, x_turned, xgT_ready = [sem(f"xg_in{i}") for i in range(2)], sem("x_turned"), sem("xgT_ready")
        h_full, g_done, gh_done, gl_done, ht_full = (sem(n) for n in ("h_full", "g_done", "gh_done", "gl_done", "ht_full"))
        gT_a, gT_d = sem("gT_a"), sem("gT_d")
        xh_ready, ya_ready = sem("xh_ready"), sem("ya_ready")
        sel1_ready, sel2_ready, y_full, y_out = (sem(n) for n in ("sel1_ready", "sel2_ready", "y_full", "y_out"))
        y_stored = [sem(f"y_stored{i}") for i in range(2)]
        gathered = [sem(f"gathered{i}") for i in range(4)]
        zero_ready = sem("zero_ready")
        out_ready = sem("out_ready")

        uses = misc_uses()

        def use(*name):
            return list(uses).index(name)

        def turned(*name):
            return sum(list(uses.values())[:use(*name)])

        def norm_x1(b):
            return max(2 * b - 1, 0)

        def norm_x2(b):
            return min(2 * b + 2, 2 * B - 1)

        def wait(eng, sm, value):
            if not isinstance(value, int) or value > 0:
                eng.wait_ge(sm, value)

        def tiles_of(eng, step):
            with eng.Fori(1, 10) as i:
                step(2 * i + 1, 1)
                step(2 * i + 2, 0)

        def pad(eng, experts):
            eng.wait_ge(tab_ready, 3)
            eng.wait_ge(zero_ready, 1)
            for e in experts:
                row = eng.value_load(tab[0:1, 2 * TILES + e:2 * TILES + e + 1], min_val=0, max_val=E * SLOT_ROWS - P)
                eng.dma_start(xd[bass.ds(row, P), :], zero[:, :]).then_inc(padded, 16)

        block = ctx.enter_context(nc.Block())
        LN_OPS = 2

        @block.sync
        def _(sp):
            xT_rows = t["xT"].rearrange("(k p) n -> p k n", p=P)
            sp.dma_start(xT[:, :, 0:S], xT_rows[:, :, 0:S]).then_inc(ld_x0, 16)
            sp.dma_start(wq[:, :, :], t["wq"].rearrange("(k p) n -> p k n", p=P)).then_inc(ld_x0, 16)
            sp.dma_start(wk[:, :, :], t["wk"].rearrange("(k p) n -> p k n", p=P)).then_inc(ld_x0, 16)
            sp.dma_start(xT[:, :, S:N], xT_rows[:, :, S:N]).then_inc(ld_x, 16)
            sp.dma_start(wv[:, :, :], t["wv"].rearrange("(k p) n -> p k n", p=P)).then_inc(ld_x, 16)
            x_tok = t["x"].rearrange("(b t p) d -> b p t d", b=B, p=P)
            for b in range(2):
                sp.dma_start(x_sb[:, b], x_tok[b]).then_inc(x_in1[b], 16)
            sp.dma_start(wo[:, :, :], t["wo"].rearrange("(k p) n -> p k n", p=P)).then_inc(ld_w, 16)
            sp.dma_start(ctxT[:, :], t["ctxT"]).then_inc(ld_gat, 16)
            sp.dma_start(w0[:, :], t["w0"]).then_inc(ld_gat, 16)
            sp.dma_start(w1g[:, :, :], t["w1g"].rearrange("(k p) n -> p k n", p=P)).then_inc(ld_gat, 16)
            sp.dma_start(bvec[:, 0, :], t["avec"][4, :].partition_broadcast(P)).then_inc(ld_gat, 16)
            sp.dma_start(bvec[:, 1, :], t["avec"][5, :].partition_broadcast(P)).then_inc(ld_gat, 16)
            sp.dma_start(gw[:, :, :], t["gw"].rearrange("(k p) n -> p k n", p=P)).then_inc(rt_in, 16)
            sp.dma_start(gb[:, :], t["gb"].partition_broadcast(P)).then_inc(rt_in, 16)
            sp.dma_start(rowc[:, :], t["rowc"].partition_broadcast(P)).then_inc(rt_in, 16)
            sp.dma_start(selc[:, :], t["selc"]).then_inc(rt_in, 16)
            for i in range(4):
                sp.dma_start(avec[:, i, :], t["avec"][i, :].partition_broadcast(P)).then_inc(ld_gat, 16)

            def parts(c):
                sp.wait_ge(rem_a, 4 * (c + 1))
                sp.wait_ge(part_a, 4 * (c + 1))
                for par in range(2):
                    sp.dma_start(qd[c, par].rearrange("a (e p) h n -> (p h) (a e) n", e=2),
                                 qp[64 * par:64 * par + 64, c].rearrange("p a e n -> p (a e) n")
                                 ).then_inc(parts_out[c], 16)
                    sp.dma_start(kd[c, par].rearrange("a (e p) h n -> (p h) (a e) n", e=2),
                                 kp[16 * par:16 * par + 16, c].rearrange("p a e n -> p (a e) n")
                                 ).then_inc(parts_out[c], 16)

            def stacks(b):
                sp.wait_ge(parts_out[b], 4 * 16)
                if b >= 2:
                    sp.wait_ge(t_full, HKV * SLOTS * (b - 1))
                for part, (j, n) in enumerate(((0, 3), (3, 2), (5, 1))):
                    for par in range(2):
                        rows = slice(64 * par + 8 * j, 64 * par + 8 * (j + n))
                        sp.dma_start(QS[rows, b % 2, :, :].rearrange("p h n -> p (h n)"),
                                     bc(qd[b, par, part].rearrange("p h n -> p (h n)"), 0, n)).then_inc(stacks_in[b], 16)
                        sp.dma_start(KS[rows, b % 2, :, :], kd[b, par, 0:n].rearrange("a p h n -> (a p) h n")
                                     ).then_inc(stacks_in[b], 16)

            def max_rows(b):
                sp.wait_ge(mt_free, b + 1)
                for par in range(2):
                    for part in range(MAX_ROWS):
                        r = 64 * par + DATA_ROWS + part
                        q0 = 32 * par + 16 * part
                        sp.dma_start(QS[r:r + 1, b % 2, :, :], mT[q0:q0 + 16, b % 2, :]).then_inc(maxrows_in[b], 16)

            w1_rows = t["w1"].rearrange("e (k p) f -> e p k f", p=P)
            w2_rows = t["w2"].rearrange("e (k p) d -> e p k d", p=P)
            sp.wait_ge(ones_ready, 1)
            parts(0)
            stacks(0)
            parts(1)
            stacks(1)
            max_rows(0)
            parts(2)
            parts(3)

            def w1_load(e):
                wait(sp, w1_split, e - 1)
                sp.dma_start(w1raw[:, e % 2], w1_rows[e]).then_inc(w1_in[e % 2], 16)

            w1_load(0)
            w1_load(1)
            stacks(2)
            for e in range(2, 5):
                w1_load(e)
            max_rows(1)
            stacks(3)
            max_rows(2)
            for b in range(2, B):
                sp.wait_ge(x1_ready, b - 1)
                sp.dma_start(x_sb[:, b % 2], x_tok[b]).then_inc(x_in1[b % 2], 16)
            w1_load(5)
            w1_load(6)
            max_rows(3)
            w1_load(7)
            sp.wait_ge(x1_ready, B)
            for e in range(E - 2):
                sp.dma_start(w2raw(e), w2_rows[e]).then_inc(w2_in[e], 16)
            sp.wait_ge(x2_ready, B)
            sp.dma_start(braw, t["b12"]).then_inc(braw_in, 16)
            for e in range(E - 2, E):
                sp.dma_start(w2raw(e), w2_rows[e]).then_inc(w2_in[e], 16)
            pad(sp, range(E // 2))
            sp.wait_ge(scattered, 16 * 4 * B)
            sp.wait_ge(padded, 16 * E)

            def tile_row(n):
                return sp.value_load(tab[0:1, bass.ds(n + TILES, 1)], min_val=0, max_val=E * SLOT_ROWS - P)

            def load_tile(n, par):
                wait(sp, x_turned, n - 1)
                wait(sp, dest_made, n - 1)
                sp.dma_start(xg[:, par, :], xd[bass.ds(tile_row(n), P), :]).then_inc(xg_in[par], 16)

            def step(n, par):
                load_tile(n + 2, par)

            load_tile(0, 0)
            load_tile(1, 1)
            load_tile(2, 0)
            step(1, 1)
            step(2, 0)
            with sp.Fori(1, 9) as i:
                step(2 * i + 1, 1)
                step(2 * i + 2, 0)
            step(19, 1)
            step(20, 0)
            sp.wait_ge(y_stored[0], 8 * (TILES + 1))
            sp.wait_ge(y_stored[1], 8 * (TILES - 1))
            sp.wait_ge(y_full, TILES)
            y_tok = yd[0:2 * N, :].rearrange("(k t p) d -> p k t d", k=2, p=P)
            for part in range(4):
                for k in range(2):
                    sp.dma_start(yg[:, 2 * part:2 * part + 2, k, :], y_tok[:, k, 2 * part:2 * part + 2, :]
                                 ).then_inc(gathered[part], 16)
            out_rows = out.rearrange("(t p) d -> p t d", p=P)
            for part in range(4):
                sp.wait_ge(out_ready, part + 1)
                sp.dma_start(out_rows[:, 2 * part:2 * part + 2, :], outs[:, 2 * part:2 * part + 2, :]).then_inc(stored, 16)
            sp.wait_ge(stored, 64)

        @block.gpsimd
        def _(pool):
            nc.gpsimd.memset(KS[:, :, :, :], 1.0).then_inc(ones_ready, 1)
            nc.gpsimd.memset(VW[:, :, :], 0.0).then_inc(ones_ready, 1)
            blocks = [VW[:, par, 0:64 * 2 * HKV].rearrange("p (n c) -> p n c", c=64) for par in range(2)]
            pool.wait_ge(ones_ready, 2)
            for par in range(2):
                nc.gpsimd.memset(blocks[par][:, :, 56:64], 1.0).then_inc(vw_ready, 1)
            nc.gpsimd.memset(mhalf[:, :], -0.5).then_inc(pool_step, 1)
            pool.wait_ge(ld_const, 16 * 7)
            nc.gpsimd.tensor_copy(ident_b[:, :], ident[:, :]).then_inc(consts_ready, 1)
            nc.gpsimd.tensor_copy(maskS[:, :], cmask[:, 0, :]).then_inc(consts_ready, 1)
            nc.gpsimd.tensor_copy(maskT[:, :], cmask[:, 1, :]).then_inc(consts_ready, 1)
            nc.gpsimd.tensor_copy(before[:, :], umat[:, :]).then_inc(consts_ready, 1)
            nc.gpsimd.tensor_copy(delta[:, :, :], bc(delta8[:, :], 2, S)).then_inc(consts_ready, 1)
            nc.gpsimd.memset(ones_b[:, :], 1.0).then_inc(consts_ready, 1)
            nc.gpsimd.memset(run[:, :], 0.0).then_inc(consts_ready, 1)
            nc.gpsimd.tensor_copy(ident_h[:, :], ident[:, :]).then_inc(consts_ready, 1)
            nc.gpsimd.memset(zero[:, :], 0.0).then_inc(ids_ready, 1)
            pool.wait_ge(ids_ready, 1)
            nc.gpsimd.tensor_copy(zero[:, D:D + 1], ids[:, T:T + 1]).then_inc(zero_ready, 1)
            nc.gpsimd.tensor_copy(x2e[:, :, D:D + 1], ids[:, 0:T].unsqueeze(2)).then_inc(ids_ready, 1)
            pool.wait_ge(ids_ready, 2)
            steps = [1]

            def inverse_root(k, n, at):
                at = slice(at, at + n)
                pool.wait_ge(var_ready, k + 1)
                nc.gpsimd.tensor_scalar(vare[:, at], mv[:, at, 1], EPS, None, ALU.add).then_inc(pool_step, 1)
                steps[0] += 1
                pool.wait_ge(pool_step, steps[0])
                nc.gpsimd.tensor_tensor(rstd[:, at], vare[:, at], mhalf[:, at], ALU.pow).then_inc(rstd_ready, 1)

            def windows(b):
                if b >= 2:
                    pool.wait_ge(pv_done, HKV * (b - 1))
                nc.gpsimd.tensor_copy(blocks[b % 2][:, :, 24:32],
                                      V[:, 2 * b:2 * b + 2].rearrange("p t g d -> p (t g) d")).then_inc(vw_ready, 1)

            pool.wait_ge(v_done, 1)
            windows(0)
            inverse_root(norm_x1(0), 2, 0)
            windows(1)
            def scatter(b):
                pool.wait_ge(slots_ready, b + 1)
                for i in range(2):
                    for k in range(2):
                        nc.gpsimd.indirect_dma_start(
                            out=xd, out_offset=bass.IndirectOffsetOnAxis(ap=slot[:, 2 * b + i, k:k + 1], axis=0),
                            in_=x2e[:, 2 * b + i, :], in_offset=None).then_inc(scattered, 16)

            for b in range(B):
                if b + 2 < B:
                    windows(b + 2)
                if b >= 1:
                    scatter(b - 1)
                if b + 1 < B:
                    inverse_root(norm_x1(b + 1), 2, 0)
                inverse_root(norm_x2(b), 2, 2)
            scatter(B - 1)
            pool.wait_ge(rt_in, 64)

            def expert(n):
                return pool.value_load(tab[0:1, bass.ds(n, 1)], min_val=0, max_val=E - 1)

            def select(par, e, sel, ready):
                nc.gpsimd.tensor_copy(sel[:, par, :], selc[:, bass.ds(e, 1)].to_broadcast([16, P])).then_inc(ready, 1)

            def select1(n, par):
                e = expert(n)
                wait(pool, h_full, 2 * n - 2)
                select(par, e, sel1, sel1_ready)

            def stored_before(n, par):
                pool.wait_ge(dest_ready, n + 1)
                wait(pool, y_stored[1 - par], 8 * (n + par))
                pool.wait_ge(y_out, n + 1)

            def store_tile(n, par):
                nc.gpsimd.indirect_dma_start(
                    out=yd, out_offset=bass.IndirectOffsetOnAxis(ap=dest[:, par:par + 1], axis=0),
                    in_=ys[:, par, :], in_offset=None).then_inc(y_stored[par], 16)

            def select2_store(n, par):
                e = expert(n)
                stored_before(n - 2, par)
                pool.wait_ge(y_full, n - 1)
                select(par, e, sel2, sel2_ready)
                store_tile(n - 2, par)

            def step(n, par):
                select2_store(n, par)
                select1(n + 1, 1 - par)

            pool.wait_ge(tab_ready, 3)
            for n in range(2):
                select1(n, n)
                select(n, expert(n), sel2, sel2_ready)
            select1(2, 0)
            step(2, 0)
            tiles_of(pool, step)
            step(21, 1)
            select2_store(22, 0)
            for n in (21, 22):
                stored_before(n, n % 2)
                store_tile(n, n % 2)
            for part in range(4):
                inverse_root(2 * B + part, 2, 2 * part)

        @block.scalar
        def _(act):
            act.dma_start(ident[:, :], t["ident"]).then_inc(ld_const, 16)
            act.dma_start(ids[:, :], t["ids"]).then_inc(ld_const, 16)
            act.dma_start(cmask[:, :, :], t["cmask"]).then_inc(ld_const, 16)
            act.dma_start(ropeq[:, :, :], t["ropeq"]).then_inc(ld_const, 16)
            act.dma_start(ropek[:, :, :], t["ropek"]).then_inc(ld_const, 16)
            act.dma_start(delta8[:, :], t["delta"]).then_inc(ld_const, 16)
            act.dma_start(umat[:, :], t["umat"]).then_inc(ld_const, 16)

            def split(c):
                for part in range(2):
                    for kind, dst in enumerate((qp[:, c], kp[:, c])):
                        if part == 0:
                            act.wait_ge(rot_done, 2 * c + kind + 1)
                        else:
                            act.wait_ge(rem_a, 4 * c + kind + 1)
                        nc.scalar.activation(dst[:, part], rot[0:(P, 32)[kind], kind], ACT.Copy).then_inc(part_a, 1)

            split(0)
            split(1)
            split(2)
            act.wait_ge(ones_ready, 1)
            act.wait_ge(v_ready, 1)
            nc.scalar.activation(V[:, :, :, :], ps[:, MB, :].rearrange("p (t g d) -> p t g d", t=T, g=HKV),
                                 ACT.Copy).then_inc(v_done, 1)

            def exps(b, g, units=range(SLOTS)):
                for u in units:
                    k = (b * HKV + g) * SLOTS + u
                    act.wait_ge(t_full, k + 1)
                    if b * HKV + g >= 2:
                        act.wait_ge(pv_done, b * HKV + g - 1)
                    nc.scalar.activation(PT[:, g % 2, u, :], ps[:, SB[k % 2], :], ACT.Exp,
                                         scale=SCALE).then_inc(t_free, 1)

            def copy_maxima(b):
                act.wait_ge(mt_full, b + 1)
                nc.scalar.activation(mT[:, b % 2, :], ps[0:64, OB, 0:S // 2].bitcast(BF16), ACT.Copy).then_inc(mt_free, 1)

            def misc_copy(dst, src, *name):
                act.wait_ge(misc_full, turned(*name) + 1)
                nc.scalar.activation(dst, src, ACT.Copy).then_inc(misc_free, 1)

            misc = ps[:, MB, :].rearrange("p (a d) -> p a d", a=2)

            def slope(gl, q):
                n = gl * 8 + q
                act.wait_ge(e_full, n + 1)
                if n >= 2:
                    act.wait_ge(p_ready, n - 1)
                nc.scalar.activation(es[:, q % 2].rearrange("p a j -> p (a j)"), ps[:, EB[q % 2], :], ACT.Copy,
                                     scale=0.2).then_inc(e_fifth, 1)

            def gexp(gl, q):
                n = gl * 8 + q
                it, hp = q // 4, q % 4
                act.wait_ge(masked, n + 1)
                if n >= 2:
                    m = n - 2
                    act.wait_ge(pt_full, (m // 8) * PTU + 2 + m % 8 + 1)
                for i in range(2):
                    ins = nc.scalar.activation(Pm[:, q % 2, i, :], es[:, q % 2, i, :], ACT.Exp,
                                               bias=nmx[:, q % 2, i:i + 1],
                                               accum_out=psums[:, it, 2 * hp + i:2 * hp + i + 1])
                ins.then_inc(p_ready, 1)

            def pt_copy(gl, q):
                n = gl * 8 + q
                act.wait_ge(pt_full, gl * PTU + 2 + q + 1)
                if n >= 2:
                    act.wait_ge(agg_done, n - 1)
                nc.scalar.activation(PTg[:, q % 2].rearrange("p h j i -> p (h j i)"), ps[:, PB[q % 2], :], ACT.Copy
                                     ).then_inc(pt_free, 1)

            def high_w1(e):
                if e == 0:
                    for c in range(B):
                        act.wait_ge(parts_out[c], 4 * 16)
                    act.wait_ge(v_ready, 1)
                    act.wait_ge(wa_ready, 6)
                    act.wait_ge(consts_ready, 8)
                act.wait_ge(w1_in[e % 2], 16 * (e // 2 + 1))
                nc.scalar.activation(W1[:, e, :, 0, :], w1raw[:, e % 2], ACT.Copy, scale=UP).then_inc(w1_high, 1)

            def high_w2(e):
                act.wait_ge(w2_in[e], 16)
                act.wait_ge(w1_split, E)
                if 2 <= e < E:
                    act.wait_ge(w2_low, e - 1)
                    act.wait_ge(w2_high, e - 1)
                nc.scalar.activation(W2[:, e, :, 0, :], w2raw(e), ACT.Copy, scale=UP).then_inc(w2_high, 1)

            def steps(b, L):
                gl = 2 * b + L
                slope(gl, 0)
                for q in range(10):
                    if 1 <= q <= 8:
                        gexp(gl, q - 1)
                    if q + 1 < 8:
                        slope(gl, q + 1)
                    if q == 7:
                        elu_exp(gl, 0)
                    more = L == 1 and b + 1 < B and q + AHEAD < HKV
                    if more:
                        exps(b + 1, q + AHEAD, range(2))
                    if q >= 2:
                        pt_copy(gl, q - 2)
                    if more:
                        exps(b + 1, q + AHEAD, range(2, SLOTS))
                    if L == 0 and b + 1 < B and q == 8:
                        copy_maxima(b + 1)
                    if (b, L, q) in W1_STEPS:
                        high_w1(W1_STEPS[b, L, q])
                    if (b, L, q) in W2_STEPS:
                        high_w2(W2_STEPS[b, L, q])
                    if L == 0 and b >= 1:
                        if q == 1:
                            copy_x2(b - 1)
                        elif q == 4:
                            route_exp(b - 1)
                elu_exp(gl, 1)

            def copy_feat(b, L):
                misc_copy(feat[:, :, :], misc, "feat", b, L)

            def elu_exp(gl, it):
                act.wait_ge(zneg, 2 * gl + it + 1)
                nc.scalar.activation(ze[:, :], zm[:, :], ACT.Exp).then_inc(zexp, 1)

            def copy_x2(b):
                act.wait_ge(x2_turned, b + 1)
                nc.scalar.activation(x2T[:, :, :], ps[:, OB, :].rearrange("p (a d) -> p a d", a=2), ACT.Copy
                                     ).then_inc(x2T_ready, 1)

            def route_exp(b):
                act.wait_ge(lexp_in, b + 1)
                nc.scalar.activation(prob[:, :, :], lg[:, :, :], ACT.Exp).then_inc(lexp, 1)

            copy_maxima(0)
            split(3)
            for g in range(HKV):
                exps(0, g)
            copy_feat(0, 0)
            for b in range(B):
                steps(b, 0)
                misc_copy(h1T[:, :, :], misc, "h1", b)
                if b + 1 < B:
                    exps(b + 1, 0, range(2))
                copy_feat(b, 1)
                if b + 1 < B:
                    exps(b + 1, 0, range(2, SLOTS))
                    exps(b + 1, 1)
                steps(b, 1)
                if b + 1 < B:
                    copy_feat(b + 1, 0)
            copy_x2(B - 1)
            route_exp(B - 1)
            act.wait_ge(braw_in, 16)
            nc.scalar.activation(braw, braw, ACT.Copy, scale=UP).then_inc(bhigh, 1)
            act.wait_ge(bhigh, 1)
            nc.scalar.activation(brow[:, :], braw, ACT.Copy).then_inc(bhigh, 1)
            high_w2(E - 2)
            high_w2(E - 1)
            pad(act, range(E // 2, E))

            def gelu_tile(n, par):
                for half in range(2):
                    cols = slice(512 * half, 512 * half + 512)
                    act.wait_ge(h_full, 2 * n + half + 1)
                    wait(act, gl_done, 2 * n + half - 1)
                    nc.scalar.activation(hid[:, cols], ps[:, 2 + half, :], ACT.Gelu_apprx_tanh, scale=1.0 / UP
                                         ).then_inc(g_done, 1)
                    act.wait_ge(g_done, 2 * n + half + 1)
                    wait(act, ht_full, 2 * n - 2)
                    nc.scalar.activation(gp[:, par, 0, cols], hid[:, cols], ACT.Copy).then_inc(gh_done, 1)
                act.wait_ge(ht_full, 2 * n + 1)
                wait(act, y_full, n - 1)
                nc.scalar.activation(gT[:, par, 0:4].rearrange("p k s n -> p (k s n)").bitcast(F32), ps[:, 4, :], ACT.Copy
                                     ).then_inc(gT_a, 1)

            for n in range(3):
                gelu_tile(n, n % 2)
            tiles_of(act, gelu_tile)
            gelu_tile(21, 1)
            gelu_tile(22, 0)

        @block.vector
        def _(dve):
            chain = [0]

            def link(ins):
                chain[0] += 1
                ins.then_inc(dve_step, 1)
                dve.wait_ge(dve_step, chain[0])

            dve.wait_ge(ld_const, 16 * 7)
            def rotate(c):
                kinds = ((P, ropeq, qp[:, c]), (32, ropek, kp[:, c]))
                dve.wait_ge(proj_ready, c + 1)
                for kind, (rows, table, dst) in enumerate(kinds):
                    src = ps[0:rows, PROJ[c % 2] + kind, :].rearrange("p (e n) -> p e n", e=2)
                    c_, s_, r_ = rc[0:rows, kind], rs[0:rows, kind], rot[0:rows, kind]
                    link(nc.vector.tensor_tensor(c_, src, bc(table[0:rows, 0, :], 1, 2), ALU.mult))
                    link(nc.vector.tensor_tensor(s_, src, bc(table[0:rows, 1, :], 1, 2), ALU.mult))
                    nc.vector.tensor_tensor(r_[:, 0], c_[:, 0], s_[:, 1], ALU.subtract)
                    nc.vector.tensor_tensor(r_[:, 1], s_[:, 0], c_[:, 1], ALU.add).then_inc(rot_done, 1)
                for part in range(2):
                    for kind, (rows, table, dst) in enumerate(kinds):
                        r_ = rot[0:rows, kind]
                        dve.wait_ge(part_a, 4 * c + 2 * part + kind + 1)
                        nc.vector.tensor_tensor(r_ if part == 0 else dst[:, 2], r_, dst[:, part], ALU.subtract
                                                ).then_inc(rem_a, 1)
                        if part == 0:
                            dve.wait_ge(rem_a, 4 * c + kind + 1)

            rotate(0)
            rotate(1)
            rotate(2)

            def fold(nth):
                L, k, i = (0, 0, nth) if nth < 2 else (1, nth // 2 - 1, nth % 2)
                rows = FIN if L == 0 else P
                w = w0[:, :] if L == 0 else w1g[:, k, :]
                o = wa0[:, 8 * i:8 * i + 8] if L == 0 else wa1[:, k, 8 * i:8 * i + 8]
                if nth:
                    dve.wait_ge(wa_ready, nth)
                link(nc.vector.tensor_tensor(watmp[0:rows, :], w, avec[0:rows, 2 * L + i, :], ALU.mult))
                nc.vector.tensor_reduce(o, watmp[0:rows, :].rearrange("p (h o) -> p h o", h=GH), AX.X, ALU.add
                                        ).then_inc(wa_ready, 1)

            def low_w1(e):
                dve.wait_ge(w1_high, e + 1)
                nc.vector.scalar_tensor_tensor(out=W1[:, e, :, 1, :], in0=w1raw[:, e % 2], scalar=UP, in1=W1[:, e, :, 0, :],
                                               op0=ALU.mult, op1=ALU.subtract).then_inc(w1_split, 1)

            def low_w2(e):
                dve.wait_ge(w2_high, e + 1)
                nc.vector.scalar_tensor_tensor(out=W2[:, e, :, 1, :], in0=w2raw(e), scalar=UP, in1=W2[:, e, :, 0, :],
                                               op0=ALU.mult, op1=ALU.subtract).then_inc(w2_low, 1)

            def maxima(b, g, units=range(SLOTS)):
                par, gg = g % 2, g // 2
                for u in units:
                    k = (b * HKV + g) * SLOTS + u
                    dve.wait_ge(s_full, k + 1)
                    if u == 0:
                        o, w = mneg[:, 0, par, 4 * gg:4 * gg + 4], 4
                    else:
                        o, w = mneg[:, 1, par, 4 * gg + 2 * u - 2:4 * gg + 2 * u], 2
                    nc.vector.tensor_reduce(o, ps[:, SB[k % 2], :].rearrange("p (h j) -> p h j", h=w), AX.X,
                                            ALU.max, negate=True).then_inc(s_free, 1)

            def maxima_parts(b):
                dve.wait_ge(s_free, (b + 1) * HKV * SLOTS)
                if b >= 1:
                    dve.wait_ge(mt_full, b)
                link(nc.vector.tensor_copy(mb[:, :, :, 0, :], mneg[:, :, :, :]))
                nc.vector.tensor_tensor(mb[:, :, :, 1, :], mneg[:, :, :, :], mb[:, :, :, 0, :], ALU.subtract
                                        ).then_inc(mparts, 1)

            def normalise(b, g):
                dve.wait_ge(pv_done, HKV * b + g + 1)
                lo = 64 * (g % 2)
                link(nc.vector.reciprocal(orv[:, g % 2, :], ps[lo + 32:lo + 64, OB, 0:S]))
                nc.vector.tensor_tensor(attnT[32 * (g % 4):32 * (g % 4) + 32, g // 4, :], ps[lo:lo + 32, OB, 0:S],
                                        orv[:, g % 2, :], ALU.mult).then_inc(o_free, 1)

            def norm_in(src, at, n=2):
                for i in range(n):
                    nc.vector.bn_stats(stats[:, at + i, :], src[:, i, :]).then_inc(dve_step, 1)
                    chain[0] += 1
                dve.wait_ge(dve_step, chain[0])
                for i in range(n):
                    ins = nc.vector.bn_aggr(mv[:, at + i, :], stats[:, at + i, :])
                ins.then_inc(var_ready, 1)

            def norm_out(k, dst, src, at, n=2):
                dve.wait_ge(rstd_ready, k + 1)
                for i in range(n):
                    ins = nc.vector.tensor_scalar(dst[:, i, :], src[:, i, :], mv[:, at + i, 0:1],
                                                  rstd[:, at + i:at + i + 1], ALU.subtract, ALU.mult)
                return ins

            def attn_out(b):
                dve.wait_ge(wo_ready, b + 1)
                dve.wait_ge(x_in1[b % 2], 16 * (b // 2) + 16)
                link(nc.vector.tensor_tensor(res[:, 0], ps[:, OB, :].rearrange("p (a d) -> p a d", a=2),
                                             x_sb[:, b % 2], ALU.add))
                norm_in(res[:, 0], 0)

            def attn_norm(b):
                norm_out(norm_x1(b), x1[:, b % 2], res[:, 0], 0).then_inc(x1_ready, 1)
                dve.wait_ge(x1_ready, b + 1)
                link(nc.vector.tensor_scalar(Mt[:, :, :], x1[:, b % 2], -1.0, 1.0, ALU.mult, ALU.add))
                link(nc.vector.tensor_scalar(Mt[:, :, :], Mt[:, :, :], MASK_VAL, None, ALU.mult))

            def graph_out(b):
                dve.wait_ge(h_ready, 4 * b + 4)
                link(nc.vector.tensor_tensor(res[:, 1], z[:, :, :], x1[:, b % 2], ALU.add))
                norm_in(res[:, 1], 2)

            def graph_norm(b):
                norm_out(norm_x2(b), x2[:, 2 * b:2 * b + 2, :], res[:, 1], 2).then_inc(x2_ready, 1)
                dve.wait_ge(x2_ready, b + 1)

            def sn_parts(gl):
                dve.wait_ge(pt_full, gl * PTU + 1)
                sn = ps[:, PB[0], 0:32].rearrange("p (t s h) -> p t s h", t=2, s=2)
                if gl >= 1:
                    dve.wait_ge(pt_full, (gl - 1) * PTU + 2)
                link(nc.vector.tensor_copy(snp[:, :, :, 0, :], sn))
                nc.vector.tensor_tensor(snr[:, :, :, :], sn, snp[:, :, :, 0, :], ALU.subtract).then_inc(pt_free, 1)
                dve.wait_ge(pt_free, gl * PTU + 1)
                link(nc.vector.tensor_copy(snp[:, :, :, 1, :], snr[:, :, :, :]))
                nc.vector.tensor_tensor(snp[:, :, :, 2, :], snr[:, :, :, :], snp[:, :, :, 1, :], ALU.subtract
                                        ).then_inc(snp_ready, 1)

            def sn_turned(gl):
                dve.wait_ge(pt_full, gl * PTU + 2)
                if gl >= 1:
                    dve.wait_ge(e_full, gl * 8)
                nc.vector.tensor_copy(snT[:, :, :], ps[0:24, PB[1], 0:S].bitcast(BF16).rearrange("p (s n) -> p s n", s=2)
                                      ).then_inc(pt_free, 1)

            def mask_max(gl, q):
                n = gl * 8 + q
                it = q // 4
                dve.wait_ge(e_fifth, n + 1)
                ee = es[:, q % 2].rearrange("p a j -> p (a j)")
                nc.vector.tensor_tensor(ee, ps[:, EB[q % 2], :], ee, ALU.max).then_inc(e_free, 1)
                dve.wait_ge(e_free, n + 1)
                if n >= 2:
                    dve.wait_ge(p_ready, n - 1)
                for i in range(2):
                    ins = nc.vector.tensor_tensor_reduce(
                        out=es[:, q % 2, i, :], in0=es[:, q % 2, i, :], in1=Mt[:, it, :], scale=1.0,
                        scalar=-3.0e38, op0=ALU.add, op1=ALU.max, accum_out=mx[:, q % 2, i:i + 1])
                link(ins)
                nc.vector.tensor_scalar(nmx[:, q % 2, :], mx[:, q % 2, :], -1.0, None, ALU.mult).then_inc(masked, 1)

            def elu_in(b, L, it):
                gl = 2 * b + L
                dve.wait_ge(agg_done, 8 * gl + 4 * it + 4)
                link(nc.vector.reciprocal(grv[:, :], psums[:, it, :]))
                nc.vector.tensor_tensor(z[:, it, :].rearrange("p (h o) -> p h o", h=GH),
                                        ps[:, MB, 0:D].rearrange("p (h o) -> p h o", h=GH),
                                        bc(grv[:, :], 2, GO), ALU.mult).then_inc(misc_free, 1)
                dve.wait_ge(misc_free, use("agg", b, L, it) + 1)
                link(nc.vector.tensor_tensor(z[:, it, :], z[:, it, :], bvec[:, L, :], ALU.add))
                nc.vector.tensor_scalar(zm[:, :], z[:, it, :], 0.0, None, ALU.min).then_inc(zneg, 1)

            def elu_out(gl, it):
                dve.wait_ge(zexp, 2 * gl + it + 1)
                nc.vector.scalar_tensor_tensor(out=z[:, it, :], in0=ze[:, :], scalar=-1.0, in1=z[:, it, :],
                                               op0=ALU.add, op1=ALU.max).then_inc(h_ready, 1)

            def steps(b, L):
                gl = 2 * b + L
                nxt = b + 1
                for q in range(9):
                    if q == 7:
                        elu_in(b, L, 0)
                    if q < 8:
                        mask_max(gl, q)
                    if q == 7:
                        elu_out(gl, 0)
                    if L == 0 and q == 0 and b >= 1:
                        graph_norm(b - 1)
                    if nxt < B and L == 0:
                        if q < HKV:
                            maxima(nxt, q)
                        else:
                            maxima_parts(nxt)
                    if L == 0 and b >= 1:
                        if q == 3:
                            route_logits(b - 1)
                        elif q == 5:
                            route_choose(b - 1)
                        elif q == 7:
                            route_slots(b - 1)
                    if nxt < B and L == 1 and 1 <= q < HKV:
                        normalise(nxt, q)
                    if (b, L, q) in W1_STEPS:
                        low_w1(W1_STEPS[b, L, q])
                    if (b, L, q) in W2_STEPS:
                        low_w2(W2_STEPS[b, L, q])

            def route_logits(b):
                dve.wait_ge(logit_ready, b + 1)
                nc.vector.tensor_tensor(lg[:, :, :], ps[:, OB, 0:2 * E].rearrange("p (t e) -> p t e", t=2),
                                        bc(gb[:, :], 1, 2), ALU.add).then_inc(logits_read, 1)
                dve.wait_ge(logits_read, b + 1)
                link(nc.vector.tensor_reduce(lmax[:, :], lg[:, :, :], AX.X, ALU.max))
                link(nc.vector.tensor_tensor(lg[:, :, :], lg[:, :, :], bc(lmax[:, :], 2, E), ALU.subtract))
                nc.vector.tensor_copy(lmax[:, :], lmax[:, :]).then_inc(lexp_in, 1)

            def route_choose(b):
                dve.wait_ge(lexp, b + 1)
                link(nc.vector.tensor_reduce(lsum[:, :], prob[:, :, :], AX.X, ALU.add))
                link(nc.vector.reciprocal(lsum[:, :], lsum[:, :]))
                link(nc.vector.tensor_tensor(prob[:, :, :], prob[:, :, :], bc(lsum[:, :], 2, E), ALU.mult))
                for i in range(2):
                    link(nc.vector.max(top[:, i, :], prob[:, i, :]))
                    link(nc.vector.max_index(topi[:, i, :], top[:, i, :], prob[:, i, :]))
                link(nc.vector.tensor_copy(topf[:, :, :], topi[:, :, 0:2]))
                link(nc.vector.tensor_copy(x2e[:, 2 * b:2 * b + 2, D + 1:D + 2], topf[:, :, 0:1]))
                link(nc.vector.tensor_tensor(wsum[:, :], top[:, :, 0], top[:, :, 1], ALU.add))
                link(nc.vector.reciprocal(wsum[:, :], wsum[:, :]))
                link(nc.vector.scalar_tensor_tensor(out=wk2[:, 2 * b:2 * b + 2, :], in0=top[:, :, 0:2], scalar=1.0 / UP,
                                                    in1=bc(wsum[:, :], 2, 2), op0=ALU.mult, op1=ALU.mult))
                for i in range(2):
                    link(nc.vector.tensor_tensor(oh[:, 2 * b + i], bc(iota_e, 1, 2), bc(topf[:, i, :], 2, E), ALU.is_equal))
                nc.vector.tensor_tensor(chosen[:, :, :], oh[:, 2 * b:2 * b + 2, 0, :], oh[:, 2 * b:2 * b + 2, 1, :], ALU.add).then_inc(chosen_ready, 1)

            def route_slots(b):
                dve.wait_ge(rank_ready, b + 1)
                link(nc.vector.tensor_tensor(pos[:, :, :], ps[:, OB, 0:2 * E].rearrange("p (t e) -> p t e", t=2),
                                             bc(run[:, :], 1, 2), ALU.add))
                nc.vector.tensor_tensor(run[:, :], run[:, :], ps[:, OB, 2 * E:3 * E], ALU.add).then_inc(ranks_read, 1)
                link(nc.vector.tensor_tensor(pos[:, :, :], pos[:, :, :], bc(stride_e, 1, 2), ALU.add))
                for i in range(2):
                    link(nc.vector.tensor_tensor(ohp[:, i], oh[:, 2 * b + i], bc(pos[:, i, :], 1, 2), ALU.mult))
                link(nc.vector.tensor_reduce(slotf[:, 2 * b:2 * b + 2, :], ohp[:, :, :, :], AX.X, ALU.add))
                nc.vector.tensor_copy(slot[:, 2 * b:2 * b + 2, :], slotf[:, 2 * b:2 * b + 2, :]).then_inc(slots_ready, 1)
                dve.wait_ge(slots_ready, b + 1)
                dve.wait_ge(ranks_read, b + 1)

            def tables():
                link(nc.vector.tensor_tensor(big[:, 0:E, :], bc(run[:, :], 2, E), bc(tile_j, 1, E), ALU.is_gt))
                link(nc.vector.tensor_reduce(tiles_e[:, :], big[:, 0:E, :], AX.X, ALU.add))
                link(nc.vector.tensor_tensor(big[:, 0:E, :], lower, bc(tiles_e[:, :], 1, E), ALU.mult))
                link(nc.vector.tensor_reduce(base_e[:, :], big[:, 0:E, :], AX.X, ALU.add))
                link(nc.vector.tensor_tensor(end_e[:, :], base_e[:, :], tiles_e[:, :], ALU.add))
                link(nc.vector.tensor_scalar(last[:, :], end_e[:, E - 1:E], -1.0, None, ALU.add))
                link(nc.vector.tensor_scalar(tcl[:, :], tau, last[:, 0:1], None, ALU.min))
                link(nc.vector.tensor_tensor(big[:, :, :], bc(tcl[:, :], 2, E), bc(end_e[:, :], 1, TILES), ALU.is_ge))
                link(nc.vector.tensor_reduce(te[:, :], big[:, :, :], AX.X, ALU.add))
                link(nc.vector.tensor_tensor(big2[:, :, :], big[:, :, :], bc(tiles_e[:, :], 1, TILES), ALU.mult))
                link(nc.vector.tensor_reduce(tb[:, :], big2[:, :, :], AX.X, ALU.add))
                link(nc.vector.tensor_tensor(trow[:, :], tcl[:, :], tb[:, :], ALU.subtract))
                link(nc.vector.tensor_scalar(trow[:, :], trow[:, :], float(P), None, ALU.mult))
                link(nc.vector.tensor_scalar(tcl[:, :], te[:, :], float(SLOT_ROWS), None, ALU.mult))
                link(nc.vector.tensor_tensor(trow[:, :], trow[:, :], tcl[:, :], ALU.add))
                link(nc.vector.tensor_tensor(padf[:, :], run[:, :], stride_e, ALU.add))
                nc.vector.tensor_copy(tab[:, 0:TILES], te[:, :]).then_inc(tab_ready, 1)
                nc.vector.tensor_copy(tab[:, TILES:2 * TILES], trow[:, :]).then_inc(tab_ready, 1)
                nc.vector.tensor_copy(tab[:, 2 * TILES:2 * TILES + E], padf[:, :]).then_inc(tab_ready, 1)
                dve.wait_ge(tab_ready, 3)
            dve.wait_ge(rt_in, 64)
            for g in range(HKV):
                maxima(0, g)
            maxima_parts(0)
            rotate(3)
            dve.wait_ge(ld_gat, 16 * 9)
            for g in range(HKV):
                normalise(0, g)
                if g < 6:
                    fold(g)
                if g == 6:
                    sn_parts(0)
            attn_out(0)
            sn_turned(0)
            attn_norm(0)
            for b in range(B):
                steps(b, 0)
                elu_in(b, 0, 1)
                elu_out(2 * b, 1)
                sn_parts(2 * b + 1)
                sn_turned(2 * b + 1)
                if b + 1 < B:
                    normalise(b + 1, 0)
                steps(b, 1)
                if b + 1 < B:
                    attn_out(b + 1)
                elu_in(b, 1, 1)
                if b + 1 < B:
                    sn_parts(2 * b + 2)
                    attn_norm(b + 1)
                elu_out(2 * b + 1, 1)
                if b + 1 < B:
                    sn_turned(2 * b + 2)
                graph_out(b)
            graph_norm(B - 1)
            route_logits(B - 1)
            route_choose(B - 1)
            route_slots(B - 1)
            tables()

            dve.wait_ge(bhigh, 2)
            nc.vector.scalar_tensor_tensor(out=brow[:, :], in0=brow[:, :], scalar=selc[:, E:E + 1], in1=braw,
                                           op0=ALU.mult, op1=ALU.add).then_inc(brow_ready, 1)
            low_w2(E - 2)
            low_w2(E - 1)

            def x_parts(n, par):
                wait(dve, h_full, 2 * n - 2)
                dve.wait_ge(x_turned, n + 1)
                src = ps[:, par, 0:D].rearrange("p (k n) -> p k n", k=2)
                nc.vector.tensor_copy(xp[:, par, :, 0, :], src).then_inc(xh_ready, 1)
                dve.wait_ge(xh_ready, n + 1)
                nc.vector.tensor_tensor(xp[:, par, :, 1, :], src, xp[:, par, :, 0, :], ALU.subtract).then_inc(xgT_ready, 1)

                nc.vector.tensor_tensor(differs[:, :], xg[:, par, D + 1:D + 2], te[:, bass.ds(n, 1)], ALU.not_equal
                                        ).then_inc(dest_step, 1)
                dve.wait_ge(dest_step, n + 1)
                nc.vector.scalar_tensor_tensor(out=dest_in[:, par:par + 1], in0=differs[:, :], scalar=float(N),
                                               in1=xg[:, par, D:D + 1], op0=ALU.mult, op1=ALU.add).then_inc(dest_made, 1)

            def keep(n, par):
                dve.wait_ge(dest_made, n + 1)
                wait(dve, y_stored[par], 8 * (n - par))
                nc.vector.tensor_copy(dest[:, par:par + 1], dest_in[:, par:par + 1]).then_inc(dest_ready, 1)

            def low_half(n, par, half):
                cols = slice(512 * half, 512 * half + 512)
                dve.wait_ge(gh_done, 2 * n + half + 1)
                nc.vector.tensor_tensor(gp[:, par, 1, cols], hid[:, cols], gp[:, par, 0, cols], ALU.subtract
                                        ).then_inc(gl_done, 1)

            def g_copy(n, par):
                dve.wait_ge(ht_full, 2 * n + 2)
                wait(dve, y_full, n - 1)
                nc.vector.tensor_copy(gT[:, par, 4:8].rearrange("p k s n -> p (k s n)").bitcast(F32), ps[:, 5, :]
                                      ).then_inc(gT_d, 1)

            def y_copy(n, par):
                wait(dve, y_stored[par], 8 * (n - par))
                dve.wait_ge(y_full, n + 1)
                nc.vector.tensor_copy(ys[:, par, :], ps[:, 6 + par, 0:D]).then_inc(ya_ready, 1)
                dve.wait_ge(ya_ready, n + 1)
                nc.vector.tensor_tensor(ys[:, par, :], ys[:, par, :], ps[:, 6 + par, D:2 * D], ALU.add).then_inc(y_out, 1)

            def step(n, par):
                keep(n - 1, 1 - par)
                dve.wait_ge(dest_ready, n)
                x_parts(n + 1, 1 - par)
                low_half(n, par, 0)
                low_half(n, par, 1)
                y_copy(n - 1, 1 - par)
                g_copy(n, par)

            x_parts(0, 0)
            x_parts(1, 1)
            low_half(0, 0, 0)
            low_half(0, 0, 1)
            g_copy(0, 0)
            step(1, 1)
            step(2, 0)
            tiles_of(dve, step)
            step(21, 1)
            keep(21, 1)
            keep(22, 0)
            low_half(22, 0, 0)
            low_half(22, 0, 1)
            y_copy(21, 1)
            g_copy(22, 0)
            y_copy(22, 0)

            def combine(part):
                dve.wait_ge(gathered[part], 16 * 2)
                for k in range(2):
                    for i in range(2 * part, 2 * part + 2):
                        ins = nc.vector.scalar_tensor_tensor(out=x2[:, i, :], in0=yg[:, i, k, :], scalar=wk2[:, i, k:k + 1],
                                                             in1=x2[:, i, :], op0=ALU.mult, op1=ALU.add)
                    link(ins)
                norm_in(x2[:, 2 * part:2 * part + 2, :], 2 * part)

            def final_norm(part):
                tiles = slice(2 * part, 2 * part + 2)
                norm_out(2 * B + part, outs[:, tiles, :], x2[:, tiles, :], 2 * part).then_inc(out_ready, 1)

            for part in range(5):
                if part < 4:
                    combine(part)
                if part >= 1:
                    final_norm(part - 1)

        @block.tensor
        def _(pe):
            def project(c):
                tok = slice(S * c, S * c + S)
                wait(pe, rot_done, 2 * (c - 1))
                for kind, (w, rows) in enumerate(((wq, P), (wk, 32))):
                    for e in range(2):
                        for k in range(2):
                            ins = nc.tensor.matmul(ps[0:rows, PROJ[c % 2] + kind, S * e:S * e + S],
                                                   w[:, k, rows * e:rows * e + rows], xT[:, k, tok],
                                                   start=(k == 0), stop=(k == 1))
                ins.then_inc(proj_ready, 1)

            pe.wait_ge(ld_x0, 48)
            project(0)
            pe.wait_ge(ld_x, 32)
            project(1)
            for tt in range(T):
                for k in range(2):
                    ins = nc.tensor.matmul(ps[:, MB, 64 * tt:64 * tt + 64], xT[:, k, 128 * tt:128 * tt + 128],
                                           wv[:, k, :], start=(k == 0), stop=(k == 1))
            ins.then_inc(v_ready, 1)
            project(2)
            project(3)
            pe.wait_ge(consts_ready, 8)
            pe.wait_ge(v_done, 1)

            def scores(b, g, units=range(SLOTS)):
                par, gg = g % 2, g // 2
                lo = 64 * par
                if g == 0 and 0 in units:
                    pe.wait_ge(stacks_in[b], 16 * 12)
                    wait(pe, t_free, b * HKV * SLOTS)
                for u in units:
                    k = (b * HKV + g) * SLOTS + u
                    if k >= 2:
                        pe.wait_ge(s_free, k - 1)
                    bank = ps[:, SB[k % 2], :]
                    if u == 0:
                        nc.tensor.matmul(bank.rearrange("p (h j) -> p h j", h=4), maskS[:, :], bc(ident_b[:, :], 1, 4),
                                         start=True, stop=False, skip_group_check=True)
                        for i in range(4):
                            ins = nc.tensor.matmul(bank[:, 128 * i:128 * i + 128],
                                                   QS[lo:lo + DATA_ROWS, b % 2, 4 * gg + i, 0:128],
                                                   KS[lo:lo + DATA_ROWS, b % 2, gg, 0:128],
                                                   start=False, stop=True, skip_group_check=True)
                    else:
                        nc.tensor.matmul(bank.rearrange("p (h j) -> p h j", h=2)[:, :, 128:256], maskS[:, :],
                                         bc(ident_b[:, :], 1, 2), start=True, stop=False, skip_group_check=True)
                        for i in range(2):
                            ins = nc.tensor.matmul(bank[:, 256 * i:256 * i + 256],
                                                   QS[lo:lo + DATA_ROWS, b % 2, 4 * gg + 2 * u - 2 + i, 128:256],
                                                   KS[lo:lo + DATA_ROWS, b % 2, gg, 0:256],
                                                   start=False, stop=True, skip_group_check=True)
                    ins.then_inc(s_full, 1)

            def turn_maxima(b):
                pe.wait_ge(mparts, b + 1)
                wait(pe, ranks_read, b - 1)
                wait(pe, x1_ready, b)
                dst = ps[0:64, OB, 0:S // 2].bitcast(BF16)
                for qt in range(2):
                    ins = nc.tensor.transpose(dst[:, 128 * qt:128 * qt + 128],
                                              mb[:, qt].rearrange("p a b h -> p (a b h)"), ident_b[:, :])
                ins.then_inc(mt_full, 1)

            def scores_t(b, g, units=range(SLOTS)):
                KR = DATA_ROWS + MAX_ROWS
                par, gg = g % 2, g // 2
                lo = 64 * par
                if g == 0 and 0 in units:
                    pe.wait_ge(maxrows_in[b], 16 * 4)
                    pe.wait_ge(s_free, (b + 1) * HKV * SLOTS)
                for u in units:
                    k = (b * HKV + g) * SLOTS + u
                    if k >= 2:
                        pe.wait_ge(t_free, k - 1)
                    bank = ps[:, SB[k % 2], :]
                    if u < 2:
                        nc.tensor.matmul(bank.rearrange("p (h j) -> p h j", h=2)[:, :, 0:128], maskT[:, :],
                                         bc(ident_b[:, :], 1, 2), start=True, stop=False, skip_group_check=True)
                        ins = nc.tensor.matmul(bank.rearrange("p (h j) -> p h j", h=2),
                                               KS[lo:lo + KR, b % 2, gg, 0:128],
                                               QS[lo:lo + KR, b % 2, 4 * gg + 2 * u:4 * gg + 2 * u + 2, :],
                                               start=False, stop=True, skip_group_check=True)
                    else:
                        nc.tensor.matmul(bank.rearrange("p (h j) -> p h j", h=4), maskT[:, :],
                                         bc(ident_b[:, :], 1, 4), start=True, stop=False, skip_group_check=True)
                        ins = nc.tensor.matmul(bank.rearrange("p (h j) -> p h j", h=4),
                                               KS[lo:lo + KR, b % 2, gg, 128:256],
                                               QS[lo:lo + KR, b % 2, 4 * gg:4 * gg + 4, 128:256],
                                               start=False, stop=True, skip_group_check=True)
                    ins.then_inc(t_full, 1)

            def values(b, g):
                pe.wait_ge(t_free, (b * HKV + g + 1) * SLOTS)
                if g == 0:
                    pe.wait_ge(vw_ready, 2 + b + 1)
                    pe.wait_ge(mt_free, b + 1)
                if g >= 2:
                    pe.wait_ge(o_free, b * HKV + g - 1)
                o = ps[64 * (g % 2):64 * (g % 2) + 64, OB, 0:S]
                for i in range(4):
                    for kt in range(2):
                        at = 64 * (kt * HKV + g) + 24 - 8 * i
                        pt = PT[:, g % 2, i // 2, S * (i % 2):S * (i % 2) + S] if kt == 0 else \
                            PT[:, g % 2, 2, P * i:P * i + P]
                        ins = nc.tensor.matmul(o[:, P * kt:S], VW[:, b % 2, at:at + 64], pt,
                                               start=(i == 0 and kt == 0), stop=(i == 3 and kt == 1),
                                               skip_group_check=True)
                ins.then_inc(pv_done, 1)

            def turn(dst, src_tile):
                for a in range(2):
                    for f in range(2):
                        ins = nc.tensor.transpose(dst[:, a * 256 + 128 * f:a * 256 + 128 * f + 128],
                                                  src_tile[:, f, 128 * a:128 * a + 128], ident[:, :])
                return ins

            def attn_proj(b):
                pe.wait_ge(o_free, HKV * (b + 1))
                pe.wait_ge(ld_w, 16)
                for qt in range(2):
                    for k in range(2):
                        ins = nc.tensor.matmul(ps[:, OB, 256 * qt:256 * qt + 256], attnT[:, k, 128 * qt:128 * qt + 128],
                                               wo[:, k, :], start=(k == 0), stop=(k == 1))
                ins.then_inc(wo_ready, 1)

            def layer_in(b, L):
                if L == 0:
                    return 1, lambda k, it: ctxT[:, S * b + P * it:S * b + P * it + P], lambda k: w0[:, :], lambda k: wa0[:, :]
                return 2, lambda k, it: h1T[:, k, P * it:P * it + P], lambda k: w1g[:, k, :], lambda k: wa1[:, k, :]

            def self_neigh(b, L):
                kt, src, _, wa = layer_in(b, L)
                gl = 2 * b + L
                if L == 1:
                    pe.wait_ge(misc_free, use("h1", b) + 1)
                wait(pe, pt_free, gl * PTU)
                for it in range(2):
                    for k in range(kt):
                        ins = nc.tensor.matmul(ps[:, PB[0], 16 * it:16 * it + 16], src(k, it), wa(k),
                                               start=(k == 0), stop=(k == kt - 1))
                ins.then_inc(pt_full, 1)

            def features(b, L):
                kt, src, w, _ = layer_in(b, L)
                wait(pe, misc_free, use("feat", b, L))
                for it in range(2):
                    for k in range(kt):
                        ins = nc.tensor.matmul(ps[:, MB, 256 * it:256 * it + 256], src(k, it), w(k),
                                               start=(k == 0), stop=(k == kt - 1))
                ins.then_inc(misc_full, 1)

            def turn_sn(gl):
                pe.wait_ge(snp_ready, gl + 1)
                pe.wait_ge(pt_free, gl * PTU + 1)
                dst = ps[0:24, PB[1], 0:S].bitcast(BF16).rearrange("p (s n) -> p s n", s=2)
                for s in range(2):
                    for it in range(2):
                        ins = nc.tensor.transpose(dst[:, s, 128 * it:128 * it + 128],
                                                  snp[:, it, s].rearrange("p a h -> p (a h)"), ident_b[:, :])
                ins.then_inc(pt_full, 1)

            def steps(b, L):
                gl = 2 * b + L
                pe.wait_ge(pt_free, gl * PTU + 2)

                def e_mm(q):
                    n = gl * 8 + q
                    it, hp = q // 4, q % 4
                    if n >= 2:
                        pe.wait_ge(e_free, n - 1)
                    nc.tensor.matmul(ps[:, EB[q % 2], :].rearrange("p (h j) -> p h j", h=2), snT[:, 0, 128 * it:128 * it + 128],
                                     delta[:, 2 * hp:2 * hp + 2, :], start=True, stop=False, skip_group_check=True)
                    for i in range(2):
                        ins = nc.tensor.matmul(ps[:, EB[q % 2], 256 * i:256 * i + 256], delta[:, 2 * hp + i, 0:128], snT[:, 1, :],
                                               start=False, stop=True, skip_group_check=True)
                    ins.then_inc(e_full, 1)

                def turn_p(q):
                    pe.wait_ge(p_ready, gl * 8 + q + 1)
                    pe.wait_ge(pt_free, gl * PTU + 1 + q)
                    for i in range(2):
                        for jt in range(2):
                            c0 = 256 * i + 128 * jt
                            ins = nc.tensor.transpose(ps[:, PB[q % 2], c0:c0 + 128], Pm[:, q % 2, i, 128 * jt:128 * jt + 128],
                                                      ident[:, :])
                    ins.then_inc(pt_full, 1)

                def agg(q):
                    it, hp = q // 4, q % 4
                    pe.wait_ge(pt_free, gl * PTU + 2 + q + 1)
                    if hp == 0:
                        pe.wait_ge(misc_free, use("agg", b, L, it))
                    for i in range(2):
                        h = 2 * hp + i
                        for jt in range(2):
                            ins = nc.tensor.matmul(ps[:, MB, GO * h:GO * h + GO], PTg[:, q % 2, i, jt, :],
                                                   feat[:, jt, GO * h:GO * h + GO], start=(jt == 0), stop=(jt == 1))
                    ins.then_inc(agg_done, 1)

                nxt = b + 1
                units = scores if L == 0 else scores_t
                e_mm(0)
                for q in range(11):
                    if q + 1 < 8:
                        e_mm(q + 1)
                    g = q if L == 0 else q + AHEAD
                    if nxt < B and g < HKV:
                        units(nxt, g, range(2))
                    if 2 <= q <= 9:
                        turn_p(q - 2)
                    if nxt < B and L == 1 and q + 1 < HKV:
                        values(nxt, q + 1)
                    if q >= 3:
                        agg(q - 3)
                    if nxt < B and g < HKV:
                        units(nxt, g, range(2, SLOTS))
                    if L == 0 and b >= 1:
                        if q == 1:
                            turn_x2(b - 1)
                        elif q == 2:
                            logits(b - 1)
                        elif q == 6:
                            ranks(b - 1)
                    if nxt < B and L == 0 and q == 9:
                        turn_maxima(nxt)
                    if nxt < B and L == 1 and q == 9:
                        attn_proj(nxt)

            def turn_h1(b):
                pe.wait_ge(h_ready, 4 * b + 2)
                pe.wait_ge(misc_free, use("h1", b))
                turn(ps[:, MB, :], z).then_inc(misc_full, 1)

            def turn_x2(b):
                pe.wait_ge(x2_ready, b + 1)
                pe.wait_ge(x1_ready, min(b + 2, B))
                turn(ps[:, OB, :], x2[:, 2 * b:2 * b + 2, :]).then_inc(x2_turned, 1)

            def logits(b):
                pe.wait_ge(x2T_ready, b + 1)
                for i in range(2):
                    for k in range(2):
                        ins = nc.tensor.matmul(ps[:, OB, E * i:E * i + E], x2T[:, k, 128 * i:128 * i + 128], gw[:, k, :],
                                               start=(k == 0), stop=(k == 1))
                ins.then_inc(logit_ready, 1)

            def ranks(b):
                pe.wait_ge(chosen_ready, b + 1)
                pe.wait_ge(logits_read, b + 1)
                nc.tensor.matmul(ps[:, OB, 0:E], before[:, :], chosen[:, 0, :], start=True, stop=True)
                nc.tensor.matmul(ps[:, OB, E:2 * E], before[:, :], chosen[:, 1, :], start=True, stop=False)
                nc.tensor.matmul(ps[:, OB, E:2 * E], ones_b[:, :], chosen[:, 0, :], start=False, stop=True)
                nc.tensor.matmul(ps[:, OB, 2 * E:3 * E], ones_b[:, :], chosen[:, 0, :], start=True, stop=False)
                nc.tensor.matmul(ps[:, OB, 2 * E:3 * E], ones_b[:, :], chosen[:, 1, :], start=False, stop=True
                                 ).then_inc(rank_ready, 1)

            for g in range(HKV):
                scores(0, g)
            turn_maxima(0)
            for g in range(HKV + 1):
                if g < HKV:
                    scores_t(0, g)
                if g == HKV:
                    pe.wait_ge(rt_in, 64)
                    pe.wait_ge(ld_gat, 16 * 9)
                    pe.wait_ge(wa_ready, 6)
                    self_neigh(0, 0)
                    features(0, 0)
                if g >= 1:
                    values(0, g - 1)
            turn_sn(0)
            attn_proj(0)
            for b in range(B):
                steps(b, 0)
                turn_h1(b)
                if b + 1 < B:
                    scores_t(b + 1, 0, range(2))
                self_neigh(b, 1)
                features(b, 1)
                if b + 1 < B:
                    scores_t(b + 1, 0, range(2, SLOTS))
                    scores_t(b + 1, 1, range(2))
                turn_sn(2 * b + 1)
                if b + 1 < B:
                    values(b + 1, 0)
                    scores_t(b + 1, 1, range(2, SLOTS))
                steps(b, 1)
                if b + 1 < B:
                    self_neigh(b + 1, 0)
                    features(b + 1, 0)
                    turn_sn(2 * b + 2)
            turn_x2(B - 1)
            logits(B - 1)
            ranks(B - 1)

            pe.wait_ge(tab_ready, 3)

            def turn_x(n, par):
                wait(pe, xgT_ready, n - 1)
                pe.wait_ge(xg_in[par], 8 * (n - par) + 16)
                for k in range(2):
                    ins = nc.tensor.transpose(ps[:, par, 128 * k:128 * k + 128], xg[:, par, 128 * k:128 * k + 128],
                                              ident[:, :])
                ins.then_inc(x_turned, 1)

            def expert(n):
                return pe.value_load(tab[0:1, bass.ds(n, 1)], min_val=0, max_val=E - 1)

            def mm1(n, par, e):
                pe.wait_ge(xgT_ready, n + 1)
                for half in range(2):
                    wait(pe, g_done, 2 * n + half - 1)
                    cols = slice(512 * half, 512 * half + 512)
                    for k in range(2):
                        for xs, ws in ((0, 0), (1, 0), (0, 1)):
                            nc.tensor.matmul(ps[:, 2 + half, :], xp[:, par, k, xs, :],
                                             W1f[:, bass.ds(e * (4 * F) + ((2 * k + ws) * F + 512 * half), 512)],
                                             start=(k == 0 and xs == 0 and ws == 0), stop=False)
                    if half == 0:
                        pe.wait_ge(sel1_ready, n + 1)
                    nc.tensor.matmul(ps[:, 2 + half, :], sel1[:, par, :], brow[:, cols], start=False, stop=True
                                     ).then_inc(h_full, 1)

            def turn_h(n, par):
                for half in range(2):
                    pe.wait_ge(gl_done, 2 * n + half + 1)
                    wait(pe, gT_d if half else gT_a, n)
                    dst = ps[:, 4 + half, :].bitcast(F16).rearrange("p (k s n) -> p k s n", k=4, s=2)
                    for k in range(4):
                        for part in range(2):
                            c0 = 512 * half + P * k
                            ins = nc.tensor.transpose(dst[:, k, part, :], gp[:, par, part, c0:c0 + P], ident_h[:, :])
                    ins.then_inc(ht_full, 1)

            def mm2(n, par, e):
                pe.wait_ge(gT_a, n + 1)
                pe.wait_ge(gT_d, n + 1)
                wait(pe, y_out, n - 1)
                for k in range(8):
                    at = e * (16 * D) + 2 * k * D
                    nc.tensor.matmul(ps[:, 6 + par, :], gT[:, par, k, 0, :], W2f[:, bass.ds(at, 2 * D)],
                                     start=(k == 0), stop=(k == 7), skip_group_check=True)
                    nc.tensor.matmul(ps[:, 6 + par, 0:D], gT[:, par, k, 1, :], W2f[:, bass.ds(at, D)],
                                     start=False, stop=False, skip_group_check=True)
                pe.wait_ge(sel2_ready, n + 1)
                nc.tensor.matmul(ps[:, 6 + par, 0:D], sel2[:, par, :], brow[:, F:F + D], start=False, stop=True,
                                 skip_group_check=True).then_inc(y_full, 1)

            def step(n, par):
                e_before, e = expert(n - 1), expert(n)
                turn_h(n - 1, 1 - par)
                turn_x(n + 1, 1 - par)
                mm1(n, par, e)
                mm2(n - 1, 1 - par, e_before)

            pe.wait_ge(w1_split, E)
            pe.wait_ge(w2_low, E)
            pe.wait_ge(brow_ready, 1)
            turn_x(0, 0)
            turn_x(1, 1)
            mm1(0, 0, expert(0))
            step(1, 1)
            step(2, 0)
            tiles_of(pe, step)
            step(21, 1)
            turn_h(21, 1)
            mm1(22, 0, expert(22))
            mm2(21, 1, expert(21))
            turn_h(22, 0)
            mm2(22, 0, expert(22))


def kernel(**inputs):
    import numpy as np
    import concourse.bacc as bacc
    from concourse import mybir as mb_
    from concourse.bass_utils import run_bass_kernel_spmd as run

    f32 = np.float32
    i = {k.replace("L0_", ""): np.asarray(v) for k, v in inputs.items()}
    wq = i["attn_Wq"].reshape(D, 4, 2, 4, 4, 2)
    wk = i["attn_Wk"].reshape(D, 4, 2, 4, 2)
    s = np.arange(S, dtype=f32)
    theta = (f32(1.0) / f32(10000.0) ** (f32(2.0) * np.arange(DK // 2, dtype=f32) / f32(DK))).astype(f32)
    ang = (s[None, :] * theta[:, None]).astype(f32)
    rope = np.stack([np.cos(ang), np.sin(ang)], 1).astype(f32)
    r = np.arange(P)
    above = np.where(r[:, None] > r[None, :], f32(-3.0e38), f32(0.0)).astype(f32)
    arrays = {
        "xT": i["x"].reshape(N, D).T, "x": i["x"].reshape(N, D), "ctxT": i["ctx_512"].reshape(N, FIN).T,
        "wq": wq.transpose(0, 5, 2, 4, 1, 3).reshape(D, 256),
        "wk": wk.transpose(0, 4, 2, 3, 1).reshape(D, 64),
        "wv": i["attn_Wv"], "wo": i["attn_Wo"],
        "w0": i["xattn_W0"].transpose(1, 0, 2).reshape(FIN, D),
        "w1g": i["xattn_W1"].transpose(1, 0, 2).reshape(D, D),
        "avec": np.stack([i["xattn_" + n].reshape(D) for n in ("a_self0", "a_neigh0", "a_self1", "a_neigh1", "b0", "b1")]),
        "ident": np.eye(P, dtype=f32),
        "ids": np.concatenate([np.arange(N).reshape(T, P), 2 * N + np.arange(P)[None]]).T.astype(f32),
        "cmask": np.stack([above, above.T], 1),
        "ropeq": np.tile(np.repeat(rope, 16, 0), (2, 1, 1)),
        "ropek": np.tile(np.repeat(rope, 4, 0), (2, 1, 1)),
        "umat": (r[:, None] < r[None, :]).astype(f32),
        "gw": i["ffn_gate_w"], "gb": i["ffn_gate_b"],
        "rowc": np.concatenate([np.arange(E), np.arange(E) * SLOT_ROWS, np.arange(E) * P,
                                (np.arange(E)[None, :] < np.arange(E)[:, None]).reshape(-1), np.arange(24)]).astype(f32),
        "b12": np.tile(np.concatenate([i["ffn_b1"], i["ffn_b2"]], 1), (2, 1)),
        "selc": np.concatenate([np.tile(np.eye(E), (2, 1)), np.repeat([[0.0], [-1.0]], E, 0)], 1).astype(f32),
        "w1": i["ffn_w1"], "w2": i["ffn_w2"],
        "delta": np.tile(np.eye(GH, dtype=f32), (3, 1)),
    }
    nc = bacc.Bacc("TRN2", target_bir_lowering=False, num_devices=1)
    t = {}
    for k in arrays:
        arrays[k] = np.ascontiguousarray(arrays[k])
        t[k] = nc.dram_tensor("in_" + k, arrays[k].shape, mb_.dt.from_np(arrays[k].dtype), kind="ExternalInput").ap()
    out = nc.dram_tensor("out_0_dram", (N, D), F32, kind="ExternalOutput").ap()
    decoder_layer(nc, t, out)
    got = run(nc, [{"in_" + k: v for k, v in arrays.items()}], core_ids=[0])
    return got.results[0]["out_0_dram"].reshape(B, S, D)
```
